# Optimizing a Trainium2 kernel written in Bass

```python
import numpy as np
import jax
import jax.numpy as jnp

def _softmax(x, axis=-1):
    return jax.nn.softmax(x, axis=axis)

def _gelu(x):
    return jax.nn.gelu(x, approximate=True)

def _silu(x):
    return jax.nn.silu(x)

def _sigmoid(x):
    return jax.nn.sigmoid(x)

def _layernorm(x, axis=-1, eps=1e-05):
    m = jnp.mean(x, axis=axis, keepdims=True)
    v = jnp.var(x, axis=axis, keepdims=True)
    return (x - m) / jnp.sqrt(v + eps)

def _scatter_add(tgt, idx, src, axis=0):
    return tgt.at[idx].add(src)

def _segment_sum(src, seg, n):
    return jax.ops.segment_sum(src, seg, n)
kernel_name = 'mk_xattn_seq_d2_seqx_r8_a2e3fc'

def setup_inputs(seed: int=0):
    np.random.seed(seed)
    _w = jnp.asarray

    def _rec_inputs():
        import jax
        import jax.numpy as jnp
        _rk = jax.random.key(seed)
        x = 7.22e-05 + 1 * jax.random.normal(jax.random.fold_in(_rk, 1), (4, 256, 256), jnp.float32)
        _lenS = 256 - jax.random.randint(jax.random.fold_in(_rk, 7), (4,), 0, max(1, 256 // 4) + 1, jnp.int32)
        _lenS2 = 64 - jax.random.randint(jax.random.fold_in(_rk, 8), (4,), 0, max(1, 64 // 4) + 1, jnp.int32)
        _ctx_2048P = jax.random.normal(jax.random.fold_in(_rk, 11), (4, 16, 256), jnp.float32)
        _ctx_2048c = jax.random.dirichlet(jax.random.fold_in(_rk, 511), 0.3 * jnp.ones((16,), jnp.float32), (4, 64))
        _ctx_2048t = jnp.einsum('bsk,bkd->bsd', _ctx_2048c, _ctx_2048P)
        _ctx_2048t = _ctx_2048t * jax.lax.rsqrt(jnp.mean(jnp.square(_ctx_2048t)) + 1e-12) * 0.953939
        ctx_2048 = 4.13588e-05 + 0.999923 * (_ctx_2048t + 0.3 * jax.random.normal(jax.random.fold_in(_rk, 611), (4, 64, 256), jnp.float32))
        _validS = jnp.arange(256)[None, :] < _lenS[:, None]
        _validS2 = jnp.arange(64)[None, :] < _lenS2[:, None]
        _causal = jnp.tril(jnp.ones((256, 256), dtype=bool))
        mask_Bx1xSxS2_ff0 = jnp.where(jnp.ones((4, 1, 256, 64), dtype=bool), 0.0, -1000000000.0).astype(jnp.float32)
        return (x, ctx_2048, mask_Bx1xSxS2_ff0)
    x, ctx_2048, mask_Bx1xSxS2_ff0 = _rec_inputs()

    def _L0_xattn_setup():
        import jax, jax.numpy as jnp
        import numpy as np
        H = 256
        NH = 32
        KVH = 8
        HD = H // NH
        GROUPS = NH // KVH
        EPS = 1e-06
        B, L, S = (4, 128, 128)

        def _gqa_forward(hidden_state, encoder_hidden_state, encoder_attention_mask, Wq, bq, Wk, bk, Wv, bv, Wo, bo, gamma, beta):
            b, l, _ = hidden_state.shape
            s = encoder_hidden_state.shape[1]
            q = hidden_state @ Wq + bq
            k = encoder_hidden_state @ Wk + bk
            v = encoder_hidden_state @ Wv + bv
            q = q.reshape(b, l, KVH, GROUPS, HD).transpose(0, 2, 3, 1, 4)
            k = k.reshape(b, s, KVH, HD).transpose(0, 2, 1, 3)
            v = v.reshape(b, s, KVH, HD).transpose(0, 2, 1, 3)
            scale = 1.0 / jnp.sqrt(jnp.asarray(HD, q.dtype))
            scores = jnp.einsum('bkgld,bksd->bkgls', q, k) * scale
            scores = scores + encoder_attention_mask[:, :, None, :, :]
            attn = jax.nn.softmax(scores, axis=-1)
            out = jnp.einsum('bkgls,bksd->bkgld', attn, v)
            out = out.transpose(0, 3, 1, 2, 4).reshape(b, l, H)
            out = out @ Wo + bo
            x = out + hidden_state
            mu = jnp.mean(x, axis=-1, keepdims=True)
            var = jnp.var(x, axis=-1, keepdims=True)
            return (x - mu) * jax.lax.rsqrt(var + EPS) * gamma + beta
        key = jax.random.key(seed)
        ks = jax.random.split(key, 12)
        sd = 0.02
        return {'hidden_state': jax.random.normal(ks[0], (B, L, H), jnp.float32), 'encoder_hidden_state': jax.random.normal(ks[1], (B, S, H), jnp.float32), 'encoder_attention_mask': jnp.zeros((B, 1, L, S), jnp.float32), 'Wq': jax.random.normal(ks[2], (H, H), jnp.float32) * sd, 'bq': jnp.zeros((H,), jnp.float32), 'Wk': jax.random.normal(ks[3], (H, KVH * HD), jnp.float32) * sd, 'bk': jnp.zeros((KVH * HD,), jnp.float32), 'Wv': jax.random.normal(ks[4], (H, KVH * HD), jnp.float32) * sd, 'bv': jnp.zeros((KVH * HD,), jnp.float32), 'Wo': jax.random.normal(ks[5], (H, H), jnp.float32) * sd, 'bo': jnp.zeros((H,), jnp.float32), 'gamma': jnp.ones((H,), jnp.float32), 'beta': jnp.zeros((H,), jnp.float32)}
    _L0_xattn_all = _L0_xattn_setup()
    _L0_xattn_in = {k: v for k, v in _L0_xattn_all.items() if k in ('Wq', 'bq', 'Wk', 'bk', 'Wv', 'bv', 'Wo', 'bo', 'gamma', 'beta')}
    del _L0_xattn_all

    def _L1_xattn_setup():
        import jax, jax.numpy as jnp
        import numpy as np
        B, Q, S1, S2 = (4, 32, 256, 256)
        D, H, K, F = (256, 16, 128, 1024)
        LN_EPS = 1e-05

        def _layer_norm(x, scale, offset):
            mu = jnp.mean(x, axis=-1, keepdims=True)
            var = jnp.var(x, axis=-1, keepdims=True)
            return (x - mu) * jax.lax.rsqrt(var + LN_EPS) * scale + offset

        def _cross_attention(q_in, kv_in, wq, bq, wk, bk, wv, bv, wo, bo, bias_k, bias_v):
            b, q_len, _ = q_in.shape
            t = kv_in.shape[1]
            qh = (q_in @ wq + bq).reshape(b, q_len, H, K)
            kh = (kv_in @ wk + bk).reshape(b, t, H, K)
            vh = (kv_in @ wv + bv).reshape(b, t, H, K)
            kh = jnp.concatenate([kh, jnp.broadcast_to(bias_k, (b, 1, H, K))], axis=1)
            vh = jnp.concatenate([vh, jnp.broadcast_to(bias_v, (b, 1, H, K))], axis=1)
            scale = jnp.sqrt(jnp.asarray(K, q_in.dtype))
            logits = jnp.einsum('bqhk,bthk->bhqt', qh, kh) / scale
            weights = jax.nn.softmax(logits, axis=-1)
            ctx = jnp.einsum('bhqt,bthk->bqhk', weights, vh).reshape(b, q_len, H * K)
            return ctx @ wo + bo

        def _forward(x, xf_1, xf_2, ln1_scale, ln1_offset, wq1, bq1, wk1, bk1, wv1, bv1, wo1, bo1, bias_k1, bias_v1, ln2_scale, ln2_offset, wq2, bq2, wk2, bk2, wv2, bv2, wo2, bo2, bias_k2, bias_v2, ln_mlp_scale, ln_mlp_offset, w_fc1, b_fc1, w_fc2, b_fc2):
            res = x
            h = _layer_norm(x, ln1_scale, ln1_offset)
            x = res + _cross_attention(h, xf_1, wq1, bq1, wk1, bk1, wv1, bv1, wo1, bo1, bias_k1, bias_v1)
            res = x
            h = _layer_norm(x, ln2_scale, ln2_offset)
            x = res + _cross_attention(h, xf_2, wq2, bq2, wk2, bk2, wv2, bv2, wo2, bo2, bias_k2, bias_v2)
            h = _layer_norm(x, ln_mlp_scale, ln_mlp_offset)
            h = jax.nn.gelu(h @ w_fc1 + b_fc1, approximate=False) @ w_fc2 + b_fc2
            return x + h
        key = jax.random.key(seed)
        ks = iter(jax.random.split(key, 64))

        def rn(shape, s=0.02):
            return jax.random.normal(next(ks), shape, jnp.float32) * s
        inp = {'x': rn((B, Q, D), 1.0), 'xf_1': rn((B, S1, D), 1.0), 'xf_2': rn((B, S2, D), 1.0)}
        for i in (1, 2):
            inp[f'ln{i}_scale'] = jnp.ones((D,), jnp.float32)
            inp[f'ln{i}_offset'] = jnp.zeros((D,), jnp.float32)
            inp[f'wq{i}'] = rn((D, H * K))
            inp[f'bq{i}'] = jnp.zeros((H * K,), jnp.float32)
            inp[f'wk{i}'] = rn((D, H * K))
            inp[f'bk{i}'] = jnp.zeros((H * K,), jnp.float32)
            inp[f'wv{i}'] = rn((D, H * K))
            inp[f'bv{i}'] = jnp.zeros((H * K,), jnp.float32)
            inp[f'wo{i}'] = rn((H * K, D))
            inp[f'bo{i}'] = jnp.zeros((D,), jnp.float32)
            inp[f'bias_k{i}'] = rn((1, 1, H, K))
            inp[f'bias_v{i}'] = rn((1, 1, H, K))
        inp['ln_mlp_scale'] = jnp.ones((D,), jnp.float32)
        inp['ln_mlp_offset'] = jnp.zeros((D,), jnp.float32)
        inp['w_fc1'] = rn((D, F))
        inp['b_fc1'] = jnp.zeros((F,), jnp.float32)
        inp['w_fc2'] = rn((F, D))
        inp['b_fc2'] = jnp.zeros((D,), jnp.float32)
        return inp
    _L1_xattn_all = _L1_xattn_setup()
    _L1_xattn_in = {k: v for k, v in _L1_xattn_all.items() if k in ('ln1_scale', 'ln1_offset', 'wq1', 'bq1', 'wk1', 'bk1', 'wv1', 'bv1', 'wo1', 'bo1', 'bias_k1', 'bias_v1', 'ln2_scale', 'ln2_offset', 'wq2', 'bq2', 'wk2', 'bk2', 'wv2', 'bv2', 'wo2', 'bo2', 'bias_k2', 'bias_v2', 'ln_mlp_scale', 'ln_mlp_offset', 'w_fc1', 'b_fc1', 'w_fc2', 'b_fc2')}
    del _L1_xattn_all
    return {'x': x, 'ctx_2048': ctx_2048, 'mask_Bx1xSxS2_ff0': mask_Bx1xSxS2_ff0, 'L0_xattn_Wq': _L0_xattn_in['Wq'], 'L0_xattn_bq': _L0_xattn_in['bq'], 'L0_xattn_Wk': _L0_xattn_in['Wk'], 'L0_xattn_bk': _L0_xattn_in['bk'], 'L0_xattn_Wv': _L0_xattn_in['Wv'], 'L0_xattn_bv': _L0_xattn_in['bv'], 'L0_xattn_Wo': _L0_xattn_in['Wo'], 'L0_xattn_bo': _L0_xattn_in['bo'], 'L0_xattn_gamma': _L0_xattn_in['gamma'], 'L0_xattn_beta': _L0_xattn_in['beta'], 'L1_xattn_ln1_scale': _L1_xattn_in['ln1_scale'], 'L1_xattn_ln1_offset': _L1_xattn_in['ln1_offset'], 'L1_xattn_wq1': _L1_xattn_in['wq1'], 'L1_xattn_bq1': _L1_xattn_in['bq1'], 'L1_xattn_wk1': _L1_xattn_in['wk1'], 'L1_xattn_bk1': _L1_xattn_in['bk1'], 'L1_xattn_wv1': _L1_xattn_in['wv1'], 'L1_xattn_bv1': _L1_xattn_in['bv1'], 'L1_xattn_wo1': _L1_xattn_in['wo1'], 'L1_xattn_bo1': _L1_xattn_in['bo1'], 'L1_xattn_bias_k1': _L1_xattn_in['bias_k1'], 'L1_xattn_bias_v1': _L1_xattn_in['bias_v1'], 'L1_xattn_ln2_scale': _L1_xattn_in['ln2_scale'], 'L1_xattn_ln2_offset': _L1_xattn_in['ln2_offset'], 'L1_xattn_wq2': _L1_xattn_in['wq2'], 'L1_xattn_bq2': _L1_xattn_in['bq2'], 'L1_xattn_wk2': _L1_xattn_in['wk2'], 'L1_xattn_bk2': _L1_xattn_in['bk2'], 'L1_xattn_wv2': _L1_xattn_in['wv2'], 'L1_xattn_bv2': _L1_xattn_in['bv2'], 'L1_xattn_wo2': _L1_xattn_in['wo2'], 'L1_xattn_bo2': _L1_xattn_in['bo2'], 'L1_xattn_bias_k2': _L1_xattn_in['bias_k2'], 'L1_xattn_bias_v2': _L1_xattn_in['bias_v2'], 'L1_xattn_ln_mlp_scale': _L1_xattn_in['ln_mlp_scale'], 'L1_xattn_ln_mlp_offset': _L1_xattn_in['ln_mlp_offset'], 'L1_xattn_w_fc1': _L1_xattn_in['w_fc1'], 'L1_xattn_b_fc1': _L1_xattn_in['b_fc1'], 'L1_xattn_w_fc2': _L1_xattn_in['w_fc2'], 'L1_xattn_b_fc2': _L1_xattn_in['b_fc2']}

def reference(x, ctx_2048, mask_Bx1xSxS2_ff0, L0_xattn_Wq, L0_xattn_bq, L0_xattn_Wk, L0_xattn_bk, L0_xattn_Wv, L0_xattn_bv, L0_xattn_Wo, L0_xattn_bo, L0_xattn_gamma, L0_xattn_beta, L1_xattn_ln1_scale, L1_xattn_ln1_offset, L1_xattn_wq1, L1_xattn_bq1, L1_xattn_wk1, L1_xattn_bk1, L1_xattn_wv1, L1_xattn_bv1, L1_xattn_wo1, L1_xattn_bo1, L1_xattn_bias_k1, L1_xattn_bias_v1, L1_xattn_ln2_scale, L1_xattn_ln2_offset, L1_xattn_wq2, L1_xattn_bq2, L1_xattn_wk2, L1_xattn_bk2, L1_xattn_wv2, L1_xattn_bv2, L1_xattn_wo2, L1_xattn_bo2, L1_xattn_bias_k2, L1_xattn_bias_v2, L1_xattn_ln_mlp_scale, L1_xattn_ln_mlp_offset, L1_xattn_w_fc1, L1_xattn_b_fc1, L1_xattn_w_fc2, L1_xattn_b_fc2):
    import jax
    import jax.numpy as jnp

    def _L0_xattn_ref(hidden_state, encoder_hidden_state, encoder_attention_mask, Wq, bq, Wk, bk, Wv, bv, Wo, bo, gamma, beta):
        import jax, jax.numpy as jnp
        import numpy as np
        H = 256
        NH = 32
        KVH = 8
        HD = H // NH
        GROUPS = NH // KVH
        EPS = 1e-06
        B, L, S = (4, 128, 128)

        def _gqa_forward(hidden_state, encoder_hidden_state, encoder_attention_mask, Wq, bq, Wk, bk, Wv, bv, Wo, bo, gamma, beta):
            b, l, _ = hidden_state.shape
            s = encoder_hidden_state.shape[1]
            q = hidden_state @ Wq + bq
            k = encoder_hidden_state @ Wk + bk
            v = encoder_hidden_state @ Wv + bv
            q = q.reshape(b, l, KVH, GROUPS, HD).transpose(0, 2, 3, 1, 4)
            k = k.reshape(b, s, KVH, HD).transpose(0, 2, 1, 3)
            v = v.reshape(b, s, KVH, HD).transpose(0, 2, 1, 3)
            scale = 1.0 / jnp.sqrt(jnp.asarray(HD, q.dtype))
            scores = jnp.einsum('bkgld,bksd->bkgls', q, k) * scale
            scores = scores + encoder_attention_mask[:, :, None, :, :]
            attn = jax.nn.softmax(scores, axis=-1)
            out = jnp.einsum('bkgls,bksd->bkgld', attn, v)
            out = out.transpose(0, 3, 1, 2, 4).reshape(b, l, H)
            out = out @ Wo + bo
            x = out + hidden_state
            mu = jnp.mean(x, axis=-1, keepdims=True)
            var = jnp.var(x, axis=-1, keepdims=True)
            return (x - mu) * jax.lax.rsqrt(var + EPS) * gamma + beta
        return _gqa_forward(hidden_state, encoder_hidden_state, encoder_attention_mask, Wq, bq, Wk, bk, Wv, bv, Wo, bo, gamma, beta)

    def _L1_xattn_ref(x, xf_1, xf_2, ln1_scale, ln1_offset, wq1, bq1, wk1, bk1, wv1, bv1, wo1, bo1, bias_k1, bias_v1, ln2_scale, ln2_offset, wq2, bq2, wk2, bk2, wv2, bv2, wo2, bo2, bias_k2, bias_v2, ln_mlp_scale, ln_mlp_offset, w_fc1, b_fc1, w_fc2, b_fc2):
        import jax, jax.numpy as jnp
        import numpy as np
        B, Q, S1, S2 = (4, 32, 256, 256)
        D, H, K, F = (256, 16, 128, 1024)
        LN_EPS = 1e-05

        def _layer_norm(x, scale, offset):
            mu = jnp.mean(x, axis=-1, keepdims=True)
            var = jnp.var(x, axis=-1, keepdims=True)
            return (x - mu) * jax.lax.rsqrt(var + LN_EPS) * scale + offset

        def _cross_attention(q_in, kv_in, wq, bq, wk, bk, wv, bv, wo, bo, bias_k, bias_v):
            b, q_len, _ = q_in.shape
            t = kv_in.shape[1]
            qh = (q_in @ wq + bq).reshape(b, q_len, H, K)
            kh = (kv_in @ wk + bk).reshape(b, t, H, K)
            vh = (kv_in @ wv + bv).reshape(b, t, H, K)
            kh = jnp.concatenate([kh, jnp.broadcast_to(bias_k, (b, 1, H, K))], axis=1)
            vh = jnp.concatenate([vh, jnp.broadcast_to(bias_v, (b, 1, H, K))], axis=1)
            scale = jnp.sqrt(jnp.asarray(K, q_in.dtype))
            logits = jnp.einsum('bqhk,bthk->bhqt', qh, kh) / scale
            weights = jax.nn.softmax(logits, axis=-1)
            ctx = jnp.einsum('bhqt,bthk->bqhk', weights, vh).reshape(b, q_len, H * K)
            return ctx @ wo + bo

        def _forward(x, xf_1, xf_2, ln1_scale, ln1_offset, wq1, bq1, wk1, bk1, wv1, bv1, wo1, bo1, bias_k1, bias_v1, ln2_scale, ln2_offset, wq2, bq2, wk2, bk2, wv2, bv2, wo2, bo2, bias_k2, bias_v2, ln_mlp_scale, ln_mlp_offset, w_fc1, b_fc1, w_fc2, b_fc2):
            res = x
            h = _layer_norm(x, ln1_scale, ln1_offset)
            x = res + _cross_attention(h, xf_1, wq1, bq1, wk1, bk1, wv1, bv1, wo1, bo1, bias_k1, bias_v1)
            res = x
            h = _layer_norm(x, ln2_scale, ln2_offset)
            x = res + _cross_attention(h, xf_2, wq2, bq2, wk2, bk2, wv2, bv2, wo2, bo2, bias_k2, bias_v2)
            h = _layer_norm(x, ln_mlp_scale, ln_mlp_offset)
            h = jax.nn.gelu(h @ w_fc1 + b_fc1, approximate=False) @ w_fc2 + b_fc2
            return x + h
        return _forward(x, xf_1, xf_2, ln1_scale, ln1_offset, wq1, bq1, wk1, bk1, wv1, bv1, wo1, bo1, bias_k1, bias_v1, ln2_scale, ln2_offset, wq2, bq2, wk2, bk2, wv2, bv2, wo2, bo2, bias_k2, bias_v2, ln_mlp_scale, ln_mlp_offset, w_fc1, b_fc1, w_fc2, b_fc2)
    x = _L0_xattn_ref(x, ctx_2048, mask_Bx1xSxS2_ff0, L0_xattn_Wq, L0_xattn_bq, L0_xattn_Wk, L0_xattn_bk, L0_xattn_Wv, L0_xattn_bv, L0_xattn_Wo, L0_xattn_bo, L0_xattn_gamma, L0_xattn_beta)
    x = _L1_xattn_ref(x, ctx_2048, ctx_2048, L1_xattn_ln1_scale, L1_xattn_ln1_offset, L1_xattn_wq1, L1_xattn_bq1, L1_xattn_wk1, L1_xattn_bk1, L1_xattn_wv1, L1_xattn_bv1, L1_xattn_wo1, L1_xattn_bo1, L1_xattn_bias_k1, L1_xattn_bias_v1, L1_xattn_ln2_scale, L1_xattn_ln2_offset, L1_xattn_wq2, L1_xattn_bq2, L1_xattn_wk2, L1_xattn_bk2, L1_xattn_wv2, L1_xattn_bv2, L1_xattn_wo2, L1_xattn_bo2, L1_xattn_bias_k2, L1_xattn_bias_v2, L1_xattn_ln_mlp_scale, L1_xattn_ln_mlp_offset, L1_xattn_w_fc1, L1_xattn_b_fc1, L1_xattn_w_fc2, L1_xattn_b_fc2)
    return x

_drawn_inputs = setup_inputs


def setup_inputs(seed=0):
    import zlib

    import numpy as np

    out = dict(_drawn_inputs(seed))
    spreads = {'L0_xattn_bq': (0.0, 0.8),
     'L0_xattn_bk': (0.0, 2.0),
     'L0_xattn_bv': (0.0, 0.1),
     'L0_xattn_bo': (0.0, 0.1),
     'L0_xattn_gamma': (1.0, 0.2),
     'L0_xattn_beta': (0.0, 0.1),
     'L1_xattn_ln1_scale': (1.0, 0.6),
     'L1_xattn_ln1_offset': (0.0, 0.8),
     'L1_xattn_bq1': (0.0, 0.8),
     'L1_xattn_bk1': (0.0, 2.0),
     'L1_xattn_bv1': (0.0, 0.1),
     'L1_xattn_bo1': (0.0, 0.1),
     'L1_xattn_ln2_scale': (1.0, 0.6),
     'L1_xattn_ln2_offset': (0.0, 0.8),
     'L1_xattn_bq2': (0.0, 0.8),
     'L1_xattn_bk2': (0.0, 2.0),
     'L1_xattn_bv2': (0.0, 0.1),
     'L1_xattn_bo2': (0.0, 0.1),
     'L1_xattn_ln_mlp_scale': (1.0, 0.6),
     'L1_xattn_ln_mlp_offset': (0.0, 0.7),
     'L1_xattn_b_fc1': (0.0, 0.1),
     'L1_xattn_b_fc2': (0.0, 0.1)}
    factors = {'L0_xattn_Wq': 8.0,
     'L0_xattn_Wk': 8.0,
     'L1_xattn_wq1': 8.0,
     'L1_xattn_wk1': 8.0,
     'L1_xattn_bias_k1': 64.0,
     'L1_xattn_bias_v1': 56.691,
     'L1_xattn_wq2': 8.0,
     'L1_xattn_wk2': 8.0,
     'L1_xattn_bias_k2': 64.0,
     'L1_xattn_bias_v2': 64.0}
    for name, (base, spread) in spreads.items():
        noise = np.random.default_rng([zlib.crc32(name.encode()), seed]).standard_normal(out[name].shape)
        drawn = base * np.exp(spread * noise) if base else spread * noise
        out[name] = jnp.asarray(drawn.astype(out[name].dtype))
    for name, factor in factors.items():
        out[name] = (out[name] * factor).astype(out[name].dtype)
    return out
```

```python
from contextlib import ExitStack

import concourse.bass as bass
from concourse import mybir

F32 = mybir.dt.float32
ALU = mybir.AluOpType
ACT = mybir.ActivationFunctionType
AX_X = mybir.AxisListType.X

P = 128
B, S, S2, D = 4, 256, 64, 256
DC = D // P
TILES = B * S // P
NH, KVH, HD = 32, 8, 8
G = NH // KVH
QUARTERS, QH = 4, NH // 4
NHC = P // HD
VO = HD + 1
LAYERS, H, K = 2, 16, 128
HP = H // 2
KEYS = S2 + 1
CK = B * S2
SLOTS = 4
F = 1024
FC = F // P
HALF = 4
W_K, W_QT, W_V, W_O, W_BV = 0, D, 2 * D, 3 * D, 4 * D
W_COL = W_BV + H
W_N = W_COL + 4
EPS0, EPS1 = 1e-6, 1e-5
SCALE0, SCALE1 = HD ** -0.5, K ** -0.5
N_FILLS = 9
LN_NM = TILES * (1 + LAYERS)


def some(n):
    return not (isinstance(n, int) and n <= 0)


def ln_of0(i):
    return TILES + 1 if isinstance(i, int) and i == TILES - 1 else i


def ln_of1(n):
    return TILES - 1 + n if isinstance(n, int) and n < 2 else TILES + n


def build(nc, x_tok, xT_d, ctxT_d, mask_d, w0_d, cols0_d, rows_d, heads_d, bo_d, ln_d, fc1_d, bfc1_d, fc2_d,
          blockmask_d, ident_d, out_d):
    with ExitStack() as ctx:
        def sb(name, shape):
            return ctx.enter_context(nc.sbuf_tensor(name, shape, F32))

        def pb(name, shape):
            return ctx.enter_context(nc.psum_tensor(name, shape, F32))

        def sem(name):
            return ctx.enter_context(nc.semaphore(name))

        ident = sb("ident", [P, P])
        ones = sb("ones", [P, P])
        expo = sb("expo", [P, 1])
        eps0, eps1 = sb("eps0", [P, 1]), sb("eps1", [P, 1])
        X = sb("X", [P, TILES, D])
        ctxT = sb("ctxT", [P, DC, CK])
        stats = sb("stats", [P, 6])
        carrier = sb("carrier", [P, 1])
        pool_carrier = sb("pool_carrier", [P, 1])
        mv = sb("mv", [P, 2])
        ve = sb("ve", [P, 1])
        rstd = sb("rstd", [P, 1])
        xT = sb("xT", [P, DC, B * S])
        mask = sb("mask", [P, TILES, S2])
        w0 = sb("w0", [P, DC, D + KVH * HD * 2 + D])
        wk_rep = sb("wk_rep", [P, DC, D])
        cols0 = sb("cols0", [P, 4])
        bq_s = sb("bq_s", [P, DC])
        rows = sb("rows", [P, 4 * D + KVH * HD])
        kT0 = sb("kT0", [P, DC, CK])
        blockmask = sb("blockmask", [P, NHC])
        kblk = sb("kblk", [P, DC, NHC, S2])
        vblk = sb("vblk", [P, B, KVH, 2 * VO])
        qT0 = sb("qT0", [P, DC, S])
        scores_sb = sb("scores_sb", [P, 2, NH * S2])
        sc0 = [scores_sb[:, i, :] for i in range(2)]
        mx0 = sb("mx0", [P, NH])
        pT0 = sb("pT0", [P, NH // 2, P])
        rden0 = sb("rden0", [P, NH])
        o0 = [sb(f"o0_{i}", [P, D]) for i in range(2)]
        oT0 = sb("oT0", [P, DC, P])
        y0 = sb("y0", [P, D])
        z0 = sb("z0", [P, D])
        z1 = sb("z1", [P, D])
        ring = [sb(f"ring{w}", [P, W_N]) for w in range(SLOTS)]
        kTs = sb("kTs", [P, CK + 1])
        vTs = sb("vTs", [P, CK])
        bq_all = sb("bq_all", [P, P])
        AC = sb("AC", [P, DC + 1, B, H, S2])
        ACb = sb("ACb", [P, DC + 1, H])
        VW = sb("VW", [P, B, HP, D])
        VWb = sb("VWb", [H + 1, D])
        ln_all = sb("ln_all", [P, (LAYERS + 1) * 4])
        xn = [sb(f"xn{i}", [P, D]) for i in range(HALF)]
        hT = [sb(f"hT{i}", [P, DC, P]) for i in range(2)]
        sx = sb("sx", [P, H, KEYS])
        px = sb("px", [P, H, KEYS])
        pm = sb("pm", [P, H, S2])
        pmb = sb("pmb", [P, H + 1])
        mx = sb("mx", [P, H])
        sm = sb("sm", [P, H])
        rs = sb("rs", [P, H])
        pT = pT0[:, 0:HP, :]
        pTb = sb("pTb", [H + 1, P])
        fc1 = sb("fc1", [P, DC, F])
        bfc1 = sb("bfc1", [P, FC])
        fc2 = kblk[:, :, :, :].rearrange("p c h t -> p (c h t)").rearrange("p (f d) -> p f d", f=FC)
        hTm = xT
        gT = scores_sb[:, :, :].rearrange("p i (f t) -> p (i f) t", t=HALF * P)

        s_banks = pb("s_banks", [P, 4, 512])
        bank4 = pb("bank4", [P, 512])
        bank5 = pb("bank5", [P, 512])
        bank6 = pb("bank6", [P, 512])
        bank7 = pb("bank7", [P, 512])
        s0_ps = s_banks[:, 0, :]
        pT0_ps = s_banks[:, 1, :]
        o0_ps = s_banks[:, 2, 0:NH * VO]
        oT0_ps = s_banks[:, 3, 0:D]
        wo0_ps = s_banks[:, 3, 256:256 + D]
        q0_ps = [s_banks[:, 3, c * S:(c + 1) * S] for c in range(DC)]
        first_hT_ps = [s_banks[:, 3, i * D:(i + 1) * D] for i in range(2)]
        kT_ps = bank4[:, 0:CK]
        vT_ps = [bank4[:, 256:256 + CK], s_banks[:, 2, 0:CK]]
        vwb_ps = [bank4[0:H, 0:D], s_banks[0:H, 1, 0:D]]
        vw_ps = bank5[:, :].rearrange("p (b d) -> p b d", b=2)
        ac_ps = [bank6[:, 0:CK + 1], bank7[:, 0:CK + 1]]
        sx_ps = s_banks[:, 0:2, :]
        sxb_ps = s_banks[:, 2, 0:H]
        pTb_ps = s_banks[0:H + 1, 3, 0:P]
        pT_ps = [bank4, bank5]
        o_ps = bank6[:, 0:D]
        hT_ps = bank7[:, 0:D]
        hTm_ps = [bank7[:, 0:D], s_banks[:, 2, 0:D]]
        g_ps = [bank4, bank5]
        y_ps = [bank6[:, 0:D], s_banks[:, 0, 0:D]]

        ctx_in, w0_in, x_in, xt0_in, xt_in, mask_in, const_in, rows_in, mlp_in = (
            sem(n) for n in ("ctx_in", "w0_in", "x_in", "xt0_in", "xt_in", "mask_in", "const_in", "rows_in", "mlp_in"))
        out_done = sem("out_done")
        fills = sem("fills")
        wkrep_done = sem("wkrep_done")
        ln_stats, ln_mv, ln_eps, ln_rstd, ln_done = (
            sem(n) for n in ("ln_stats", "ln_mv", "ln_eps", "ln_rstd", "ln_done"))
        bqs_done, kT0_mm, kT0_out, v0_mm, v0_out, q0_mm, q0_out, kblk_done = (
            sem(n) for n in ("bqs_done", "kT0_mm", "kT0_out", "v0_mm", "v0_out", "q0_mm", "q0_out", "kblk_done"))
        s0_mm, sc0_done, mx0_done, sub0_done, exp0_done = (
            sem(n) for n in ("s0_mm", "sc0_done", "mx0_done", "sub0_done", "exp0_done"))
        pT0_mm, pT0_out, pv0_mm, rden0_done, o0_done, oT0_mm, oT0_out, wo0_mm, y0_done = (
            sem(n) for n in ("pT0_mm", "pT0_out", "pv0_mm", "rden0_done", "o0_done", "oT0_mm", "oT0_out",
                             "wo0_mm", "y0_done"))
        xbo_done, z1_done, x1_done = (sem(n) for n in ("xbo_done", "z1_done", "x1_done"))
        w_in = [sem(f"w_in{w}") for w in range(SLOTS)]
        bo_in = sem("bo_in")
        kT_mm, kT_out, vT_mm, vT_out, headcols, ac_mm, ac_out = (
            sem(n) for n in ("kT_mm", "kT_out", "vT_mm", "vT_out", "headcols", "ac_mm", "ac_out"))
        vw_mm, vw_out_dve, vw_out_act, vwb_mm, vwb_out = (
            sem(n) for n in ("vw_mm", "vw_out_dve", "vw_out_act", "vwb_mm", "vwb_out"))
        vwb_zero = sem("vwb_zero")
        hT_mm, hT_out, s_mm, sx_done, mx_done, sub_done, exp_done, sm_done, rs_done, pm_done = (
            sem(n) for n in ("hT_mm", "hT_out", "s_mm", "sx_done", "mx_done", "sub_done", "exp_done", "sm_done",
                             "rs_done", "pm_done"))
        pT_mm, pT_out, o_mm, x_done = (sem(n) for n in ("pT_mm", "pT_out", "o_mm", "x_done"))
        hTm_mm, hTm_out, g_mm, g_out, y_mm, y_done = (
            sem(n) for n in ("hTm_mm", "hTm_out", "g_mm", "g_out", "y_mm", "y_done"))
        xb2_done = sem("xb2_done")

        block = ctx.enter_context(nc.Block())
        ROUNDS = LAYERS * H // SLOTS
        HEADS0 = H

        @block.sync
        def _(sp):
            sp.dma_start(ctxT[:], ctxT_d).then_inc(ctx_in, 16)
            sp.dma_start(w0[:], w0_d).then_inc(w0_in, 16)
            sp.dma_start(ring[0][:], heads_d[0]).then_inc(w_in[0], 16)
            sp.dma_start(mask[:], mask_d).then_inc(mask_in, 16)
            sp.dma_start(ring[1][:], heads_d[1]).then_inc(w_in[1], 16)
            sp.dma_start(X[:], x_tok).then_inc(x_in, 16)
            for w in range(2, SLOTS):
                sp.dma_start(ring[w][:], heads_d[w]).then_inc(w_in[w], 16)
            sp.dma_start(xT[:, :, S:], xT_d[:, :, S:]).then_inc(xt_in, 16)
            sp.dma_start(VWb[H:H + 1, :], bo_d[0:1, :]).then_inc(bo_in, 16)
            with sp.Fori(1, ROUNDS) as r:
                for w in range(SLOTS):
                    sp.wait_ge(vw_mm, SLOTS * (r - 1) + w + 1)
                    sp.dma_start(ring[w][:], heads_d[SLOTS * r + w]).then_inc(w_in[w], 16)
            sp.wait_ge(x_done, TILES)
            sp.dma_start(VWb[H:H + 1, :], bo_d[1:2, :]).then_inc(bo_in, 16)
            sp.dma_start(fc1[:], fc1_d).then_inc(mlp_in, 16)
            sp.dma_start(bfc1[:], bfc1_d).then_inc(mlp_in, 16)
            sp.dma_start(fc2[:], fc2_d).then_inc(mlp_in, 16)
            for i in range(TILES):
                sp.wait_ge(y_done, i + 1)
                sp.dma_start(out_d[:, i, :], X[:, i, :]).then_inc(out_done, 16)
            sp.wait_ge(out_done, 16 * TILES)

        @block.gpsimd
        def _(pool):
            pool.memset(ones[:], 1.0).then_inc(fills, 1)
            pool.memset(expo[:], -0.5).then_inc(fills, 1)
            pool.memset(eps0[:], EPS0).then_inc(fills, 1)
            pool.memset(eps1[:], EPS1).then_inc(fills, 1)
            pool.memset(vblk[:], 0.0).then_inc(fills, 1)
            pool.memset(pmb[:], 1.0).then_inc(fills, 1)
            pool.memset(VWb[0:H, :], 0.0).then_inc(fills, 1)
            pool.wait_ge(fills, 7)
            pool.memset(vblk[0:S2, :, :, HD:HD + 1], 1.0).then_inc(fills, 1)
            pool.wait_ge(fills, 8)
            pool.memset(vblk[S2:P, :, :, VO + HD:VO + HD + 1], 1.0).then_inc(fills, 1)
            pool.wait_ge(fills, N_FILLS)

            def key_blocks(b):
                pool.wait_ge(s0_mm, 2 * QUARTERS * b)
                for c in range(DC):
                    pool.tensor_tensor(
                        kblk[:, c], kT0[:, c, bass.ds(b * S2, S2)].unsqueeze(1).to_broadcast([P, NHC, S2]),
                        blockmask[:, :].unsqueeze(2).to_broadcast([P, NHC, S2]), ALU.mult).then_inc(kblk_done, 1)

            def rstd_of(n, eps):
                pool.wait_ge(ln_mv, n + 1)
                pool.tensor_tensor(ve[:], mv[:, 1:2], eps, ALU.add).then_inc(ln_eps, 1)
                pool.wait_ge(ln_eps, n + 1)
                pool.tensor_tensor(rstd[:], ve[:], expo[:], ALU.pow).then_inc(ln_rstd, 1)

            def x_plus_bo(i):
                at = X[:, bass.ds(i, 1), :].rearrange("p a d -> p (a d)")
                pool.tensor_tensor(at, at, rows[:, 0:D], ALU.add).then_inc(xbo_done, 1)

            def gamma_beta(i):
                pool.wait_ge(ln_done, ln_of0(i) + 1)
                pool.tensor_tensor(z1[:], z0[:], rows[:, D:2 * D], ALU.mult).then_inc(z1_done, 1)
                pool.wait_ge(z1_done, i + 1)
                pool.tensor_tensor(pool_carrier[:], ones[:, 0:1], ones[:, 0:1], ALU.mult)
                pool.tensor_tensor(X[:, bass.ds(i, 1), :].rearrange("p a d -> p (a d)"), z1[:], rows[:, 2 * D:3 * D],
                                   ALU.add).then_inc(x1_done, 1)

            def head_columns(h, w):
                pool.wait_ge(w_in[w], (h - w) * 4 + 16)
                if some(h):
                    pool.wait_ge(ac_mm, 3 * h)
                pool.tensor_tensor(kTs[:, CK:CK + 1], ones[:, 0:1], ring[w][:, W_COL + 2:W_COL + 3], ALU.mult)\
                    .then_inc(headcols, 1)
                pool.tensor_tensor(bq_all[:], ones[:], ring[w][:, W_COL + 1:W_COL + 2].to_broadcast([P, P]), ALU.mult)\
                    .then_inc(headcols, 1)

            def pair0(b, first=False, last=False):
                for p in range(2):
                    i = 2 * b + p
                    for w in (2 * p, 2 * p + 1):
                        head_columns(SLOTS * b + w, w)
                    if not (first and p == 0):
                        rstd_of(i - 1, eps0[:])
                    if p == 0 and not last:
                        key_blocks(b + 1)
                    x_plus_bo(i)
                    if not (first and p == 0):
                        gamma_beta(i - 1)

            pool.wait_ge(const_in, 64)
            pool.wait_ge(kT0_out, DC)
            pool.wait_ge(x_in, 16)
            pool.wait_ge(rows_in, 16 * 5)
            pair0(0, first=True)
            with pool.Fori(1, B - 1) as b:
                pair0(b)
            pair0(B - 1, last=True)
            for n in range(2):
                rstd_of(ln_of1(n), eps1[:])
            rstd_of(ln_of0(TILES - 1), eps0[:])
            gamma_beta(TILES - 1)
            with pool.Fori(2, TILES + 2) as n:
                rstd_of(ln_of1(n), eps1[:])
            with pool.Fori(H, LAYERS * H, SLOTS) as h:
                for w in range(SLOTS):
                    head_columns(h + w, w)
            with pool.Fori(TILES + 2, LAYERS * TILES + TILES) as n:
                rstd_of(ln_of1(n), eps1[:])

        @block.scalar
        def _(act):
            act.dma_start(xT[:, :, 0:S], xT_d[:, :, 0:S]).then_inc(xt0_in, 16)
            act.dma_start(cols0[:], cols0_d).then_inc(const_in, 16)
            act.dma_start(blockmask[:], blockmask_d).then_inc(const_in, 16)
            act.dma_start(rows[:, 4 * D:], rows_d[0:1, 4 * D:].to_broadcast([P, KVH * HD])).then_inc(rows_in, 16)
            act.dma_start(ident[:], ident_d).then_inc(const_in, 16)
            act.dma_start(ln_all[:], ln_d).then_inc(const_in, 16)
            for j in range(4):
                act.dma_start(rows[:, j * D:(j + 1) * D], rows_d[0:1, j * D:(j + 1) * D].to_broadcast([P, D]))\
                    .then_inc(rows_in, 16)
            act.wait_ge(const_in, 64)
            nc.scalar.mul(bq_s[:], cols0[:, 0:DC], SCALE0).then_inc(bqs_done, 1)
            for c in range(DC):
                act.wait_ge(kT0_mm, c + 1)
                nc.scalar.activation(kT0[:, c], s_banks[:, c, 0:CK], ACT.Identity,
                                     bias=cols0[:, DC + c:DC + c + 1]).then_inc(kT0_out, 1)

            def q_out(b):
                if some(b):
                    act.wait_ge(s0_mm, 2 * QUARTERS * b)
                act.wait_ge(q0_mm, DC * b + DC)
                for c in range(DC):
                    nc.scalar.activation(qT0[:, c], q0_ps[c], ACT.Identity, bias=bq_s[:, c:c + 1],
                                         scale=SCALE0).then_inc(q0_out, 1)

            def exp0(i, p):
                act.wait_ge(sub0_done, i + 1)
                nc.scalar.activation(sc0[p], sc0[p], ACT.Exp).then_inc(exp0_done, 1)

            def pT0_copy(i, g):
                act.wait_ge(pT0_mm, 4 * i + g + 1)
                if g == 0 and some(i):
                    act.wait_ge(pv0_mm, i)
                nc.scalar.copy(pT0[:, 4 * g:4 * g + 4], pT0_ps.rearrange("p (j t) -> p j t", j=4))\
                    .then_inc(pT0_out, 1)

            def oT0_copy(i):
                act.wait_ge(oT0_mm, i + 1)
                nc.scalar.copy(oT0[:], oT0_ps.rearrange("p (c t) -> p c t", c=DC)).then_inc(oT0_out, 1)

            def kT_copy(h, w):
                act.wait_ge(kT_mm, h + 1)
                nc.scalar.activation(kTs[:, 0:CK], kT_ps, ACT.Identity, bias=ring[w][:, W_COL:W_COL + 1])\
                    .then_inc(kT_out, 1)

            def vT_copy(h, w, layer):
                act.wait_ge(vT_mm, h + 1)
                nc.scalar.activation(vTs[:], vT_ps[layer], ACT.Identity, bias=ring[w][:, W_COL + 3:W_COL + 4])\
                    .then_inc(vT_out, 1)

            def vw_odd(h, hp, w):
                act.wait_ge(vw_mm, h + 1)
                rows_to = slice(S2 * (w % 2), S2 * (w % 2) + S2)
                nc.scalar.copy(VW[rows_to, 1::2, hp, :], vw_ps[S2:P]).then_inc(vw_out_act, 1)

            def hT_out_of(ps, n, p, layer):
                at = 4 * layer
                for c in range(DC):
                    nc.scalar.activation(hT[p][:, c], ps[:, c * P:(c + 1) * P], ACT.Identity,
                                         bias=ln_all[:, at + DC + c:at + DC + c + 1],
                                         scale=ln_all[:, at + c:at + c + 1]).then_inc(hT_out, 1)

            def tile0(b, p, first=False, last=False):
                i = 2 * b + p
                w1, w2 = 2 * p, 2 * p + 1
                h1, h2 = SLOTS * b + w1, SLOTS * b + w2
                hp = 2 * b + p
                kT_copy(h1, w1)
                vT_copy(h1, w1, 0)
                if not (first and p == 0):
                    oT0_copy(i - 1)
                pT0_copy(i, 0)
                vw_odd(h1, hp, w1)
                pT0_copy(i, 1)
                kT_copy(h2, w2)
                pT0_copy(i, 2)
                vT_copy(h2, w2, 0)
                pT0_copy(i, 3)
                if p == 0 and not last:
                    q_out(b + 1)
                if p == 1 and last:
                    act.wait_ge(hT_mm, 2)
                    for n in range(2):
                        hT_out_of(first_hT_ps[n], n, n, 0)
                    oT0_copy(i)
                else:
                    exp0(i + 1, 1 - p)
                vw_odd(h2, hp, w2)

            act.wait_ge(bqs_done, 1)
            q_out(0)
            exp0(0, 0)
            tile0(0, 0, first=True)
            tile0(0, 1, first=True)
            with act.Fori(1, B - 1) as b:
                tile0(b, 0)
                tile0(b, 1)
            tile0(B - 1, 0, last=True)
            tile0(B - 1, 1, last=True)

            def hT_copies(n, p, layer):
                act.wait_ge(hT_mm, n + 1)
                act.wait_ge(s_mm, n - 1)
                hT_out_of(hT_ps, n, p, layer)

            def exp1(n):
                act.wait_ge(sub_done, n + 1)
                nc.scalar.activation(px[:], sx[:], ACT.Exp, scale=SCALE1).then_inc(exp_done, 1)

            def pT_copies(n):
                for g in range(2):
                    act.wait_ge(pT_mm, 3 * n + g + 1)
                    if g == 0 and some(n):
                        act.wait_ge(o_mm, n)
                    nc.scalar.copy(pT[:, 4 * g:4 * g + 4], pT_ps[g][:, :].rearrange("p (j t) -> p j t", j=4))\
                        .then_inc(pT_out, 1)
                act.wait_ge(pT_mm, 3 * n + 3)
                nc.scalar.copy(pTb[:], pTb_ps).then_inc(pT_out, 1)

            def hTm_copies(i):
                act.wait_ge(hTm_mm, i + 1)
                at = 4 * LAYERS
                for c in range(DC):
                    nc.scalar.activation(hTm[:, c, i * P:(i + 1) * P], hTm_ps[i % 2][:, c * P:(c + 1) * P],
                                         ACT.Identity, bias=ln_all[:, at + DC + c:at + DC + c + 1],
                                         scale=ln_all[:, at + c:at + c + 1]).then_inc(hTm_out, 1)

            def attention(layer):
                def pair(n, last=False):
                    for p in range(2):
                        exp1(n + p)
                        pT_copies(n + p)
                        if not last:
                            hT_copies(n + p + 2, p, layer)
                        elif layer + 1 < LAYERS:
                            hT_copies(n + p + 2, p, layer + 1)
                        else:
                            hTm_copies(2 * p)
                            hTm_copies(2 * p + 1)

                n0 = layer * TILES
                pair(n0)
                with act.Fori(1, B - 1) as b:
                    pair(b * 2 + n0)
                pair(n0 + TILES - 2, last=True)

            attention(0)
            with act.Fori(SLOTS, LAYERS * SLOTS) as r:
                for w in range(SLOTS):
                    h = r * SLOTS + w
                    kT_copy(h, w)
                    vT_copy(h, w, 1)
                    vw_odd(h, (r - SLOTS) * 2 + w // 2, w)
            attention(1)

            act.wait_ge(mlp_in, 48)
            for half in range(TILES // HALF):
                if half:
                    act.wait_ge(y_mm, half * HALF)
                for f in range(FC):
                    if half == 0 and f >= HALF:
                        hTm_copies(f)
                    act.wait_ge(g_mm, half * FC + f + 1)
                    nc.scalar.activation(gT[:, f], g_ps[f % 2][:, :], ACT.Gelu, bias=bfc1[:, f:f + 1])\
                        .then_inc(g_out, 1)

        @block.vector
        def _(dve):
            dve.wait_ge(w0_in, 16)
            for c in range(DC):
                nc.vector.tensor_copy(
                    wk_rep[:, c].rearrange("p (k g d) -> p k g d", k=KVH, g=G),
                    w0[:, c, D:D + KVH * HD].rearrange("p (k d) -> p k d", k=KVH).unsqueeze(2)
                    .to_broadcast([P, KVH, G, HD])).then_inc(wkrep_done, 1)
            dve.wait_ge(const_in, 64)
            for c in range(DC):
                dve.wait_ge(kT0_out, c + 1)
                nc.vector.tensor_tensor(
                    kblk[:, c], kT0[:, c, 0:S2].unsqueeze(1).to_broadcast([P, NHC, S2]),
                    blockmask[:, :].unsqueeze(2).to_broadcast([P, NHC, S2]), ALU.mult).then_inc(kblk_done, 1)
            dve.wait_ge(fills, N_FILLS)
            dve.wait_ge(rows_in, 16 * 5)
            dve.wait_ge(v0_mm, 1)
            v_ps = s_banks[:, 2, 0:B * KVH * HD].rearrange("p (b k d) -> p b k d", b=B, k=KVH)
            bv = rows[:, 4 * D:].rearrange("p (k d) -> p k d", k=KVH).unsqueeze(1).to_broadcast([P, B, KVH, HD])
            for half in range(2):
                part = slice(S2 * half, S2 * half + S2)
                nc.vector.tensor_tensor(vblk[part, :, :, VO * half:VO * half + HD], v_ps[part], bv[part], ALU.add)\
                    .then_inc(v0_out, 1)

            def tile_of(i):
                return X[:, bass.ds(i, 1), :].rearrange("p a d -> p (a d)")

            def ln_moments(x, n):
                if some(n):
                    dve.wait_ge(ln_done, n)
                nc.vector.bn_stats(stats[:], x).then_inc(ln_stats, 1)
                dve.wait_ge(ln_stats, n + 1)
                nc.vector.tensor_copy(carrier[:], stats[:, 0:1])
                nc.vector.bn_aggr(mv[:], stats[:]).then_inc(ln_mv, 1)

            def ln_normal(out, x, n):
                dve.wait_ge(ln_rstd, n + 1)
                nc.vector.tensor_scalar(out, x, mv[:, 0:1], rstd[:], ALU.subtract, ALU.mult).then_inc(ln_done, 1)

            dve.wait_ge(mask_in, 16)

            def masked0(i, p, q):
                if q == 0 and not (isinstance(i, int) and i < 2):
                    dve.wait_ge(pT0_mm, 4 * i - 4)
                dve.wait_ge(s0_mm, QUARTERS * i + q + 1)
                nc.vector.tensor_tensor(
                    sc0[p][:, q * QH * S2:(q + 1) * QH * S2].rearrange("p (h t) -> p h t", t=S2),
                    s0_ps.rearrange("p (j t) -> p j t", t=S2),
                    mask[:, bass.ds(i, 1), :].to_broadcast([P, QH, S2]), ALU.add).then_inc(sc0_done, 1)

            def max0(i, p):
                dve.wait_ge(sc0_done, QUARTERS * i + QUARTERS)
                nc.vector.tensor_reduce(mx0[:], sc0[p].rearrange("p (h t) -> p h t", t=S2), AX_X, ALU.max)\
                    .then_inc(mx0_done, 1)

            def sub0(i, p):
                dve.wait_ge(mx0_done, i + 1)
                nc.vector.tensor_tensor(
                    sc0[p].rearrange("p (h t) -> p h t", t=S2), sc0[p].rearrange("p (h t) -> p h t", t=S2),
                    mx0[:].unsqueeze(2).to_broadcast([P, NH, S2]), ALU.subtract).then_inc(sub0_done, 1)

            def out0(i, p):
                dve.wait_ge(pv0_mm, i + 1)
                o = o0_ps.rearrange("p (h e) -> p h e", e=VO)
                nc.vector.reciprocal(rden0[:].unsqueeze(2), o[:, :, HD:VO]).then_inc(rden0_done, 1)
                dve.wait_ge(rden0_done, i + 1)
                nc.vector.tensor_tensor(o0[p][:].rearrange("p (h d) -> p h d", d=HD), o[:, :, 0:HD],
                                        rden0[:].unsqueeze(2).to_broadcast([P, NH, HD]), ALU.mult)\
                    .then_inc(o0_done, 1)

            def residual0(i):
                dve.wait_ge(wo0_mm, i + 1)
                if some(i):
                    dve.wait_ge(ln_done, ln_of0(i))
                dve.wait_ge(xbo_done, i + 1)
                nc.vector.tensor_tensor(y0[:], wo0_ps, tile_of(i), ALU.add).then_inc(y0_done, 1)
                dve.wait_ge(y0_done, i + 1)
                ln_moments(y0[:], ln_of0(i))

            def normal0(i):
                if some(i):
                    dve.wait_ge(z1_done, i)
                ln_normal(z0[:], y0[:], ln_of0(i))

            def ac_copy(h, hh, w, j):
                dve.wait_ge(ac_mm, 3 * h + j + 1)
                ps = ac_ps[(w + j) % 2]
                nc.vector.tensor_copy(AC[:, j, :, hh, :].rearrange("p b a t -> p b (a t)"),
                                      ps[:, 0:CK].rearrange("p (b t) -> p b t", b=B)).then_inc(ac_out, 1)
                nc.vector.tensor_copy(ACb[:, j, hh], ps[:, CK:CK + 1]).then_inc(ac_out, 1)

            def vwb_add(h, layer):
                dve.wait_ge(vwb_mm, h + 1)
                if some(h):
                    dve.wait_ge(vwb_out, h)
                nc.vector.tensor_tensor(VWb[0:H, :], VWb[0:H, :], vwb_ps[layer], ALU.add).then_inc(vwb_out, 1)

            def vw_even(h, hp, w):
                dve.wait_ge(vw_mm, h + 1)
                rows_to = slice(S2 * (w % 2), S2 * (w % 2) + S2)
                nc.vector.tensor_copy(VW[rows_to, 0::2, bass.ds(hp, 1), :].rearrange("p b a d -> p b (a d)"),
                                      vw_ps[0:S2]).then_inc(vw_out_dve, 1)

            def tile0(b, p, first=False, last=False):
                i = 2 * b + p
                w1, w2 = 2 * p, 2 * p + 1
                h1, h2 = SLOTS * b + w1, SLOTS * b + w2
                hh1, hh2 = bass.ds(SLOTS * b + w1, 1), bass.ds(SLOTS * b + w2, 1)
                hp = 2 * b + p
                next_tile = not (last and p == 1)
                if next_tile:
                    masked0(i + 1, 1 - p, 0)
                    masked0(i + 1, 1 - p, 1)
                    masked0(i + 1, 1 - p, 2)
                ac_copy(h1, hh1, w1, 0)
                if next_tile:
                    masked0(i + 1, 1 - p, 3)
                ac_copy(h1, hh1, w1, 1)
                ac_copy(h1, hh1, w1, 2)
                if not (first and p == 0):
                    residual0(i - 1)
                vwb_add(h1, 0)
                if next_tile:
                    max0(i + 1, 1 - p)
                vw_even(h1, hp, w1)
                if next_tile:
                    sub0(i + 1, 1 - p)
                if not (first and p == 0):
                    normal0(i - 1)
                if not next_tile:
                    for n in range(2):
                        dve.wait_ge(x1_done, 2)
                        ln_moments(tile_of(n), ln_of1(n))
                        ln_normal(xn[n][:], tile_of(n), ln_of1(n))
                ac_copy(h2, hh2, w2, 0)
                out0(i, p)
                ac_copy(h2, hh2, w2, 1)
                ac_copy(h2, hh2, w2, 2)
                vwb_add(h2, 0)
                vw_even(h2, hp, w2)

            for q in range(QUARTERS):
                masked0(0, 0, q)
            max0(0, 0)
            sub0(0, 0)
            tile0(0, 0, first=True)
            tile0(0, 1, first=True)
            with dve.Fori(1, B - 1) as b:
                tile0(b, 0)
                tile0(b, 1)
            tile0(B - 1, 0, last=True)
            tile0(B - 1, 1, last=True)
            residual0(TILES - 1)

            def scores_out(n, b):
                dve.wait_ge(s_mm, n + 1)
                nc.vector.tensor_tensor(
                    sx[:, :, 0:S2], sx_ps.rearrange("p r (j t) -> p (r j) t", t=S2),
                    AC[:, DC, bass.ds(b, 1)].rearrange("p a h t -> p (a h) t"), ALU.add).then_inc(sx_done, 1)
                nc.vector.tensor_tensor(sx[:, :, S2:KEYS], sxb_ps.unsqueeze(2), ACb[:, DC, :].unsqueeze(2), ALU.add)\
                    .then_inc(sx_done, 1)
                dve.wait_ge(sx_done, 2 * n + 2)
                nc.vector.tensor_reduce(mx[:], sx[:], AX_X, ALU.max).then_inc(mx_done, 1)
                dve.wait_ge(mx_done, n + 1)
                nc.vector.tensor_tensor(sx[:], sx[:], mx[:].unsqueeze(2).to_broadcast([P, H, KEYS]), ALU.subtract)\
                    .then_inc(sub_done, 1)

            def sums(n):
                dve.wait_ge(exp_done, n + 1)
                nc.vector.tensor_reduce(sm[:], px[:], AX_X, ALU.add).then_inc(sm_done, 1)
                dve.wait_ge(sm_done, n + 1)
                nc.vector.reciprocal(rs[:], sm[:]).then_inc(rs_done, 1)

            def weights(n):
                dve.wait_ge(rs_done, n + 1)
                if some(n):
                    dve.wait_ge(pT_mm, 3 * n)
                nc.vector.tensor_tensor(pm[:], px[:, :, 0:S2], rs[:].unsqueeze(2).to_broadcast([P, H, S2]),
                                        ALU.mult).then_inc(pm_done, 1)
                nc.vector.tensor_tensor(pmb[:, 0:H].unsqueeze(2), px[:, :, S2:KEYS], rs[:].unsqueeze(2), ALU.mult)\
                    .then_inc(pm_done, 1)

            def x_add(n, i):
                dve.wait_ge(o_mm, n + 1)
                nc.vector.tensor_tensor(tile_of(i), tile_of(i), o_ps, ALU.add).then_inc(x_done, 1)

            def mlp_normal(i):
                if i >= HALF:
                    dve.wait_ge(hTm_mm, i - HALF + 1)
                else:
                    dve.wait_ge(hT_mm, LAYERS * TILES)
                ln_normal(xn[i % HALF][:], tile_of(i), LN_NM + i)

            def attention(layer):
                n0 = layer * TILES

                def pair(b, first=False, last=False):
                    for p in range(2):
                        i = 2 * b + p
                        n = n0 + i
                        mlp = last and layer + 1 == LAYERS
                        ahead = p if last else i + 2
                        scores_out(n, b)
                        if layer == 0 and first and p == 0:
                            normal0(TILES - 1)
                        if layer == 0 and first and p == 1:
                            dve.wait_ge(x1_done, TILES)
                        if mlp:
                            ln_moments(tile_of(2 * p), LN_NM + 2 * p)
                        else:
                            ln_moments(tile_of(ahead), ln_of1(n + 2))
                        sums(n)
                        if mlp:
                            mlp_normal(2 * p)
                        else:
                            dve.wait_ge(hT_mm, n + 1)
                            ln_normal(xn[p][:], tile_of(ahead), ln_of1(n + 2))
                        weights(n)
                        if mlp:
                            ln_moments(tile_of(2 * p + 1), LN_NM + 2 * p + 1)
                        if not (first and p == 0):
                            x_add(n - 1, i - 1)
                        if mlp:
                            mlp_normal(2 * p + 1)

                pair(0, first=True)
                with dve.Fori(1, B - 1) as b:
                    pair(b)
                pair(B - 1, last=True)
                x_add(n0 + TILES - 1, TILES - 1)

            attention(0)
            dve.wait_ge(x_done, TILES)
            nc.vector.memset(VWb[0:H, :], 0.0).then_inc(vwb_zero, 1)
            dve.wait_ge(vwb_zero, 1)
            with dve.Fori(SLOTS, LAYERS * SLOTS) as r:
                for w in range(SLOTS):
                    h = r * SLOTS + w
                    hh = bass.ds((r - SLOTS) * SLOTS + w, 1)
                    ac_copy(h, hh, w, 0)
                    ac_copy(h, hh, w, 1)
                    vwb_add(h, 1)
                    ac_copy(h, hh, w, 2)
                    vw_even(h, (r - SLOTS) * 2 + w // 2, w)
            attention(1)

            def x_plus_b2(i):
                if i < HALF:
                    dve.wait_ge(x_done, LAYERS * TILES)
                nc.vector.tensor_tensor(tile_of(i), tile_of(i), rows[:, 3 * D:4 * D], ALU.add).then_inc(xb2_done, 1)

            dve.wait_ge(x_done, LAYERS * TILES)
            for j in range(HALF):
                i = HALF + j
                ln_moments(tile_of(i), LN_NM + i)
                x_plus_b2(j)
                mlp_normal(i)
            for j in range(HALF):
                dve.wait_ge(ln_done, LN_NM + HALF + j + 1)
                x_plus_b2(HALF + j)
            for i in range(TILES):
                dve.wait_ge(xb2_done, i + 1)
                dve.wait_ge(y_mm, i + 1)
                nc.vector.tensor_tensor(tile_of(i), tile_of(i), y_ps[i % 2], ALU.add).then_inc(y_done, 1)

        @block.tensor
        def _(pe):
            def mm(out, lhsT, rhs, k=0, n=1, **kw):
                return nc.tensor.matmul(out, lhsT, rhs, start=(k == 0), stop=(k == n - 1), **kw)

            pe.wait_ge(ctx_in, 16)
            pe.wait_ge(w0_in, 16)
            pe.wait_ge(wkrep_done, DC)
            for m in range(DC):
                for c in range(DC):
                    last = mm(s_banks[:, m, 0:CK], wk_rep[:, c, m * P:(m + 1) * P], ctxT[:, c], c, DC)
                last.then_inc(kT0_mm, 1)

            def q0(b, i=None):
                if i is None:
                    pe.wait_ge(xt0_in, 16)
                else:
                    pe.wait_ge(xt_in, 16)
                    if some(i):
                        pe.wait_ge(y0_done, i)
                for m in range(DC):
                    for c in range(DC):
                        last = mm(q0_ps[m], w0[:, c, m * P:(m + 1) * P], xT[:, c, bass.ds(b * S, S)], c, DC,
                                  skip_group_check=True)
                    last.then_inc(q0_mm, 1)

            q0(0)
            wv = slice(D + KVH * HD, D + 2 * KVH * HD)
            for b in range(B):
                for half in range(2):
                    for c in range(DC):
                        last = mm(s_banks[S2 * half:S2 * half + S2, 2, b * KVH * HD:(b + 1) * KVH * HD],
                                  ctxT[:, c, b * S2:(b + 1) * S2], w0[:, c, wv], c, DC)
            last.then_inc(v0_mm, 1)

            def s0(i, p, q):
                if p == 0 and q == 0:
                    pe.wait_ge(q0_out, i + DC)
                    pe.wait_ge(kblk_done, i + DC)
                if isinstance(i, int) and i == 0 and q == 0:
                    pe.wait_ge(kT0_out, DC)
                else:
                    pe.wait_ge(sc0_done, QUARTERS * i + q)
                c, half = q // 2, q % 2
                mm(s0_ps, qT0[:, c, p * P:(p + 1) * P],
                   kblk[:, c, half * QH:(half + 1) * QH, :].rearrange("p h t -> p (h t)")).then_inc(s0_mm, 1)

            def turn0(i, p, g):
                if g == 0:
                    pe.wait_ge(exp0_done, i + 1)
                if some(4 * i + g):
                    pe.wait_ge(pT0_out, 4 * i + g)
                for j in range(4):
                    last = nc.tensor.transpose(pT0_ps[:, j * P:(j + 1) * P],
                                               sc0[p][:, (4 * g + j) * P:(4 * g + j + 1) * P], ident[:])
                last.then_inc(pT0_mm, 1)

            def values0(i, g, b):
                pe.wait_ge(pT0_out, 4 * i + g + 1)
                if g == 0:
                    if some(i):
                        pe.wait_ge(o0_done, i)
                    pe.wait_ge(v0_out, 2)
                for j in range(4):
                    hp = 4 * g + j
                    last = mm(o0_ps[:, hp * 2 * VO:(hp + 1) * 2 * VO], pT0[:, hp],
                              vblk[:, bass.ds(b, 1), hp * 2 // G, :].rearrange("p a e -> p (a e)"),
                              skip_group_check=True)
                if g == 3:
                    last.then_inc(pv0_mm, 1)

            def turn_o0(i, p, batches):
                pe.wait_ge(o0_done, i + 1)
                pe.wait_ge(q0_out, DC * batches)
                if some(i):
                    pe.wait_ge(y0_done, i)
                for c in range(DC):
                    last = nc.tensor.transpose(oT0_ps[:, c * P:(c + 1) * P], o0[p][:, c * P:(c + 1) * P], ident[:])
                last.then_inc(oT0_mm, 1)

            def wo0(i):
                pe.wait_ge(oT0_out, i + 1)
                for c in range(DC):
                    last = mm(wo0_ps, oT0[:, c], w0[:, c, D + 2 * KVH * HD:], c, DC, skip_group_check=True)
                last.then_inc(wo0_mm, 1)

            def col(w, at, n=P):
                return ring[w][:, at:at + n]

            def keys(h, w, layer):
                pe.wait_ge(w_in[w], (h - w) * 4 + 16)
                if some(h):
                    if layer == 0:
                        pe.wait_ge(vwb_out, h)
                    else:
                        pe.wait_ge(kT_out, h)
                for c in range(DC):
                    last = mm(kT_ps, col(w, W_K + c * K), ctxT[:, c], c, DC)
                last.then_inc(kT_mm, 1)

            def vals(h, w, layer):
                pe.wait_ge(kT_out, h + 1) if layer == 0 else pe.wait_ge(vT_out, h)
                for c in range(DC):
                    last = mm(vT_ps[layer], col(w, W_V + c * K), ctxT[:, c], c, DC, skip_group_check=True)
                last.then_inc(vT_mm, 1)

            def ac(h, w, j):
                if j == 0:
                    pe.wait_ge(kT_out, h + 1)
                    pe.wait_ge(headcols, 2 * h + 2)
                if some(3 * h + j - 1):
                    pe.wait_ge(ac_out, 2 * (3 * h + j) - 2)
                lhsT = col(w, W_QT + j * P) if j < DC else bq_all[:]
                mm(ac_ps[(w + j) % 2], lhsT, kTs[:]).then_inc(ac_mm, 1)

            def vwb(h, w, layer):
                pe.wait_ge(vT_out, h + 1) if layer == 0 else pe.wait_ge(vwb_out, h)
                mm(vwb_ps[layer], col(w, W_BV, H), col(w, W_O, D)).then_inc(vwb_mm, 1)

            def vw(h, w):
                pe.wait_ge(vT_out, h + 1)
                if some(h):
                    pe.wait_ge(vw_out_dve, h)
                    pe.wait_ge(vw_out_act, h)
                for pair_of in range(2):
                    last = mm(vw_ps[:, pair_of], vTs[:, pair_of * P:(pair_of + 1) * P], col(w, W_O, D),
                              skip_group_check=True)
                last.then_inc(vw_mm, 1)

            def hT_turn(ps, n, p):
                pe.wait_ge(ln_done, ln_of1(n) + 1)
                for c in range(DC):
                    last = nc.tensor.transpose(ps[:, c * P:(c + 1) * P], xn[p][:, c * P:(c + 1) * P], ident[:])
                last.then_inc(hT_mm, 1)

            def tile0(b, p, first=False, last=False):
                i = 2 * b + p
                w1, w2 = 2 * p, 2 * p + 1
                h1, h2 = SLOTS * b + w1, SLOTS * b + w2
                next_tile = not (last and p == 1)
                if next_tile:
                    s0(i + 1, 1 - p, 0)
                keys(h1, w1, 0)
                if next_tile:
                    s0(i + 1, 1 - p, 1)
                vals(h1, w1, 0)
                if next_tile:
                    s0(i + 1, 1 - p, 2)
                ac(h1, w1, 0)
                if next_tile:
                    s0(i + 1, 1 - p, 3)
                ac(h1, w1, 1)
                if not (first and p == 0):
                    turn_o0(i - 1, 1 - p, b + 1 if p == 0 or last else b + 2)
                ac(h1, w1, 2)
                if not (first and p == 0):
                    wo0(i - 1)
                vwb(h1, w1, 0)
                turn0(i, p, 0)
                vw(h1, w1)
                turn0(i, p, 1)
                values0(i, 0, b)
                keys(h2, w2, 0)
                turn0(i, p, 2)
                values0(i, 1, b)
                vals(h2, w2, 0)
                turn0(i, p, 3)
                values0(i, 2, b)
                ac(h2, w2, 0)
                values0(i, 3, b)
                ac(h2, w2, 1)
                if p == 0 and not last:
                    q0(b + 1, i)
                if not next_tile:
                    pe.wait_ge(y0_done, i)
                    for n in range(2):
                        hT_turn(first_hT_ps[n], n, n)
                ac(h2, w2, 2)
                if not next_tile:
                    pe.wait_ge(hT_out, 2 * DC)
                    turn_o0(i, p, B)
                vwb(h2, w2, 0)
                vw(h2, w2)

            pe.wait_ge(const_in, 64)
            for q in range(QUARTERS):
                s0(0, 0, q)
            tile0(0, 0, first=True)
            tile0(0, 1, first=True)
            with pe.Fori(1, B - 1) as b:
                tile0(b, 0)
                tile0(b, 1)
            tile0(B - 1, 0, last=True)
            tile0(B - 1, 1, last=True)
            wo0(TILES - 1)

            def hT_turn_ahead(n, p):
                pe.wait_ge(hT_out, DC * n)
                hT_turn(hT_ps, n, p)

            def scores(n, p, b):
                pe.wait_ge(hT_out, DC * n + DC)
                if some(n):
                    pe.wait_ge(sx_done, 2 * n)
                for half in range(2):
                    for c in range(DC):
                        mm(sx_ps[:, half], hT[p][:, c],
                           AC[:, c, bass.ds(b, 1), half * HP:(half + 1) * HP, :].rearrange("p a h t -> p (a h t)"),
                           c, DC)
                for c in range(DC):
                    last = mm(sxb_ps, hT[p][:, c], ACb[:, c, :], c, DC)
                last.then_inc(s_mm, 1)

            def weights_turn(n):
                pe.wait_ge(pm_done, 2 * n + 2)
                if some(n):
                    pe.wait_ge(pT_out, 3 * n)
                for g in range(2):
                    for j in range(4):
                        hp = 4 * g + j
                        last = nc.tensor.transpose(pT_ps[g][:, j * P:(j + 1) * P],
                                                   pm[:, 2 * hp:2 * hp + 2, :].rearrange("p h t -> p (h t)"), ident[:])
                    last.then_inc(pT_mm, 1)
                nc.tensor.transpose(pTb_ps, pmb[:], ident[:]).then_inc(pT_mm, 1)

            def values(n, b):
                if some(n):
                    pe.wait_ge(x_done, n)
                for hp in range(HP):
                    if hp % 4 == 0:
                        pe.wait_ge(pT_out, 3 * n + hp // 4 + 1)
                    mm(o_ps, pT[:, hp], VW[:, bass.ds(b, 1), hp, :].rearrange("p a d -> p (a d)"), hp, HP + 1)
                pe.wait_ge(pT_out, 3 * n + 3)
                mm(o_ps, pTb[:], VWb[:], HP, HP + 1).then_inc(o_mm, 1)

            def hTm_turn(i):
                pe.wait_ge(ln_done, LN_NM + i + 1)
                if i < 2:
                    pe.wait_ge(hT_out, LAYERS * TILES * DC)
                    pe.wait_ge(sx_done, 2 * LAYERS * TILES)
                else:
                    pe.wait_ge(hTm_out, DC * (i - 1))
                for c in range(DC):
                    last = nc.tensor.transpose(hTm_ps[i % 2][:, c * P:(c + 1) * P], xn[i % HALF][:, c * P:(c + 1) * P],
                                               ident[:])
                last.then_inc(hTm_mm, 1)

            def attention(layer):
                n0 = layer * TILES
                heads = layer * H + H

                def pair(b, last=False):
                    n = n0 + 2 * b
                    mlp = last and layer + 1 == LAYERS
                    for p in range(2):
                        if p == 0:
                            scores(n + 1, 1, b)
                        elif not last:
                            scores(n + 2, 0, b + 1)
                        weights_turn(n + p)
                        if not mlp:
                            hT_turn_ahead(n + p + 2, p)
                        elif p == 0:
                            hTm_turn(0)
                        else:
                            hTm_turn(2)
                            hTm_turn(3)
                        values(n + p, b)
                        if mlp and p == 0:
                            hTm_turn(1)

                pe.wait_ge(ac_out, 6 * heads)
                pe.wait_ge(vwb_out, heads)
                pe.wait_ge(vT_out, heads)
                scores(n0, 0, 0)
                pe.wait_ge(vw_out_dve, heads)
                pe.wait_ge(vw_out_act, heads)
                pe.wait_ge(y0_done, TILES)
                pe.wait_ge(bo_in, 16 * layer + 16)
                pair(0)
                with pe.Fori(1, B - 1) as b:
                    pair(b)
                pair(B - 1, last=True)

            attention(0)
            with pe.Fori(SLOTS, LAYERS * SLOTS) as r:
                for w in range(SLOTS):
                    h = r * SLOTS + w
                    keys(h, w, 1)
                    vals(h, w, 1)
                    pe.wait_ge(x_done, TILES)
                    pe.wait_ge(hT_out, DC * (TILES + 2))
                    ac(h, w, 0)
                    ac(h, w, 1)
                    vwb(h, w, 1)
                    ac(h, w, 2)
                    vw(h, w)
            attention(1)

            pe.wait_ge(mlp_in, 48)
            for half in range(TILES // HALF):
                pe.wait_ge(hTm_out, (half + 1) * HALF * DC)
                for f in range(FC):
                    if half == 0 and f >= HALF:
                        hTm_turn(f)
                    if half or f >= 2:
                        pe.wait_ge(g_out, half * FC + f - 1)
                    for c in range(DC):
                        last = mm(g_ps[f % 2][:, :], fc1[:, c, f * P:(f + 1) * P],
                                  hTm[:, c, half * HALF * P:(half + 1) * HALF * P], c, DC)
                    last.then_inc(g_mm, 1)
                for j in range(HALF):
                    i = half * HALF + j
                    if i >= 2:
                        pe.wait_ge(y_done, i - 1)
                    elif i == 0:
                        pe.wait_ge(x_done, LAYERS * TILES)
                    for f in range(FC):
                        if j == 0:
                            pe.wait_ge(g_out, half * FC + f + 1)
                        last = mm(y_ps[i % 2], gT[:, f, j * P:(j + 1) * P], fc2[:, f], f, FC)
                    last.then_inc(y_mm, 1)


def kernel(**inputs):
    import numpy as np
    import concourse.bacc as _bacc
    from concourse.bass_utils import run_bass_kernel_spmd as _run

    a = {n: np.asarray(v) for n, v in inputs.items()}

    def columns(v):
        return v.reshape(-1, P).T

    def rows_by_chunk(w):
        return w.reshape(DC, P, -1).transpose(1, 0, 2)

    x, c = a["x"], a["ctx_2048"]
    p0, p1 = "L0_xattn_", "L1_xattn_"
    bk_rep = np.broadcast_to(a[p0 + "bk"].reshape(KVH, 1, HD), (KVH, G, HD)).reshape(-1)
    heads = np.zeros((LAYERS, H, P, W_N), np.float32)
    for i in range(LAYERS):
        def get(name):
            return a[f"{p1}{name}{i + 1}"]
        for at, name in ((W_K, "wk"), (W_V, "wv")):
            heads[i, :, :, at:at + D] = get(name).reshape(DC, P, H, K).transpose(2, 1, 0, 3).reshape(H, P, D)
        heads[i, :, :, W_QT:W_QT + D] = get("wq").reshape(D, H, K).transpose(1, 2, 0)
        heads[i, :, :, W_O:W_O + D] = get("wo").reshape(H, K, D)
        for h in range(H):
            heads[i, h, :, W_BV + h] = get("bias_v").reshape(H, K)[h]
        for j, name in enumerate(("bk", "bq", "bias_k", "bv")):
            heads[i, :, :, W_COL + j] = get(name).reshape(H, K)
    blockmask = np.zeros((P, NHC), np.float32)
    for row in range(P):
        blockmask[row, row // HD] = 1.0
    arrays = {
        "x_tok": x.reshape(TILES, P, D).transpose(1, 0, 2),
        "xT": rows_by_chunk(x.reshape(-1, D).T),
        "ctxT": rows_by_chunk(c.reshape(-1, D).T),
        "mask": a["mask_Bx1xSxS2_ff0"].reshape(TILES, P, S2).transpose(1, 0, 2),
        "w0": np.concatenate([rows_by_chunk(a[p0 + n]) for n in ("Wq", "Wk", "Wv", "Wo")], axis=2),
        "cols0": np.concatenate([columns(a[p0 + "bq"]), columns(bk_rep)], axis=1),
        "rows": np.concatenate([a[p0 + "bo"], a[p0 + "gamma"], a[p0 + "beta"], a[p1 + "b_fc2"], a[p0 + "bv"]])[None],
        "heads": heads.reshape(LAYERS * H, P, W_N),
        "bo": np.stack([a[f"{p1}bo{i + 1}"] for i in range(LAYERS)]),
        "ln": np.concatenate([columns(a[p1 + n]) for n in ("ln1_scale", "ln1_offset", "ln2_scale", "ln2_offset",
                                                           "ln_mlp_scale", "ln_mlp_offset")], axis=1),
        "fc1": rows_by_chunk(a[p1 + "w_fc1"]),
        "bfc1": columns(a[p1 + "b_fc1"]),
        "fc2": a[p1 + "w_fc2"].reshape(FC, P, D).transpose(1, 0, 2),
        "blockmask": blockmask,
        "ident": np.eye(P, dtype=np.float32),
    }
    nc = _bacc.Bacc("TRN2", target_bir_lowering=False, num_devices=1)
    feed, args = {}, []
    for name, value in arrays.items():
        value = np.ascontiguousarray(value)
        feed[f"in_{name}_dram"] = value
        args.append(nc.dram_tensor(f"in_{name}_dram", value.shape, mybir.dt.from_np(value.dtype),
                                   kind="ExternalInput").ap())
    args.append(nc.dram_tensor("out_dram", (P, TILES, D), F32, kind="ExternalOutput").ap())
    build(nc, *args)
    got = _run(nc, [feed], core_ids=[0]).results[0]["out_dram"]
    return got.transpose(1, 0, 2).reshape(B, S, D)
```

```python
from contextlib import ExitStack

import concourse.bass as bass
from concourse import mybir

F32 = mybir.dt.float32
ALU = mybir.AluOpType
ACT = mybir.ActivationFunctionType
AX_X = mybir.AxisListType.X

P = 128
B, S, S2, D = 4, 256, 64, 256
DC = D // P
TILES = B * S // P
NH, KVH, HD = 32, 8, 8
G = NH // KVH
QUARTERS, QH = 4, NH // 4
NHC = P // HD
VO = HD + 1
LAYERS, H, K = 2, 16, 128
HP = H // 2
KEYS = S2 + 1
CK = B * S2
SLOTS = 4
F = 1024
FC = F // P
HALF = 4
W_K, W_QT, W_V, W_O, W_BV = 0, D, 2 * D, 3 * D, 4 * D
W_COL = W_BV + H
W_N = W_COL + 4
EPS0, EPS1 = 1e-6, 1e-5
SCALE0, SCALE1 = HD ** -0.5, K ** -0.5
N_FILLS = 9


def some(n):
    return not (isinstance(n, int) and n <= 0)


def ln_of0(i):
    return TILES + 1 if isinstance(i, int) and i == TILES - 1 else i


def ln_of1(n):
    return TILES - 1 + n if isinstance(n, int) and n < 2 else TILES + n


def build(nc, x_tok, xT_d, ctxT_d, mask_d, w0_d, cols0_d, rows_d, heads_d, bo_d, ln_d, fc1_d, bfc1_d, fc2_d,
          blockmask_d, ident_d, out_d):
    with ExitStack() as ctx:
        def sb(name, shape):
            return ctx.enter_context(nc.sbuf_tensor(name, shape, F32))

        def pb(name, shape):
            return ctx.enter_context(nc.psum_tensor(name, shape, F32))

        def sem(name):
            return ctx.enter_context(nc.semaphore(name))

        ident = sb("ident", [P, P])
        ones = sb("ones", [P, P])
        expo = sb("expo", [P, 1])
        eps0, eps1 = sb("eps0", [P, 1]), sb("eps1", [P, 1])
        X = sb("X", [P, TILES, D])
        ctxT = sb("ctxT", [P, DC, CK])
        stats = sb("stats", [P, 6])
        carrier = sb("carrier", [P, 1])
        pool_carrier = sb("pool_carrier", [P, 1])
        mv = sb("mv", [P, 2])
        ve = sb("ve", [P, 1])
        rstd = sb("rstd", [P, 1])
        stats4, mv4 = sb("stats4", [P, HALF, 6]), sb("mv4", [P, HALF, 2])
        ve4, rstd4 = sb("ve4", [P, HALF]), sb("rstd4", [P, HALF])
        xT = sb("xT", [P, DC, B * S])
        mask = sb("mask", [P, TILES, S2])
        w0 = sb("w0", [P, DC, D + KVH * HD * 2 + D])
        wk_rep = sb("wk_rep", [P, DC, D])
        cols0 = sb("cols0", [P, 4])
        bq_s = sb("bq_s", [P, DC])
        rows = sb("rows", [P, 4 * D + KVH * HD])
        kT0 = sb("kT0", [P, DC, CK])
        blockmask = sb("blockmask", [P, NHC])
        kblk = sb("kblk", [P, DC, NHC, S2])
        vblk = sb("vblk", [P, B, KVH, 2 * VO])
        qT0 = sb("qT0", [P, DC, S])
        scores_sb = sb("scores_sb", [P, 2, NH * S2])
        sc0 = [scores_sb[:, i, :] for i in range(2)]
        mx0 = sb("mx0", [P, NH])
        pT0 = sb("pT0", [P, NH // 2, P])
        rden0 = sb("rden0", [P, NH])
        o0 = [sb(f"o0_{i}", [P, D]) for i in range(2)]
        oT0 = sb("oT0", [P, DC, P])
        y0 = sb("y0", [P, D])
        z0 = sb("z0", [P, D])
        z1 = sb("z1", [P, D])
        ring = [sb(f"ring{w}", [P, W_N]) for w in range(SLOTS)]
        kTs = sb("kTs", [P, CK + 1])
        vTs = sb("vTs", [P, CK])
        bq_all = sb("bq_all", [P, P])
        AC = sb("AC", [P, DC + 1, B, H, S2])
        ACb = sb("ACb", [P, DC + 1, H])
        VW = sb("VW", [P, B, HP, D])
        VWb = sb("VWb", [H + 1, D])
        ln_all = sb("ln_all", [P, (LAYERS + 1) * 4])
        xn = [sb(f"xn{i}", [P, D]) for i in range(HALF)]
        hT = [sb(f"hT{i}", [P, DC, P]) for i in range(2)]
        sx = sb("sx", [P, H, KEYS])
        px = sb("px", [P, H, KEYS])
        pm = sb("pm", [P, H, S2])
        pmb = sb("pmb", [P, H + 1])
        mx = sb("mx", [P, H])
        sm = sb("sm", [P, H])
        rs = sb("rs", [P, H])
        pT = pT0[:, 0:HP, :]
        pTb = sb("pTb", [H + 1, P])
        fc1 = sb("fc1", [P, DC, F])
        bfc1 = sb("bfc1", [P, FC])
        fc2 = kblk[:, :, :, :].rearrange("p c h t -> p (c h t)").rearrange("p (f d) -> p f d", f=FC)
        hTm = xT
        gT = scores_sb[:, :, :].rearrange("p i (f t) -> p (i f) t", t=HALF * P)

        s_banks = pb("s_banks", [P, 4, 512])
        bank4 = pb("bank4", [P, 512])
        bank5 = pb("bank5", [P, 512])
        bank6 = pb("bank6", [P, 512])
        bank7 = pb("bank7", [P, 512])
        s0_ps = s_banks[:, 0, :]
        pT0_ps = s_banks[:, 1, :]
        o0_ps = s_banks[:, 2, 0:NH * VO]
        oT0_ps = s_banks[:, 3, 0:D]
        wo0_ps = s_banks[:, 3, 256:256 + D]
        q0_ps = [s_banks[:, 3, c * S:(c + 1) * S] for c in range(DC)]
        first_hT_ps = [s_banks[:, 3, i * D:(i + 1) * D] for i in range(2)]
        kT_ps = [bank4[:, 0:CK], s_banks[:, 0, 0:CK]]
        vT_ps = [bank4[:, 256:256 + CK], s_banks[:, 3, 0:CK]]
        vwb_ps = [bank4[0:H, 0:D], bank6[0:H, 0:D]]
        vw_ps = bank5[:, :].rearrange("p (b d) -> p b d", b=2)
        ac_ps = [[bank6[:, 0:CK + 1], bank7[:, 0:CK + 1]], [s_banks[:, 1, 0:CK + 1], s_banks[:, 2, 0:CK + 1]]]
        sx_ps = s_banks[:, 0:2, :]
        sxb_ps = s_banks[:, 2, 0:H]
        pTb_ps = s_banks[0:H + 1, 3, 0:P]
        pT_ps = [bank4, bank5]
        o_ps = bank6[:, 0:D]
        hT_ps = bank7[:, 0:D]
        hTm_ps = [bank7[:, 0:D], s_banks[:, 2, 0:D]]
        g_ps = [s_banks[:, 0, :], s_banks[:, 1, :]]
        y_ps = [bank4[:, 0:D], bank5[:, 0:D]]

        ident_in, bv_in, ln_in = (sem(n) for n in ("ident_in", "bv_in", "ln_in"))
        ctx_in, w0_in, x_in, xt0_in, xt_in, mask_in, const_in, rows_in, mlp_in = (
            sem(n) for n in ("ctx_in", "w0_in", "x_in", "xt0_in", "xt_in", "mask_in", "const_in", "rows_in", "mlp_in"))
        out_done = sem("out_done")
        fills = sem("fills")
        wkrep_done = sem("wkrep_done")
        ln_stats, ln_mv, ln_eps, ln_rstd, ln_done = (
            sem(n) for n in ("ln_stats", "ln_mv", "ln_eps", "ln_rstd", "ln_done"))
        bqs_done, kT0_mm, kT0_out, v0_mm, v0_out, q0_mm, q0_out, kblk_done = (
            sem(n) for n in ("bqs_done", "kT0_mm", "kT0_out", "v0_mm", "v0_out", "q0_mm", "q0_out", "kblk_done"))
        s0_mm, sc0_done, mx0_done, sub0_done, exp0_done = (
            sem(n) for n in ("s0_mm", "sc0_done", "mx0_done", "sub0_done", "exp0_done"))
        pT0_mm, pT0_out, pv0_mm, rden0_done, o0_done, oT0_mm, oT0_out, wo0_mm, y0_done = (
            sem(n) for n in ("pT0_mm", "pT0_out", "pv0_mm", "rden0_done", "o0_done", "oT0_mm", "oT0_out",
                             "wo0_mm", "y0_done"))
        xbo_done, z1_done, x1_done = (sem(n) for n in ("xbo_done", "z1_done", "x1_done"))
        w_in = [sem(f"w_in{w}") for w in range(SLOTS)]
        bo_in = sem("bo_in")
        kT_mm, kT_out, vT_mm, vT_out, headcols, ac_mm, ac_out = (
            sem(n) for n in ("kT_mm", "kT_out", "vT_mm", "vT_out", "headcols", "ac_mm", "ac_out"))
        vw_mm, vw_out_dve, vw_out_act, vwb_mm, vwb_out = (
            sem(n) for n in ("vw_mm", "vw_out_dve", "vw_out_act", "vwb_mm", "vwb_out"))
        vwb_zero = sem("vwb_zero")
        hT_mm, hT_out, s_mm, sx_done, mx_done, sub_done, exp_done, sm_done, rs_done, pm_done = (
            sem(n) for n in ("hT_mm", "hT_out", "s_mm", "sx_done", "mx_done", "sub_done", "exp_done", "sm_done",
                             "rs_done", "pm_done"))
        pT_mm, pT_out, o_mm, x_done = (sem(n) for n in ("pT_mm", "pT_out", "o_mm", "x_done"))
        hTm_mm, hTm_out, g_mm, g_out, y_mm, y_done = (
            sem(n) for n in ("hTm_mm", "hTm_out", "g_mm", "g_out", "y_mm", "y_done"))
        xb2_done = sem("xb2_done")
        m_stats, m_mv, m_eps, m_rstd, m_done = (sem(n) for n in ("m_stats", "m_mv", "m_eps", "m_rstd", "m_done"))

        block = ctx.enter_context(nc.Block())
        ROUNDS = LAYERS * H // SLOTS
        HEADS0 = H

        @block.sync
        def _(sp):
            sp.dma_start(ctxT[:], ctxT_d).then_inc(ctx_in, 16)
            sp.dma_start(w0[:], w0_d).then_inc(w0_in, 16)
            sp.dma_start(ring[0][:], heads_d[0]).then_inc(w_in[0], 16)
            sp.dma_start(mask[:], mask_d).then_inc(mask_in, 16)
            sp.dma_start(ident[:], ident_d).then_inc(ident_in, 16)
            sp.dma_start(rows[:, 4 * D:], rows_d[0:1, 4 * D:].to_broadcast([P, KVH * HD])).then_inc(bv_in, 16)
            sp.dma_start(ring[1][:], heads_d[1]).then_inc(w_in[1], 16)
            sp.dma_start(X[:], x_tok).then_inc(x_in, 16)
            for j in range(4):
                sp.dma_start(rows[:, j * D:(j + 1) * D], rows_d[0:1, j * D:(j + 1) * D].to_broadcast([P, D]))\
                    .then_inc(rows_in, 16)
            for w in range(2, SLOTS):
                sp.dma_start(ring[w][:], heads_d[w]).then_inc(w_in[w], 16)
            sp.dma_start(ln_all[:], ln_d).then_inc(ln_in, 16)
            sp.dma_start(xT[:, :, S:], xT_d[:, :, S:]).then_inc(xt_in, 16)
            sp.dma_start(VWb[H:H + 1, :], bo_d[0:1, :]).then_inc(bo_in, 16)
            with sp.Fori(1, ROUNDS) as r:
                for w in range(SLOTS):
                    sp.wait_ge(vw_mm, SLOTS * (r - 1) + w + 1)
                    sp.dma_start(ring[w][:], heads_d[SLOTS * r + w]).then_inc(w_in[w], 16)
            sp.wait_ge(x_done, TILES)
            sp.dma_start(VWb[H:H + 1, :], bo_d[1:2, :]).then_inc(bo_in, 16)
            sp.dma_start(fc1[:], fc1_d).then_inc(mlp_in, 16)
            sp.dma_start(bfc1[:], bfc1_d).then_inc(mlp_in, 16)
            sp.dma_start(fc2[:], fc2_d).then_inc(mlp_in, 16)
            for i in range(TILES):
                sp.wait_ge(y_done, i + 1)
                sp.dma_start(out_d[:, i, :], X[:, i, :]).then_inc(out_done, 16)
            sp.wait_ge(out_done, 16 * TILES)

        @block.gpsimd
        def _(pool):
            pool.memset(ones[:], 1.0).then_inc(fills, 1)
            pool.memset(expo[:], -0.5).then_inc(fills, 1)
            pool.memset(eps0[:], EPS0).then_inc(fills, 1)
            pool.memset(eps1[:], EPS1).then_inc(fills, 1)
            pool.memset(vblk[:], 0.0).then_inc(fills, 1)
            pool.memset(pmb[:], 1.0).then_inc(fills, 1)
            pool.memset(VWb[0:H, :], 0.0).then_inc(fills, 1)
            pool.wait_ge(fills, 7)
            pool.memset(vblk[0:S2, :, :, HD:HD + 1], 1.0).then_inc(fills, 1)
            pool.wait_ge(fills, 8)
            pool.memset(vblk[S2:P, :, :, VO + HD:VO + HD + 1], 1.0).then_inc(fills, 1)
            pool.wait_ge(fills, N_FILLS)

            def key_blocks(b):
                pool.wait_ge(s0_mm, 2 * QUARTERS * b)
                for c in range(DC):
                    pool.tensor_tensor(
                        kblk[:, c], kT0[:, c, bass.ds(b * S2, S2)].unsqueeze(1).to_broadcast([P, NHC, S2]),
                        blockmask[:, :].unsqueeze(2).to_broadcast([P, NHC, S2]), ALU.mult).then_inc(kblk_done, 1)

            def rstd_of(n, eps):
                pool.wait_ge(ln_mv, n + 1)
                pool.tensor_tensor(ve[:], mv[:, 1:2], eps, ALU.add).then_inc(ln_eps, 1)
                pool.wait_ge(ln_eps, n + 1)
                pool.tensor_tensor(rstd[:], ve[:], expo[:], ALU.pow).then_inc(ln_rstd, 1)

            def x_plus_bo(i):
                at = X[:, bass.ds(i, 1), :].rearrange("p a d -> p (a d)")
                pool.tensor_tensor(at, at, rows[:, 0:D], ALU.add).then_inc(xbo_done, 1)

            def gamma_beta(i):
                pool.wait_ge(ln_done, ln_of0(i) + 1)
                pool.tensor_tensor(z1[:], z0[:], rows[:, D:2 * D], ALU.mult).then_inc(z1_done, 1)
                pool.wait_ge(z1_done, i + 1)
                pool.tensor_tensor(pool_carrier[:], ones[:, 0:1], ones[:, 0:1], ALU.mult)
                pool.tensor_tensor(X[:, bass.ds(i, 1), :].rearrange("p a d -> p (a d)"), z1[:], rows[:, 2 * D:3 * D],
                                   ALU.add).then_inc(x1_done, 1)

            def head_columns(h, w):
                pool.wait_ge(w_in[w], (h - w) * 4 + 16)
                if some(h):
                    pool.wait_ge(ac_mm, 3 * h)
                pool.tensor_tensor(kTs[:, CK:CK + 1], ones[:, 0:1], ring[w][:, W_COL + 2:W_COL + 3], ALU.mult)\
                    .then_inc(headcols, 1)
                pool.tensor_tensor(bq_all[:], ones[:], ring[w][:, W_COL + 1:W_COL + 2].to_broadcast([P, P]), ALU.mult)\
                    .then_inc(headcols, 1)

            def pair0(b, first=False, last=False):
                for p in range(2):
                    i = 2 * b + p
                    for w in (2 * p, 2 * p + 1):
                        head_columns(SLOTS * b + w, w)
                    if not (first and p == 0):
                        rstd_of(i - 1, eps0[:])
                    if p == 0 and not last:
                        key_blocks(b + 1)
                    if first and p == 0:
                        pool.wait_ge(x_in, 16)
                        pool.wait_ge(rows_in, 16 * 4)
                    x_plus_bo(i)
                    if not (first and p == 0):
                        gamma_beta(i - 1)

            pool.wait_ge(const_in, 32)
            pool.wait_ge(kT0_out, DC)
            pair0(0, first=True)
            with pool.Fori(1, B - 1) as b:
                pair0(b)
            pair0(B - 1, last=True)
            for n in range(2):
                rstd_of(ln_of1(n), eps1[:])
            rstd_of(ln_of0(TILES - 1), eps0[:])
            gamma_beta(TILES - 1)
            with pool.Fori(2, TILES + 1) as n:
                rstd_of(ln_of1(n), eps1[:])
            head_columns(H, 0)
            rstd_of(ln_of1(TILES + 1), eps1[:])
            with pool.Fori(SLOTS, LAYERS * SLOTS - 1) as r:
                for w in range(SLOTS):
                    head_columns(r * SLOTS + w + 1, (w + 1) % SLOTS)
            for w in range(1, SLOTS):
                head_columns(LAYERS * H - SLOTS + w, w)
            with pool.Fori(TILES + 2, LAYERS * TILES) as n:
                rstd_of(ln_of1(n), eps1[:])
            for half in range(TILES // HALF):
                pool.wait_ge(m_mv, HALF * (half + 1))
                pool.tensor_tensor(ve4[:], mv4[:, :, 1:2].rearrange("p j a -> p (j a)"),
                                   eps1[:].to_broadcast([P, HALF]), ALU.add).then_inc(m_eps, 1)
                pool.wait_ge(m_eps, half + 1)
                pool.tensor_tensor(rstd4[:], ve4[:], expo[:].to_broadcast([P, HALF]), ALU.pow).then_inc(m_rstd, 1)

        @block.scalar
        def _(act):
            act.dma_start(cols0[:], cols0_d).then_inc(const_in, 16)
            act.dma_start(blockmask[:], blockmask_d).then_inc(const_in, 16)
            act.dma_start(xT[:, :, 0:S], xT_d[:, :, 0:S]).then_inc(xt0_in, 16)
            act.wait_ge(const_in, 32)
            nc.scalar.mul(bq_s[:], cols0[:, 0:DC], SCALE0).then_inc(bqs_done, 1)
            for c in range(DC):
                act.wait_ge(kT0_mm, c + 1)
                nc.scalar.activation(kT0[:, c], s_banks[:, c, 0:CK], ACT.Identity,
                                     bias=cols0[:, DC + c:DC + c + 1]).then_inc(kT0_out, 1)

            def q_out(b):
                if some(b):
                    act.wait_ge(s0_mm, 2 * QUARTERS * b)
                act.wait_ge(q0_mm, DC * b + DC)
                for c in range(DC):
                    nc.scalar.activation(qT0[:, c], q0_ps[c], ACT.Identity, bias=bq_s[:, c:c + 1],
                                         scale=SCALE0).then_inc(q0_out, 1)

            def exp0(i, p):
                act.wait_ge(sub0_done, i + 1)
                nc.scalar.activation(sc0[p], sc0[p], ACT.Exp).then_inc(exp0_done, 1)

            def pT0_copy(i, g):
                act.wait_ge(pT0_mm, 4 * i + g + 1)
                if g == 0 and some(i):
                    act.wait_ge(pv0_mm, i)
                nc.scalar.copy(pT0[:, 4 * g:4 * g + 4], pT0_ps.rearrange("p (j t) -> p j t", j=4))\
                    .then_inc(pT0_out, 1)

            def oT0_copy(i):
                act.wait_ge(oT0_mm, i + 1)
                nc.scalar.copy(oT0[:], oT0_ps.rearrange("p (c t) -> p c t", c=DC)).then_inc(oT0_out, 1)

            def kT_copy(h, w, layer=0):
                act.wait_ge(kT_mm, h + 1)
                nc.scalar.activation(kTs[:, 0:CK], kT_ps[layer], ACT.Identity,
                                     bias=ring[w][:, W_COL:W_COL + 1])\
                    .then_inc(kT_out, 1)

            def vT_copy(h, w, layer):
                act.wait_ge(vT_mm, h + 1)
                nc.scalar.activation(vTs[:], vT_ps[layer], ACT.Identity, bias=ring[w][:, W_COL + 3:W_COL + 4])\
                    .then_inc(vT_out, 1)

            def vw_odd(h, hp, w):
                act.wait_ge(vw_mm, h + 1)
                rows_to = slice(S2 * (w % 2), S2 * (w % 2) + S2)
                nc.scalar.copy(VW[rows_to, 1::2, hp, :], vw_ps[S2:P]).then_inc(vw_out_act, 1)

            def hT_out_of(ps, n, p, layer):
                at = 4 * layer
                for c in range(DC):
                    nc.scalar.activation(hT[p][:, c], ps[:, c * P:(c + 1) * P], ACT.Identity,
                                         bias=ln_all[:, at + DC + c:at + DC + c + 1],
                                         scale=ln_all[:, at + c:at + c + 1]).then_inc(hT_out, 1)

            def tile0(b, p, first=False, last=False):
                i = 2 * b + p
                w1, w2 = 2 * p, 2 * p + 1
                h1, h2 = SLOTS * b + w1, SLOTS * b + w2
                hp = 2 * b + p
                kT_copy(h1, w1)
                if not (first and p == 0):
                    oT0_copy(i - 1)
                vT_copy(h1, w1, 0)
                pT0_copy(i, 0)
                vw_odd(h1, hp, w1)
                pT0_copy(i, 1)
                kT_copy(h2, w2)
                pT0_copy(i, 2)
                vT_copy(h2, w2, 0)
                pT0_copy(i, 3)
                if p == 0 and not last:
                    q_out(b + 1)
                if p == 1 and last:
                    act.wait_ge(ln_in, 16)
                    act.wait_ge(hT_mm, 2)
                    for n in range(2):
                        hT_out_of(first_hT_ps[n], n, n, 0)
                else:
                    exp0(i + 1, 1 - p)
                    vw_odd(h2, hp, w2)

            act.wait_ge(bqs_done, 1)
            q_out(0)
            exp0(0, 0)
            tile0(0, 0, first=True)
            tile0(0, 1, first=True)
            with act.Fori(1, B - 1) as b:
                tile0(b, 0)
                tile0(b, 1)
            tile0(B - 1, 0, last=True)
            tile0(B - 1, 1, last=True)

            def hT_copies(n, p, layer):
                act.wait_ge(hT_mm, n + 1)
                act.wait_ge(s_mm, n - 1)
                hT_out_of(hT_ps, n, p, layer)

            def exp1(n):
                act.wait_ge(sub_done, n + 1)
                nc.scalar.activation(px[:], sx[:], ACT.Exp, scale=SCALE1).then_inc(exp_done, 1)

            def pT_copies(n):
                for g in range(2):
                    act.wait_ge(pT_mm, 3 * n + g + 1)
                    if g == 0 and some(n):
                        act.wait_ge(o_mm, n)
                    nc.scalar.copy(pT[:, 4 * g:4 * g + 4], pT_ps[g][:, :].rearrange("p (j t) -> p j t", j=4))\
                        .then_inc(pT_out, 1)
                act.wait_ge(pT_mm, 3 * n + 3)
                nc.scalar.copy(pTb[:], pTb_ps).then_inc(pT_out, 1)

            def hTm_copies(i):
                act.wait_ge(hTm_mm, i + 1)
                at = 4 * LAYERS
                for c in range(DC):
                    nc.scalar.activation(hTm[:, c, i * P:(i + 1) * P], hTm_ps[i % 2][:, c * P:(c + 1) * P],
                                         ACT.Identity, bias=ln_all[:, at + DC + c:at + DC + c + 1],
                                         scale=ln_all[:, at + c:at + c + 1]).then_inc(hTm_out, 1)

            def attention(layer):
                def pair(n, last=False):
                    for p in range(2):
                        exp1(n + p)
                        if last and p == 1 and layer + 1 < LAYERS:
                            kT_copy((layer + 1) * H, 0, layer + 1)
                        pT_copies(n + p)
                        if not last:
                            hT_copies(n + p + 2, p, layer)
                        elif layer + 1 < LAYERS:
                            hT_copies(n + p + 2, p, layer + 1)
                        elif p == 0:
                            for i in range(HALF):
                                hTm_copies(i)

                n0 = layer * TILES
                vw_odd((layer + 1) * H - 1, HP - 1, SLOTS - 1)
                if layer == 0:
                    oT0_copy(TILES - 1)
                pair(n0)
                with act.Fori(1, B - 1) as b:
                    pair(b * 2 + n0)
                pair(n0 + TILES - 2, last=True)

            attention(0)

            def round1(r, last=False):
                for w in range(SLOTS):
                    h = r * SLOTS + w
                    vT_copy(h, w, 1)
                    if not (last and w == SLOTS - 1):
                        kT_copy(h + 1, (w + 1) % SLOTS, 1)
                        vw_odd(h, (r - SLOTS) * 2 + w // 2, w)

            with act.Fori(SLOTS, LAYERS * SLOTS - 1) as r:
                round1(r)
            round1(LAYERS * SLOTS - 1, last=True)
            attention(1)

            act.wait_ge(mlp_in, 48)
            for half in range(TILES // HALF):
                if half:
                    act.wait_ge(y_mm, half * HALF)
                for f in range(FC):
                    if half == 0 and f >= HALF:
                        hTm_copies(f)
                    act.wait_ge(g_mm, half * FC + f + 1)
                    nc.scalar.activation(gT[:, f], g_ps[f % 2], ACT.Gelu, bias=bfc1[:, f:f + 1])\
                        .then_inc(g_out, 1)

        @block.vector
        def _(dve):
            dve.wait_ge(w0_in, 16)
            for c in range(DC):
                nc.vector.tensor_copy(
                    wk_rep[:, c].rearrange("p (k g d) -> p k g d", k=KVH, g=G),
                    w0[:, c, D:D + KVH * HD].rearrange("p (k d) -> p k d", k=KVH).unsqueeze(2)
                    .to_broadcast([P, KVH, G, HD])).then_inc(wkrep_done, 1)
            dve.wait_ge(const_in, 32)
            for c in range(DC):
                dve.wait_ge(kT0_out, c + 1)
                nc.vector.tensor_tensor(
                    kblk[:, c], kT0[:, c, 0:S2].unsqueeze(1).to_broadcast([P, NHC, S2]),
                    blockmask[:, :].unsqueeze(2).to_broadcast([P, NHC, S2]), ALU.mult).then_inc(kblk_done, 1)
            def tile_of(i):
                return X[:, bass.ds(i, 1), :].rearrange("p a d -> p (a d)")

            def ln_moments(x, n):
                if some(n):
                    dve.wait_ge(ln_done, n)
                nc.vector.bn_stats(stats[:], x).then_inc(ln_stats, 1)
                dve.wait_ge(ln_stats, n + 1)
                nc.vector.tensor_copy(carrier[:], stats[:, 0:1])
                nc.vector.bn_aggr(mv[:], stats[:]).then_inc(ln_mv, 1)

            def ln_normal(out, x, n):
                dve.wait_ge(ln_rstd, n + 1)
                nc.vector.tensor_scalar(out, x, mv[:, 0:1], rstd[:], ALU.subtract, ALU.mult).then_inc(ln_done, 1)

            dve.wait_ge(mask_in, 16)

            def masked0(i, p, q):
                if q == 0 and not (isinstance(i, int) and i < 2):
                    dve.wait_ge(pT0_mm, 4 * i - 4)
                dve.wait_ge(s0_mm, QUARTERS * i + q + 1)
                nc.vector.tensor_tensor(
                    sc0[p][:, q * QH * S2:(q + 1) * QH * S2].rearrange("p (h t) -> p h t", t=S2),
                    s0_ps.rearrange("p (j t) -> p j t", t=S2),
                    mask[:, bass.ds(i, 1), :].to_broadcast([P, QH, S2]), ALU.add).then_inc(sc0_done, 1)

            def max0(i, p):
                dve.wait_ge(sc0_done, QUARTERS * i + QUARTERS)
                nc.vector.tensor_reduce(mx0[:], sc0[p].rearrange("p (h t) -> p h t", t=S2), AX_X, ALU.max)\
                    .then_inc(mx0_done, 1)

            def sub0(i, p):
                dve.wait_ge(mx0_done, i + 1)
                nc.vector.tensor_tensor(
                    sc0[p].rearrange("p (h t) -> p h t", t=S2), sc0[p].rearrange("p (h t) -> p h t", t=S2),
                    mx0[:].unsqueeze(2).to_broadcast([P, NH, S2]), ALU.subtract).then_inc(sub0_done, 1)

            def out0(i, p):
                dve.wait_ge(pv0_mm, i + 1)
                o = o0_ps.rearrange("p (h e) -> p h e", e=VO)
                nc.vector.reciprocal(rden0[:].unsqueeze(2), o[:, :, HD:VO]).then_inc(rden0_done, 1)
                dve.wait_ge(rden0_done, i + 1)
                nc.vector.tensor_tensor(o0[p][:].rearrange("p (h d) -> p h d", d=HD), o[:, :, 0:HD],
                                        rden0[:].unsqueeze(2).to_broadcast([P, NH, HD]), ALU.mult)\
                    .then_inc(o0_done, 1)

            def residual0(i):
                dve.wait_ge(wo0_mm, i + 1)
                if some(i):
                    dve.wait_ge(ln_done, ln_of0(i))
                dve.wait_ge(xbo_done, i + 1)
                nc.vector.tensor_tensor(y0[:], wo0_ps, tile_of(i), ALU.add).then_inc(y0_done, 1)
                dve.wait_ge(y0_done, i + 1)
                ln_moments(y0[:], ln_of0(i))

            def normal0(i):
                if some(i):
                    dve.wait_ge(z1_done, i)
                ln_normal(z0[:], y0[:], ln_of0(i))

            def ac_copy(h, hh, w, j, layer=0):
                dve.wait_ge(ac_mm, 3 * h + j + 1)
                ps = ac_ps[layer][(w + j) % 2]
                nc.vector.tensor_copy(AC[:, j, :, hh, :].rearrange("p b a t -> p b (a t)"),
                                      ps[:, 0:CK].rearrange("p (b t) -> p b t", b=B)).then_inc(ac_out, 1)
                nc.vector.tensor_copy(ACb[:, j, hh], ps[:, CK:CK + 1]).then_inc(ac_out, 1)

            def vwb_add(h, layer):
                dve.wait_ge(vwb_mm, h + 1)
                if some(h):
                    dve.wait_ge(vwb_out, h)
                nc.vector.tensor_tensor(VWb[0:H, :], VWb[0:H, :], vwb_ps[layer], ALU.add).then_inc(vwb_out, 1)

            def vw_even(h, hp, w):
                dve.wait_ge(vw_mm, h + 1)
                rows_to = slice(S2 * (w % 2), S2 * (w % 2) + S2)
                nc.vector.tensor_copy(VW[rows_to, 0::2, bass.ds(hp, 1), :].rearrange("p b a d -> p b (a d)"),
                                      vw_ps[0:S2]).then_inc(vw_out_dve, 1)

            def tile0(b, p, first=False, last=False):
                i = 2 * b + p
                w1, w2 = 2 * p, 2 * p + 1
                h1, h2 = SLOTS * b + w1, SLOTS * b + w2
                hh1, hh2 = bass.ds(SLOTS * b + w1, 1), bass.ds(SLOTS * b + w2, 1)
                hp = 2 * b + p
                next_tile = not (last and p == 1)
                if next_tile:
                    masked0(i + 1, 1 - p, 0)
                    masked0(i + 1, 1 - p, 1)
                ac_copy(h1, hh1, w1, 0)
                if next_tile:
                    masked0(i + 1, 1 - p, 2)
                ac_copy(h1, hh1, w1, 1)
                if not (first and p == 0):
                    residual0(i - 1)
                if next_tile:
                    masked0(i + 1, 1 - p, 3)
                ac_copy(h1, hh1, w1, 2)
                vwb_add(h1, 0)
                if next_tile:
                    max0(i + 1, 1 - p)
                vw_even(h1, hp, w1)
                if next_tile:
                    sub0(i + 1, 1 - p)
                if not (first and p == 0):
                    normal0(i - 1)
                if not next_tile:
                    for n in range(2):
                        dve.wait_ge(x1_done, 2)
                        ln_moments(tile_of(n), ln_of1(n))
                        ln_normal(xn[n][:], tile_of(n), ln_of1(n))
                ac_copy(h2, hh2, w2, 0)
                out0(i, p)
                ac_copy(h2, hh2, w2, 1)
                ac_copy(h2, hh2, w2, 2)
                if next_tile:
                    vwb_add(h2, 0)
                    vw_even(h2, hp, w2)

            for q in range(QUARTERS):
                masked0(0, 0, q)
            max0(0, 0)
            sub0(0, 0)
            dve.wait_ge(fills, N_FILLS)
            dve.wait_ge(bv_in, 16)
            dve.wait_ge(v0_mm, 1)
            v_ps = s_banks[:, 2, 0:B * KVH * HD].rearrange("p (b k d) -> p b k d", b=B, k=KVH)
            bv = rows[:, 4 * D:].rearrange("p (k d) -> p k d", k=KVH).unsqueeze(1).to_broadcast([P, B, KVH, HD])
            for half in range(2):
                part = slice(S2 * half, S2 * half + S2)
                nc.vector.tensor_tensor(vblk[part, :, :, VO * half:VO * half + HD], v_ps[part], bv[part], ALU.add)\
                    .then_inc(v0_out, 1)
            tile0(0, 0, first=True)
            tile0(0, 1, first=True)
            with dve.Fori(1, B - 1) as b:
                tile0(b, 0)
                tile0(b, 1)
            tile0(B - 1, 0, last=True)
            tile0(B - 1, 1, last=True)

            def scores_out(n, b):
                dve.wait_ge(s_mm, n + 1)
                nc.vector.tensor_tensor(
                    sx[:, :, 0:S2], sx_ps.rearrange("p r (j t) -> p (r j) t", t=S2),
                    AC[:, DC, bass.ds(b, 1)].rearrange("p a h t -> p (a h) t"), ALU.add).then_inc(sx_done, 1)
                nc.vector.tensor_tensor(sx[:, :, S2:KEYS], sxb_ps.unsqueeze(2), ACb[:, DC, :].unsqueeze(2), ALU.add)\
                    .then_inc(sx_done, 1)
                dve.wait_ge(sx_done, 2 * n + 2)
                nc.vector.tensor_reduce(mx[:], sx[:], AX_X, ALU.max).then_inc(mx_done, 1)
                dve.wait_ge(mx_done, n + 1)
                nc.vector.tensor_tensor(sx[:], sx[:], mx[:].unsqueeze(2).to_broadcast([P, H, KEYS]), ALU.subtract)\
                    .then_inc(sub_done, 1)

            def sums(n):
                dve.wait_ge(exp_done, n + 1)
                nc.vector.tensor_reduce(sm[:], px[:], AX_X, ALU.add).then_inc(sm_done, 1)
                dve.wait_ge(sm_done, n + 1)
                nc.vector.reciprocal(rs[:], sm[:]).then_inc(rs_done, 1)

            def weights(n):
                dve.wait_ge(rs_done, n + 1)
                if some(n):
                    dve.wait_ge(pT_mm, 3 * n)
                nc.vector.tensor_tensor(pm[:], px[:, :, 0:S2], rs[:].unsqueeze(2).to_broadcast([P, H, S2]),
                                        ALU.mult).then_inc(pm_done, 1)
                nc.vector.tensor_tensor(pmb[:, 0:H].unsqueeze(2), px[:, :, S2:KEYS], rs[:].unsqueeze(2), ALU.mult)\
                    .then_inc(pm_done, 1)

            def x_add(n, i):
                dve.wait_ge(o_mm, n + 1)
                nc.vector.tensor_tensor(tile_of(i), tile_of(i), o_ps, ALU.add).then_inc(x_done, 1)

            def mlp_moments(half):
                if half:
                    dve.wait_ge(m_mv, HALF * half)
                for j in range(HALF):
                    nc.vector.bn_stats(stats4[:, j, :], tile_of(half * HALF + j)).then_inc(m_stats, 1)
                if half:
                    dve.wait_ge(m_done, HALF * half)
                for j in range(HALF):
                    dve.wait_ge(m_stats, half * HALF + j + 1)
                    nc.vector.bn_aggr(mv4[:, j, :], stats4[:, j, :]).then_inc(m_mv, 1)

            def mlp_normal(half):
                dve.wait_ge(m_rstd, half + 1)
                for j in range(HALF):
                    i = half * HALF + j
                    if half:
                        dve.wait_ge(hTm_mm, j + 1)
                    else:
                        dve.wait_ge(hT_mm, LAYERS * TILES)
                    nc.vector.tensor_scalar(xn[j][:], tile_of(i), mv4[:, j, 0:1], rstd4[:, j:j + 1], ALU.subtract,
                                            ALU.mult).then_inc(m_done, 1)

            def attention(layer):
                n0 = layer * TILES
                heads = layer * H + H

                def pair(b, first=False, last=False):
                    for p in range(2):
                        i = 2 * b + p
                        n = n0 + i
                        mlp = last and layer + 1 == LAYERS
                        ahead = p if last else i + 2
                        scores_out(n, b)
                        if first and p == 0:
                            vwb_add(heads - 1, layer)
                            vw_even(heads - 1, HP - 1, SLOTS - 1)
                        if layer == 0 and first and p == 0:
                            residual0(TILES - 1)
                            sums(n)
                            normal0(TILES - 1)
                        if layer == 0 and first and p == 1:
                            dve.wait_ge(x1_done, TILES)
                        if mlp and p == 0:
                            mlp_moments(0)
                        if not mlp:
                            ln_moments(tile_of(ahead), ln_of1(n + 2))
                        if not (layer == 0 and first and p == 0):
                            sums(n)
                        if not mlp:
                            dve.wait_ge(hT_mm, n + 1)
                            ln_normal(xn[p][:], tile_of(ahead), ln_of1(n + 2))
                        weights(n)
                        if last and p == 1 and not mlp:
                            for j in range(DC):
                                ac_copy(heads, slice(0, 1), 0, j, layer + 1)
                        if not (first and p == 0):
                            x_add(n - 1, i - 1)
                        if mlp and p == 0:
                            mlp_normal(0)

                pair(0, first=True)
                with dve.Fori(1, B - 1) as b:
                    pair(b)
                pair(B - 1, last=True)
                x_add(n0 + TILES - 1, TILES - 1)

            attention(0)
            dve.wait_ge(x_done, TILES)
            nc.vector.memset(VWb[0:H, :], 0.0).then_inc(vwb_zero, 1)
            dve.wait_ge(vwb_zero, 1)

            def round1(r, last=False):
                for w in range(SLOTS):
                    h, at = r * SLOTS + w, (r - SLOTS) * SLOTS + w
                    ac_copy(h, bass.ds(at, 1), w, 2, 1)
                    if not (last and w == SLOTS - 1):
                        vwb_add(h, 1)
                        vw_even(h, (r - SLOTS) * 2 + w // 2, w)
                        for j in range(DC):
                            ac_copy(h + 1, bass.ds(at + 1, 1), (w + 1) % SLOTS, j, 1)

            with dve.Fori(SLOTS, LAYERS * SLOTS - 1) as r:
                round1(r)
            round1(LAYERS * SLOTS - 1, last=True)
            attention(1)

            def x_plus_b2(i):
                if i < HALF:
                    dve.wait_ge(x_done, LAYERS * TILES)
                nc.vector.tensor_tensor(tile_of(i), tile_of(i), rows[:, 3 * D:4 * D], ALU.add).then_inc(xb2_done, 1)

            dve.wait_ge(rows_in, 16 * 4)
            dve.wait_ge(x_done, LAYERS * TILES)
            mlp_moments(1)
            for j in range(HALF):
                x_plus_b2(j)
            mlp_normal(1)
            for j in range(HALF):
                dve.wait_ge(m_done, HALF + j + 1)
                x_plus_b2(HALF + j)
            for i in range(TILES):
                dve.wait_ge(xb2_done, i + 1)
                dve.wait_ge(y_mm, i + 1)
                nc.vector.tensor_tensor(tile_of(i), tile_of(i), y_ps[i % 2], ALU.add).then_inc(y_done, 1)

        @block.tensor
        def _(pe):
            def mm(out, lhsT, rhs, k=0, n=1, **kw):
                return nc.tensor.matmul(out, lhsT, rhs, start=(k == 0), stop=(k == n - 1), **kw)

            pe.wait_ge(ctx_in, 16)
            pe.wait_ge(w0_in, 16)
            pe.wait_ge(wkrep_done, DC)
            for m in range(DC):
                for c in range(DC):
                    last = mm(s_banks[:, m, 0:CK], wk_rep[:, c, m * P:(m + 1) * P], ctxT[:, c], c, DC)
                last.then_inc(kT0_mm, 1)

            def q0(b, i=None):
                if i is None:
                    pe.wait_ge(xt0_in, 16)
                else:
                    pe.wait_ge(xt_in, 16)
                    if some(i):
                        pe.wait_ge(y0_done, i)
                for m in range(DC):
                    for c in range(DC):
                        last = mm(q0_ps[m], w0[:, c, m * P:(m + 1) * P], xT[:, c, bass.ds(b * S, S)], c, DC,
                                  skip_group_check=True)
                    last.then_inc(q0_mm, 1)

            q0(0)
            wv = slice(D + KVH * HD, D + 2 * KVH * HD)
            for b in range(B):
                for half in range(2):
                    for c in range(DC):
                        last = mm(s_banks[S2 * half:S2 * half + S2, 2, b * KVH * HD:(b + 1) * KVH * HD],
                                  ctxT[:, c, b * S2:(b + 1) * S2], w0[:, c, wv], c, DC)
            last.then_inc(v0_mm, 1)

            def s0(i, p, q):
                if p == 0 and q == 0:
                    pe.wait_ge(q0_out, i + DC)
                    pe.wait_ge(kblk_done, i + DC)
                if isinstance(i, int) and i == 0 and q == 0:
                    pe.wait_ge(kT0_out, DC)
                else:
                    pe.wait_ge(sc0_done, QUARTERS * i + q)
                c, half = q // 2, q % 2
                mm(s0_ps, qT0[:, c, p * P:(p + 1) * P],
                   kblk[:, c, half * QH:(half + 1) * QH, :].rearrange("p h t -> p (h t)")).then_inc(s0_mm, 1)

            def turn0(i, p, g):
                if g == 0:
                    pe.wait_ge(exp0_done, i + 1)
                if some(4 * i + g):
                    pe.wait_ge(pT0_out, 4 * i + g)
                for j in range(4):
                    last = nc.tensor.transpose(pT0_ps[:, j * P:(j + 1) * P],
                                               sc0[p][:, (4 * g + j) * P:(4 * g + j + 1) * P], ident[:])
                last.then_inc(pT0_mm, 1)

            def values0(i, g, b):
                pe.wait_ge(pT0_out, 4 * i + g + 1)
                if g == 0:
                    if some(i):
                        pe.wait_ge(o0_done, i)
                    pe.wait_ge(v0_out, 2)
                for j in range(4):
                    hp = 4 * g + j
                    last = mm(o0_ps[:, hp * 2 * VO:(hp + 1) * 2 * VO], pT0[:, hp],
                              vblk[:, bass.ds(b, 1), hp * 2 // G, :].rearrange("p a e -> p (a e)"),
                              skip_group_check=True)
                if g == 3:
                    last.then_inc(pv0_mm, 1)

            def turn_o0(i, p, batches):
                pe.wait_ge(o0_done, i + 1)
                pe.wait_ge(q0_out, DC * batches)
                if some(i):
                    pe.wait_ge(y0_done, i)
                for c in range(DC):
                    last = nc.tensor.transpose(oT0_ps[:, c * P:(c + 1) * P], o0[p][:, c * P:(c + 1) * P], ident[:])
                last.then_inc(oT0_mm, 1)

            def wo0(i):
                pe.wait_ge(oT0_out, i + 1)
                for c in range(DC):
                    last = mm(wo0_ps, oT0[:, c], w0[:, c, D + 2 * KVH * HD:], c, DC, skip_group_check=True)
                last.then_inc(wo0_mm, 1)

            def col(w, at, n=P):
                return ring[w][:, at:at + n]

            def keys(h, w, layer):
                pe.wait_ge(w_in[w], (h - w) * 4 + 16)
                if some(h):
                    if layer == 0:
                        pe.wait_ge(vwb_out, h)
                    else:
                        pe.wait_ge(kT_out, h)
                for c in range(DC):
                    last = mm(kT_ps[layer], col(w, W_K + c * K), ctxT[:, c], c, DC)
                last.then_inc(kT_mm, 1)

            def vals(h, w, layer):
                pe.wait_ge(kT_out, h + 1) if layer == 0 else pe.wait_ge(vT_out, h)
                for c in range(DC):
                    last = mm(vT_ps[layer], col(w, W_V + c * K), ctxT[:, c], c, DC, skip_group_check=True)
                last.then_inc(vT_mm, 1)

            def ac(h, w, j, layer=0):
                if j == 0:
                    pe.wait_ge(kT_out, h + 1)
                    pe.wait_ge(headcols, 2 * h + 2)
                if some(3 * h + j - 1):
                    pe.wait_ge(ac_out, 2 * (3 * h + j) - 2)
                lhsT = col(w, W_QT + j * P) if j < DC else bq_all[:]
                mm(ac_ps[layer][(w + j) % 2], lhsT, kTs[:]).then_inc(ac_mm, 1)

            def vwb(h, w, layer):
                pe.wait_ge(vT_out, h + 1) if layer == 0 else pe.wait_ge(vwb_out, h)
                mm(vwb_ps[layer], col(w, W_BV, H), col(w, W_O, D)).then_inc(vwb_mm, 1)

            def vw(h, w):
                pe.wait_ge(vT_out, h + 1)
                if some(h):
                    pe.wait_ge(vw_out_dve, h)
                    pe.wait_ge(vw_out_act, h)
                for pair_of in range(2):
                    last = mm(vw_ps[:, pair_of], vTs[:, pair_of * P:(pair_of + 1) * P], col(w, W_O, D),
                              skip_group_check=True)
                last.then_inc(vw_mm, 1)

            def hT_turn(ps, n, p):
                pe.wait_ge(ln_done, ln_of1(n) + 1)
                for c in range(DC):
                    last = nc.tensor.transpose(ps[:, c * P:(c + 1) * P], xn[p][:, c * P:(c + 1) * P], ident[:])
                last.then_inc(hT_mm, 1)

            def tile0(b, p, first=False, last=False):
                i = 2 * b + p
                w1, w2 = 2 * p, 2 * p + 1
                h1, h2 = SLOTS * b + w1, SLOTS * b + w2
                next_tile = not (last and p == 1)
                if next_tile:
                    s0(i + 1, 1 - p, 0)
                keys(h1, w1, 0)
                if not (first and p == 0):
                    turn_o0(i - 1, 1 - p, b + 1 if p == 0 or last else b + 2)
                if next_tile:
                    s0(i + 1, 1 - p, 1)
                vals(h1, w1, 0)
                ac(h1, w1, 0)
                if next_tile:
                    s0(i + 1, 1 - p, 2)
                ac(h1, w1, 1)
                if not (first and p == 0):
                    wo0(i - 1)
                if next_tile:
                    s0(i + 1, 1 - p, 3)
                ac(h1, w1, 2)
                vwb(h1, w1, 0)
                turn0(i, p, 0)
                vw(h1, w1)
                turn0(i, p, 1)
                values0(i, 0, b)
                keys(h2, w2, 0)
                turn0(i, p, 2)
                values0(i, 1, b)
                vals(h2, w2, 0)
                turn0(i, p, 3)
                values0(i, 2, b)
                ac(h2, w2, 0)
                values0(i, 3, b)
                ac(h2, w2, 1)
                if p == 0 and not last:
                    q0(b + 1, i)
                if not next_tile:
                    pe.wait_ge(y0_done, i)
                    for n in range(2):
                        hT_turn(first_hT_ps[n], n, n)
                ac(h2, w2, 2)
                if next_tile:
                    vwb(h2, w2, 0)
                    vw(h2, w2)

            for q in range(QUARTERS):
                s0(0, 0, q)
            pe.wait_ge(ident_in, 16)
            tile0(0, 0, first=True)
            tile0(0, 1, first=True)
            with pe.Fori(1, B - 1) as b:
                tile0(b, 0)
                tile0(b, 1)
            tile0(B - 1, 0, last=True)
            tile0(B - 1, 1, last=True)

            def hT_turn_ahead(n, p):
                pe.wait_ge(hT_out, DC * n)
                hT_turn(hT_ps, n, p)

            def scores(n, p, b):
                pe.wait_ge(hT_out, DC * n + DC)
                if some(n):
                    pe.wait_ge(sx_done, 2 * n)
                for half in range(2):
                    for c in range(DC):
                        mm(sx_ps[:, half], hT[p][:, c],
                           AC[:, c, bass.ds(b, 1), half * HP:(half + 1) * HP, :].rearrange("p a h t -> p (a h t)"),
                           c, DC)
                for c in range(DC):
                    last = mm(sxb_ps, hT[p][:, c], ACb[:, c, :], c, DC)
                last.then_inc(s_mm, 1)

            def weights_turn(n):
                pe.wait_ge(pm_done, 2 * n + 2)
                if some(n):
                    pe.wait_ge(pT_out, 3 * n)
                for g in range(2):
                    for j in range(4):
                        hp = 4 * g + j
                        last = nc.tensor.transpose(pT_ps[g][:, j * P:(j + 1) * P],
                                                   pm[:, 2 * hp:2 * hp + 2, :].rearrange("p h t -> p (h t)"), ident[:])
                    last.then_inc(pT_mm, 1)
                nc.tensor.transpose(pTb_ps, pmb[:], ident[:]).then_inc(pT_mm, 1)

            def values(n, b):
                if some(n):
                    pe.wait_ge(x_done, n)
                for hp in range(HP):
                    if hp % 4 == 0:
                        pe.wait_ge(pT_out, 3 * n + hp // 4 + 1)
                    mm(o_ps, pT[:, hp], VW[:, bass.ds(b, 1), hp, :].rearrange("p a d -> p (a d)"), hp, HP + 1)
                pe.wait_ge(pT_out, 3 * n + 3)
                mm(o_ps, pTb[:], VWb[:], HP, HP + 1).then_inc(o_mm, 1)

            def hTm_turn(i):
                pe.wait_ge(m_done, i + 1)
                if i < 2:
                    pe.wait_ge(hT_out, LAYERS * TILES * DC)
                    pe.wait_ge(sx_done, 2 * LAYERS * TILES)
                else:
                    pe.wait_ge(hTm_out, DC * (i - 1))
                for c in range(DC):
                    last = nc.tensor.transpose(hTm_ps[i % 2][:, c * P:(c + 1) * P], xn[i % HALF][:, c * P:(c + 1) * P],
                                               ident[:])
                last.then_inc(hTm_mm, 1)

            def fc1_product(half, f):
                if f == 0:
                    pe.wait_ge(mlp_in, 48)
                    pe.wait_ge(hTm_out, (half + 1) * HALF * DC)
                if half or f >= 2:
                    pe.wait_ge(g_out, half * FC + f - 1)
                for c in range(DC):
                    last = mm(g_ps[f % 2], fc1[:, c, f * P:(f + 1) * P],
                              hTm[:, c, half * HALF * P:(half + 1) * HALF * P], c, DC)
                last.then_inc(g_mm, 1)

            def attention(layer):
                n0 = layer * TILES
                heads = layer * H + H

                def pair(b, last=False):
                    n = n0 + 2 * b
                    mlp = last and layer + 1 == LAYERS
                    for p in range(2):
                        if p == 0:
                            scores(n + 1, 1, b)
                        elif not last:
                            scores(n + 2, 0, b + 1)
                        elif not mlp:
                            pe.wait_ge(sx_done, 2 * n + 4)
                            keys(heads, 0, layer + 1)
                            for j in range(DC):
                                ac(heads, 0, j, layer + 1)
                        weights_turn(n + p)
                        if not mlp:
                            hT_turn_ahead(n + p + 2, p)
                        values(n + p, b)
                        if mlp and p == 0:
                            for i in range(HALF):
                                hTm_turn(i)
                            for f in range(2):
                                fc1_product(0, f)

                pe.wait_ge(ac_out, 6 * heads)
                pe.wait_ge(vwb_out, heads - 1)
                pe.wait_ge(vT_out, heads)
                if layer == 0:
                    pe.wait_ge(o0_done, TILES)
                scores(n0, 0, 0)
                vwb(heads - 1, SLOTS - 1, layer)
                vw(heads - 1, SLOTS - 1)
                if layer == 0:
                    pe.wait_ge(hT_out, 2 * DC)
                    turn_o0(TILES - 1, 1, B)
                    wo0(TILES - 1)
                    pe.wait_ge(y0_done, TILES)
                pe.wait_ge(vwb_out, heads)
                pe.wait_ge(vw_out_dve, heads)
                pe.wait_ge(vw_out_act, heads)
                pe.wait_ge(bo_in, 16 * layer + 16)
                pair(0)
                with pe.Fori(1, B - 1) as b:
                    pair(b)
                pair(B - 1, last=True)

            attention(0)

            def round1(r, last=False):
                for w in range(SLOTS):
                    h = r * SLOTS + w
                    if not (last and w == SLOTS - 1):
                        vals(h, w, 1)
                        ac(h, w, 2, 1)
                        keys(h + 1, (w + 1) % SLOTS, 1)
                        pe.wait_ge(x_done, TILES)
                        vwb(h, w, 1)
                        vw(h, w)
                        for j in range(DC):
                            ac(h + 1, (w + 1) % SLOTS, j, 1)
                    else:
                        ac(h, w, 2, 1)
                        vals(h, w, 1)

            with pe.Fori(SLOTS, LAYERS * SLOTS - 1) as r:
                round1(r)
            round1(LAYERS * SLOTS - 1, last=True)
            attention(1)

            for half in range(TILES // HALF):
                for f in range(0 if half else 2, FC):
                    if half == 0 and f >= HALF:
                        hTm_turn(f)
                    fc1_product(half, f)
                for j in range(HALF):
                    i = half * HALF + j
                    if i >= 2:
                        pe.wait_ge(y_done, i - 1)
                    for f in range(FC):
                        if j == 0:
                            pe.wait_ge(g_out, half * FC + f + 1)
                        last = mm(y_ps[i % 2], gT[:, f, j * P:(j + 1) * P], fc2[:, f], f, FC)
                    last.then_inc(y_mm, 1)


def kernel(**inputs):
    import numpy as np
    import concourse.bacc as _bacc
    from concourse.bass_utils import run_bass_kernel_spmd as _run

    a = {n: np.asarray(v) for n, v in inputs.items()}

    def columns(v):
        return v.reshape(-1, P).T

    def rows_by_chunk(w):
        return w.reshape(DC, P, -1).transpose(1, 0, 2)

    x, c = a["x"], a["ctx_2048"]
    p0, p1 = "L0_xattn_", "L1_xattn_"
    bk_rep = np.broadcast_to(a[p0 + "bk"].reshape(KVH, 1, HD), (KVH, G, HD)).reshape(-1)
    heads = np.zeros((LAYERS, H, P, W_N), np.float32)
    for i in range(LAYERS):
        def get(name):
            return a[f"{p1}{name}{i + 1}"]
        for at, name in ((W_K, "wk"), (W_V, "wv")):
            heads[i, :, :, at:at + D] = get(name).reshape(DC, P, H, K).transpose(2, 1, 0, 3).reshape(H, P, D)
        heads[i, :, :, W_QT:W_QT + D] = get("wq").reshape(D, H, K).transpose(1, 2, 0)
        heads[i, :, :, W_O:W_O + D] = get("wo").reshape(H, K, D)
        for h in range(H):
            heads[i, h, :, W_BV + h] = get("bias_v").reshape(H, K)[h]
        for j, name in enumerate(("bk", "bq", "bias_k", "bv")):
            heads[i, :, :, W_COL + j] = get(name).reshape(H, K)
    blockmask = np.zeros((P, NHC), np.float32)
    for row in range(P):
        blockmask[row, row // HD] = 1.0
    arrays = {
        "x_tok": x.reshape(TILES, P, D).transpose(1, 0, 2),
        "xT": rows_by_chunk(x.reshape(-1, D).T),
        "ctxT": rows_by_chunk(c.reshape(-1, D).T),
        "mask": a["mask_Bx1xSxS2_ff0"].reshape(TILES, P, S2).transpose(1, 0, 2),
        "w0": np.concatenate([rows_by_chunk(a[p0 + n]) for n in ("Wq", "Wk", "Wv", "Wo")], axis=2),
        "cols0": np.concatenate([columns(a[p0 + "bq"]), columns(bk_rep)], axis=1),
        "rows": np.concatenate([a[p0 + "bo"], a[p0 + "gamma"], a[p0 + "beta"], a[p1 + "b_fc2"], a[p0 + "bv"]])[None],
        "heads": heads.reshape(LAYERS * H, P, W_N),
        "bo": np.stack([a[f"{p1}bo{i + 1}"] for i in range(LAYERS)]),
        "ln": np.concatenate([columns(a[p1 + n]) for n in ("ln1_scale", "ln1_offset", "ln2_scale", "ln2_offset",
                                                           "ln_mlp_scale", "ln_mlp_offset")], axis=1),
        "fc1": rows_by_chunk(a[p1 + "w_fc1"]),
        "bfc1": columns(a[p1 + "b_fc1"]),
        "fc2": a[p1 + "w_fc2"].reshape(FC, P, D).transpose(1, 0, 2),
        "blockmask": blockmask,
        "ident": np.eye(P, dtype=np.float32),
    }
    nc = _bacc.Bacc("TRN2", target_bir_lowering=False, num_devices=1)
    feed, args = {}, []
    for name, value in arrays.items():
        value = np.ascontiguousarray(value)
        feed[f"in_{name}_dram"] = value
        args.append(nc.dram_tensor(f"in_{name}_dram", value.shape, mybir.dt.from_np(value.dtype),
                                   kind="ExternalInput").ap())
    args.append(nc.dram_tensor("out_dram", (P, TILES, D), F32, kind="ExternalOutput").ap())
    build(nc, *args)
    got = _run(nc, [feed], core_ids=[0]).results[0]["out_dram"]
    return got.transpose(1, 0, 2).reshape(B, S, D)
```

```python
from contextlib import ExitStack

import concourse.bass as bass
from concourse import mybir

F32, F32R = mybir.dt.float32, mybir.dt.float32r
ALU = mybir.AluOpType
ACT = mybir.ActivationFunctionType
AX_X = mybir.AxisListType.X

P = 128
B, S, S2, D = 4, 256, 64, 256
DC = D // P
TILES = B * S // P
NH, KVH, HD = 32, 8, 8
G = NH // KVH
QUARTERS, QH = 4, NH // 4
NHC = P // HD
VO = HD + 1
LAYERS, H, K = 2, 16, 128
HP = H // 2
KEYS = S2 + 1
CK = B * S2
SLOTS = 4
F = 1024
FC = F // P
HALF = 4
W_K, W_QT, W_V, W_O, W_BV = 0, D, 2 * D, 3 * D, 4 * D
W_COL = W_BV + H
W_N = W_COL + 4
W_POOL = W_O
EPS0, EPS1 = 1e-6, 1e-5
SCALE0, SCALE1 = HD ** -0.5, K ** -0.5
N_FILLS = 11
WARM_UPS = 12


def some(n):
    return not (isinstance(n, int) and n <= 0)


def ln_of1(n):
    return TILES + n - 2


BATCHES = ((0, 2), (0, HALF), (HALF, HALF))
BATCH_END = (2, 2 + HALF, 2 + 2 * HALF)


def build(nc, x_tok, xT_d, ctxT_d, mask_d, w0_d, cols0_d, rows_d, heads_d, bo_d, ln_d, fc1_d, bfc1_d, fc2_d,
          blockmask_d, ident_d, out_d):
    with ExitStack() as ctx:
        place = {}

        def sb(name, shape, dtype=F32):
            place[name] = -(-nc.sbuf_base // 32) * 32
            return ctx.enter_context(nc.sbuf_tensor(name, shape, dtype))

        def over(name, shape, where, skip=0, dtype=F32R):
            return nc.alloc_sbuf_tensor_at(name, shape, dtype, offset=place[where] + 4 * skip)

        def pb(name, shape):
            return ctx.enter_context(nc.psum_tensor(name, shape, F32))

        def sem(name):
            return ctx.enter_context(nc.semaphore(name))

        ident = sb("ident", [P, P])
        ones = sb("ones", [P, P])
        expo = sb("expo", [P, 1])
        eps0, eps1 = sb("eps0", [P, 1]), sb("eps1", [P, 1])
        X = sb("X", [P, TILES, D])
        ctxT = sb("ctxT", [P, DC, CK])
        stats = sb("stats", [P, 6])
        carrier = sb("carrier", [P, 1])
        pool_carrier = sb("pool_carrier", [P, 1])
        mv = sb("mv", [P, 2])
        ve = sb("ve", [P, 1])
        rstd = sb("rstd", [P, 1])
        stats4, mv4 = sb("stats4", [P, HALF, 6]), sb("mv4", [P, HALF, 2])
        ve4, rstd4 = sb("ve4", [P, HALF]), sb("rstd4", [P, HALF])
        xT = sb("xT", [P, DC, B * S])
        mask = sb("mask", [P, TILES, S2])
        w0 = sb("w0", [P, DC, D + KVH * HD * 2 + D])
        wk_rep = sb("wk_rep", [P, DC, D])
        cols0 = sb("cols0", [P, 4])
        bq_s = sb("bq_s", [P, DC])
        rows = sb("rows", [P, 4 * D + KVH * HD])
        kT0 = sb("kT0", [P, DC, CK])
        blockmask = sb("blockmask", [P, NHC])
        kblk = sb("kblk", [P, DC, NHC, S2])
        vblk = sb("vblk", [P, B, KVH, 2 * VO])
        qT0 = sb("qT0", [P, DC, S])
        scores_sb = sb("scores_sb", [P, 2, NH * S2])
        sc0 = [scores_sb[:, i, :] for i in range(2)]
        mx0 = sb("mx0", [P, NH])
        pT0 = sb("pT0", [P, NH // 2, P])
        rden0 = sb("rden0", [P, NH])
        o0 = [sb(f"o0_{i}", [P, D]) for i in range(2)]
        oT0 = sb("oT0", [P, DC, P])
        y0 = sb("y0", [P, D])
        z0 = sb("z0", [P, D])
        z1 = sb("z1", [P, D])
        ring = [sb(f"ring{w}", [P, W_N]) for w in range(SLOTS)]
        cols_hi = [sb(f"cols_hi{w}", [P, 4], F32R) for w in range(SLOTS)]
        cols_lo = [sb(f"cols_lo{w}", [P, 4], F32R) for w in range(SLOTS)]
        kTh = sb("kTh", [P, CK + 2], F32R)
        kTl = sb("kTl", [P, CK + 2], F32R)
        vTh = sb("vTh", [P, CK], F32R)
        bqh = sb("bqh", [P, P], F32R)
        vTl = over("vTl", [P, CK], "wk_rep")[:]
        bql = over("bql", [P, P], "wk_rep", CK)[:]
        ctxh = sb("ctxh", [P, DC, CK], F32R)
        ctxl = over("ctxl", [P, DC, CK], "ctxT")
        AC = sb("AC", [P, DC + 1, B, H, S2])
        ACb = sb("ACb", [P, DC + 1, H])
        VW = sb("VW", [P, B, HP, D])
        VWb = sb("VWb", [H + 1, D])
        ln_all = sb("ln_all", [P, (LAYERS + 1) * 4])
        xn = [sb(f"xn{i}", [P, D]) for i in range(HALF)]
        hT = [sb(f"hT{i}", [P, DC, P]) for i in range(2)]
        sx = sb("sx", [P, H, KEYS])
        pxm = sb("pxm", [P, 2, H * KEYS])
        px = pxm[:, 0, :].rearrange("p (h t) -> p h t", t=KEYS)
        pm = pxm[:, 1, 0:H * S2].rearrange("p (h t) -> p h t", t=S2)
        wh0 = [over(f"wh0_{w}", [P, W_COL], "pxm", w * H * KEYS) for w in range(2)]
        wh = [wh0 + wh0, [over(f"wh1_{w}", [P, W_COL], "scores_sb", w * W_COL) for w in range(SLOTS - 1)]
              + [over("wh1_3", [P, W_COL], "w0")]]
        wl = [over(f"wl{w}", [P, W_COL], f"ring{w}") for w in range(SLOTS)]
        pmb = sb("pmb", [P, H + 1])
        mx = sb("mx", [P, H])
        sm = sb("sm", [P, H])
        rs = sb("rs", [P, H])
        pT = pT0[:, 0:HP, :]
        pTb = sb("pTb", [H + 1, P])
        fc1 = sb("fc1", [P, DC, F])
        bfc1 = sb("bfc1", [P, FC])
        fc2 = over("fc2", [P, FC, D], "kblk", 0, F32)
        fc1h, fc1l = over("fc1h", [P, DC, F], "ring0"), over("fc1l", [P, DC, F], "fc1")
        fc2h, fc2l = over("fc2h", [P, FC, D], "ring2"), over("fc2l", [P, FC, D], "kblk")
        hTm = [z[:].rearrange("p (c t) -> p c t", c=DC) for z in (z0, z1)]
        hTmh, hTml = over("hTmh", [P, DC, B * S], "xT"), over("hTml", [P, DC, B * S], "mask")
        gTh, gTl = over("gTh", [P, FC, HALF * P], "scores_sb"), over("gTl", [P, FC, HALF * P], "AC")
        GELUS = 4
        gelu = over("gelu", [P, GELUS, HALF * P], "AC", FC * HALF * P, F32)

        s_banks = pb("s_banks", [P, 4, 512])
        bank4 = pb("bank4", [P, 512])
        bank5 = pb("bank5", [P, 512])
        bank6 = pb("bank6", [P, 512])
        bank7 = pb("bank7", [P, 512])
        s0_ps = s_banks[:, 0, :]
        pT0_ps = s_banks[:, 1, :]
        o0_ps = s_banks[:, 2, 0:NH * VO]
        oT0_ps = s_banks[:, 3, 0:D]
        wo0_ps = s_banks[:, 3, 256:256 + D]
        q0_ps = [s_banks[:, 3, c * S:(c + 1) * S] for c in range(DC)]
        first_hT_ps = [s_banks[:, 3, i * D:(i + 1) * D] for i in range(2)]
        kT_ps = [bank4[:, 0:CK], s_banks[:, 0, 0:CK]]
        vT_ps = [bank4[:, 256:256 + CK], s_banks[:, 3, 0:CK]]
        vwb_ps = [bank4[0:H, 0:D], bank6[0:H, 0:D]]
        vw_ps = bank5[:, :].rearrange("p (b d) -> p b d", b=2)
        ac_banks = [[bank6, bank7], [s_banks[:, 1, :], s_banks[:, 2, :], bank4]]

        def ac_ps(layer, w, j):
            return ac_banks[layer][(w + j) % 2 if layer == 0 else j][:, 0:CK + 2]

        sx_ps = s_banks[:, 0:2, :]
        sxb_ps = s_banks[:, 2, 0:H]
        pTb_ps = s_banks[0:H + 1, 3, 0:P]
        pT_ps = [bank4, bank5]
        o_ps = bank6[:, 0:D]
        hT_ps = bank7[:, 0:D]
        hTm_ps = [[bank7, bank7, bank7, s_banks[:, 2, :]][i // 2][:, i % 2 * D:(i % 2 + 1) * D] for i in range(TILES)]
        g_ps = [s_banks[:, 0, :], s_banks[:, 1, :]]
        y_ps = [bank4[:, 0:D], bank5[:, 0:D]]

        ident_in, bv_in, ln_in = (sem(n) for n in ("ident_in", "bv_in", "ln_in"))
        ctx_in, w0_in, x_in, xt0_in, xt_in, mask_in, const_in, rows_in, mlp_in = (
            sem(n) for n in ("ctx_in", "w0_in", "x_in", "xt0_in", "xt_in", "mask_in", "const_in", "rows_in", "mlp_in"))
        out_done = sem("out_done")
        fills = sem("fills")
        wkrep_done = sem("wkrep_done")
        ln_stats, ln_mv, ln_eps, ln_rstd, ln_done = (
            sem(n) for n in ("ln_stats", "ln_mv", "ln_eps", "ln_rstd", "ln_done"))
        bqs_done, kT0_mm, kT0_out, v0_mm, v0_out, q0_mm, q0_out, kblk_done = (
            sem(n) for n in ("bqs_done", "kT0_mm", "kT0_out", "v0_mm", "v0_out", "q0_mm", "q0_out", "kblk_done"))
        s0_mm, sc0_done, mx0_done, sub0_done, exp0_done = (
            sem(n) for n in ("s0_mm", "sc0_done", "mx0_done", "sub0_done", "exp0_done"))
        pT0_mm, pT0_out, pv0_mm, rden0_done, o0_done, oT0_mm, oT0_out, wo0_mm, y0_done = (
            sem(n) for n in ("pT0_mm", "pT0_out", "pv0_mm", "rden0_done", "o0_done", "oT0_mm", "oT0_out",
                             "wo0_mm", "y0_done"))
        xbo_done, z1_done, x1_done = (sem(n) for n in ("xbo_done", "z1_done", "x1_done"))
        w_in = [sem(f"w_in{w}") for w in range(SLOTS)]
        bo_in = sem("bo_in")
        kT_mm, kT_out, vT_mm, vT_out, headcols, ac_mm, ac_out, bqk_out = (
            sem(n) for n in ("kT_mm", "kT_out", "vT_mm", "vT_out", "headcols", "ac_mm", "ac_out", "bqk_out"))
        kTh_out, vTh_out, w_hi, w_lo, w_lo_dve, ctx_hi, ctx_lo = (
            sem(n) for n in ("kTh_out", "vTh_out", "w_hi", "w_lo", "w_lo_dve", "ctx_hi", "ctx_lo"))
        vw_mm, vw_out_dve, vw_out_act, vwb_mm, vwb_out = (
            sem(n) for n in ("vw_mm", "vw_out_dve", "vw_out_act", "vwb_mm", "vwb_out"))
        vwb_zero = sem("vwb_zero")
        hT_mm, hT_out, s_mm, sx_done, mx_done, sub_done, exp_done, sm_done, rs_done, pm_done = (
            sem(n) for n in ("hT_mm", "hT_out", "s_mm", "sx_done", "mx_done", "sub_done", "exp_done", "sm_done",
                             "rs_done", "pm_done"))
        half_mm, half_sx, half_mx, half_sub, half_exp, half_sm, half_rs, half_pm = (
            sem(n) for n in ("half_mm", "half_sx", "half_mx", "half_sub", "half_exp", "half_sm", "half_rs", "half_pm"))
        pT_mm, pT_out, o_mm, x_done = (sem(n) for n in ("pT_mm", "pT_out", "o_mm", "x_done"))
        hTm_mm, hTm_out, g_mm, g_out, y_mm, y_done = (
            sem(n) for n in ("hTm_mm", "hTm_out", "g_mm", "g_out", "y_mm", "y_done"))
        xb2_done = sem("xb2_done")
        fc_hi, fc_lo, hTm_hi, hTm_lo, g_hi, g_lo = (
            sem(n) for n in ("fc_hi", "fc_lo", "hTm_hi", "hTm_lo", "g_hi", "g_lo"))
        m_stats, m_mv, m_eps, m_rstd, m_done = (sem(n) for n in ("m_stats", "m_mv", "m_eps", "m_rstd", "m_done"))

        def fc_quarter(q):
            if q < DC:
                return fc1l[:, q], fc1[:, q], fc1h[:, q]
            at = slice((q - DC) * FC // 2, (q - DC + 1) * FC // 2)
            return fc2l[:, at], fc2[:, at], fc2h[:, at]

        block = ctx.enter_context(nc.Block())
        ROUNDS = LAYERS * H // SLOTS
        HEADS0 = H

        @block.sync
        def _(sp):
            sp.dma_start(ctxT[:], ctxT_d).then_inc(ctx_in, 16)
            sp.dma_start(w0[:], w0_d).then_inc(w0_in, 16)
            sp.dma_start(ring[0][:], heads_d[0]).then_inc(w_in[0], 16)
            sp.dma_start(mask[:], mask_d).then_inc(mask_in, 16)
            sp.dma_start(ident[:], ident_d).then_inc(ident_in, 16)
            sp.dma_start(rows[:, 4 * D:], rows_d[0:1, 4 * D:].to_broadcast([P, KVH * HD])).then_inc(bv_in, 16)
            sp.dma_start(ring[1][:], heads_d[1]).then_inc(w_in[1], 16)
            sp.dma_start(X[:], x_tok).then_inc(x_in, 16)
            for j in range(4):
                sp.dma_start(rows[:, j * D:(j + 1) * D], rows_d[0:1, j * D:(j + 1) * D].to_broadcast([P, D]))\
                    .then_inc(rows_in, 16)
            for w in range(2, SLOTS):
                sp.dma_start(ring[w][:], heads_d[w]).then_inc(w_in[w], 16)
            sp.dma_start(ln_all[:], ln_d).then_inc(ln_in, 16)
            sp.dma_start(xT[:, :, S:], xT_d[:, :, S:]).then_inc(xt_in, 16)
            sp.dma_start(VWb[H:H + 1, :], bo_d[0:1, :]).then_inc(bo_in, 16)
            with sp.Fori(1, ROUNDS) as r:
                for w in range(SLOTS):
                    sp.wait_ge(vw_mm, SLOTS * (r - 1) + w + 1)
                    sp.dma_start(ring[w][:], heads_d[SLOTS * r + w]).then_inc(w_in[w], 16)
            sp.wait_ge(x_done, TILES)
            sp.dma_start(VWb[H:H + 1, :], bo_d[1:2, :]).then_inc(bo_in, 16)
            sp.dma_start(fc1[:], fc1_d).then_inc(mlp_in, 16)
            sp.dma_start(bfc1[:], bfc1_d).then_inc(mlp_in, 16)
            sp.dma_start(fc2[:], fc2_d).then_inc(mlp_in, 16)
            for i in range(TILES):
                sp.wait_ge(y_done, i + 1)
                sp.dma_start(out_d[:, i, :], X[:, i, :]).then_inc(out_done, 16)
            sp.wait_ge(out_done, 16 * TILES)

        @block.gpsimd
        def _(pool):
            pool.memset(ones[:], 1.0).then_inc(fills, 1)
            pool.memset(expo[:], -0.5).then_inc(fills, 1)
            pool.memset(eps0[:], EPS0).then_inc(fills, 1)
            pool.memset(eps1[:], EPS1).then_inc(fills, 1)
            pool.memset(vblk[:], 0.0).then_inc(fills, 1)
            pool.memset(pmb[:], 1.0).then_inc(fills, 1)
            pool.memset(VWb[0:H, :], 0.0).then_inc(fills, 1)
            pool.memset(kTh[:, CK + 1:CK + 2].bitcast(F32), 0.0).then_inc(fills, 1)
            pool.memset(kTl[:, CK + 1:CK + 2].bitcast(F32), 0.0).then_inc(fills, 1)
            pool.wait_ge(fills, 9)
            pool.memset(vblk[0:S2, :, :, HD:HD + 1], 1.0).then_inc(fills, 1)
            pool.wait_ge(fills, 10)
            pool.memset(vblk[S2:P, :, :, VO + HD:VO + HD + 1], 1.0).then_inc(fills, 1)
            pool.wait_ge(fills, N_FILLS)

            def key_blocks(b):
                pool.wait_ge(s0_mm, 2 * QUARTERS * b)
                for c in range(DC):
                    pool.tensor_tensor(
                        kblk[:, c], kT0[:, c, bass.ds(b * S2, S2)].unsqueeze(1).to_broadcast([P, NHC, S2]),
                        blockmask[:, :].unsqueeze(2).to_broadcast([P, NHC, S2]), ALU.mult).then_inc(kblk_done, 1)

            def rstd_of(n, eps):
                pool.wait_ge(ln_mv, n + 1)
                pool.tensor_tensor(ve[:], mv[:, 1:2], eps, ALU.add).then_inc(ln_eps, 1)
                pool.wait_ge(ln_eps, n + 1)
                pool.tensor_tensor(rstd[:], ve[:], expo[:], ALU.pow).then_inc(ln_rstd, 1)

            def batch_rstd(k):
                n = BATCHES[k][1]
                pool.wait_ge(m_mv, BATCH_END[k])
                pool.tensor_tensor(ve4[:, 0:n], mv4[:, 0:n, 1:2].rearrange("p j a -> p (j a)"),
                                   eps1[:].to_broadcast([P, n]), ALU.add).then_inc(m_eps, 1)
                pool.wait_ge(m_eps, k + 1)
                pool.tensor_tensor(rstd4[:, 0:n], ve4[:, 0:n], expo[:].to_broadcast([P, n]), ALU.pow)\
                    .then_inc(m_rstd, 1)

            def x_plus_bo(i):
                at = X[:, bass.ds(i, 1), :].rearrange("p a d -> p (a d)")
                pool.tensor_tensor(at, at, rows[:, 0:D], ALU.add).then_inc(xbo_done, 1)

            def gamma_beta(i):
                pool.wait_ge(ln_done, i + 1)
                pool.tensor_tensor(z1[:], z0[:], rows[:, D:2 * D], ALU.mult).then_inc(z1_done, 1)
                pool.wait_ge(z1_done, i + 1)
                pool.tensor_tensor(pool_carrier[:], ones[:, 0:1], ones[:, 0:1], ALU.mult)
                pool.tensor_tensor(X[:, bass.ds(i, 1), :].rearrange("p a d -> p (a d)"), z1[:], rows[:, 2 * D:3 * D],
                                   ALU.add).then_inc(x1_done, 1)

            def low_parts(h, w, layer=0):
                pool.wait_ge(w_hi, 2 * h + 2)
                n = W_COL if layer == 0 else W_POOL
                pool.tensor_tensor(wl[w][:, 0:n], ring[w][:, 0:n], wh[layer][w][:, 0:n].bitcast(F32), ALU.subtract)\
                    .then_inc(w_lo, 1)
                pool.tensor_tensor(cols_lo[w][:], ring[w][:, W_COL:W_N], cols_hi[w][:].bitcast(F32),
                                   ALU.subtract).then_inc(w_lo, 1)

            def head_columns(h, w):
                pool.wait_ge(w_lo, 2 * h + 2)
                if some(h):
                    pool.wait_ge(ac_mm, 3 * h)
                for k_to, bq_to, part in ((kTh, bqh[:], cols_hi[w]), (kTl, bql, cols_lo[w])):
                    pool.tensor_tensor(k_to[:, CK:CK + 1], ones[:, 0:1], part[:, 2:3].bitcast(F32), ALU.mult)\
                        .then_inc(headcols, 1)
                    pool.tensor_tensor(bq_to, ones[:], part[:, 1:2].bitcast(F32).to_broadcast([P, P]), ALU.mult)\
                        .then_inc(headcols, 1)

            def pair0(b, first=False, last=False):
                for p in range(2):
                    i = 2 * b + p
                    w1, w2 = 2 * p, 2 * p + 1
                    head_columns(SLOTS * b + w1, w1)
                    if last and p == 1:
                        batch_rstd(0)
                    low_parts(SLOTS * b + w2, w2)
                    if not (first and p == 0):
                        rstd_of(i - 1, eps0[:])
                    head_columns(SLOTS * b + w2, w2)
                    if not (last and p == 1):
                        low_parts(SLOTS * b + w2 + 1, (w2 + 1) % SLOTS)
                    if p == 0 and not last:
                        key_blocks(b + 1)
                    if first and p == 0:
                        pool.wait_ge(x_in, 16)
                        pool.wait_ge(rows_in, 16 * 4)
                    x_plus_bo(i)
                    if not (first and p == 0):
                        gamma_beta(i - 1)

            low_parts(0, 0)
            for c in range(DC):
                pool.wait_ge(ctx_hi, c + 1)
                pool.wait_ge(v0_mm, 1)
                pool.tensor_tensor(ctxl[:, c], ctxT[:, c], ctxh[:, c].bitcast(F32), ALU.subtract).then_inc(ctx_lo, 1)
            pool.wait_ge(const_in, 32)
            pool.wait_ge(kT0_out, DC)
            pair0(0, first=True)
            with pool.Fori(1, B - 1) as b:
                pair0(b)
            pair0(B - 1, last=True)
            rstd_of(TILES - 1, eps0[:])
            gamma_beta(TILES - 1)
            with pool.Fori(2, TILES + 1) as n:
                rstd_of(ln_of1(n), eps1[:])
            low_parts(H, 0, 1)
            head_columns(H, 0)
            rstd_of(ln_of1(TILES + 1), eps1[:])
            low_parts(H + 1, 1, 1)
            with pool.Fori(SLOTS, LAYERS * SLOTS - 1) as r:
                for w in range(SLOTS):
                    head_columns(r * SLOTS + w + 1, (w + 1) % SLOTS)
                    low_parts(r * SLOTS + w + 2, (w + 2) % SLOTS, 1)
            for w in range(1, SLOTS):
                head_columns(LAYERS * H - SLOTS + w, w)
                if w + 1 < SLOTS:
                    low_parts(LAYERS * H - SLOTS + w + 1, w + 1, 1)
            for n in range(TILES + 2, TILES + 6):
                rstd_of(ln_of1(n), eps1[:])
                q = n - TILES - 2
                pool.wait_ge(fc_hi, q + 1)
                low, w, high = fc_quarter(q)
                pool.tensor_tensor(low, w, high.bitcast(F32), ALU.subtract).then_inc(fc_lo, 1)
            for n in range(TILES + 6, LAYERS * TILES):
                rstd_of(ln_of1(n), eps1[:])

            def hTm_low(i):
                pool.wait_ge(hTm_hi, i + 1)
                at = slice(i * P, (i + 1) * P)
                pool.tensor_tensor(hTml[:, :, at], hTm[i % 2], hTmh[:, :, at].bitcast(F32), ALU.subtract)\
                    .then_inc(hTm_lo, 1)

            def x_plus_b2(i):
                pool.tensor_tensor(X[:, i, :], X[:, i, :], rows[:, 3 * D:4 * D], ALU.add).then_inc(xb2_done, 1)

            for half in range(TILES // HALF):
                batch_rstd(half + 1)
                for i in range(half * HALF, (half + 1) * HALF):
                    hTm_low(i)
                pool.wait_ge(m_done, BATCH_END[half + 1])
                for i in range(half * HALF, (half + 1) * HALF):
                    x_plus_b2(i)

        @block.scalar
        def _(act):
            act.dma_start(cols0[:], cols0_d).then_inc(const_in, 16)
            act.dma_start(blockmask[:], blockmask_d).then_inc(const_in, 16)
            act.dma_start(xT[:, :, 0:S], xT_d[:, :, 0:S]).then_inc(xt0_in, 16)
            for c in range(DC):
                act.wait_ge(ctx_in, 16)
                nc.scalar.copy(ctxh[:, c], ctxT[:, c]).then_inc(ctx_hi, 1)
            act.wait_ge(const_in, 32)
            nc.scalar.mul(bq_s[:], cols0[:, 0:DC], SCALE0).then_inc(bqs_done, 1)
            for c in range(DC):
                act.wait_ge(kT0_mm, c + 1)
                nc.scalar.activation(kT0[:, c], s_banks[:, c, 0:CK], ACT.Identity,
                                     bias=cols0[:, DC + c:DC + c + 1]).then_inc(kT0_out, 1)

            def q_out(b):
                if some(b):
                    act.wait_ge(s0_mm, 2 * QUARTERS * b)
                act.wait_ge(q0_mm, DC * b + DC)
                for c in range(DC):
                    nc.scalar.activation(qT0[:, c], q0_ps[c], ACT.Identity, bias=bq_s[:, c:c + 1],
                                         scale=SCALE0).then_inc(q0_out, 1)

            def exp0(i, p):
                act.wait_ge(sub0_done, i + 1)
                nc.scalar.activation(sc0[p], sc0[p], ACT.Exp).then_inc(exp0_done, 1)

            def pT0_copy(i, g):
                act.wait_ge(pT0_mm, 4 * i + g + 1)
                if g == 0 and some(i):
                    act.wait_ge(pv0_mm, i)
                nc.scalar.copy(pT0[:, 4 * g:4 * g + 4], pT0_ps.rearrange("p (j t) -> p j t", j=4))\
                    .then_inc(pT0_out, 1)

            def oT0_copy(i):
                act.wait_ge(oT0_mm, i + 1)
                nc.scalar.copy(oT0[:], oT0_ps.rearrange("p (c t) -> p c t", c=DC)).then_inc(oT0_out, 1)

            def high_parts(h, w, layer=0):
                act.wait_ge(w_in[w], (h - w) * 4 + 16)
                if layer == 0 and not (isinstance(h, int) and h < 2):
                    act.wait_ge(vw_mm, h - 1)
                nc.scalar.copy(wh[layer][w][:], ring[w][:, 0:W_COL]).then_inc(w_hi, 1)
                nc.scalar.copy(cols_hi[w][:], ring[w][:, W_COL:W_N]).then_inc(w_hi, 1)

            def kT_copy(h, w, layer=0):
                act.wait_ge(kT_mm, h + 1)
                if some(h):
                    act.wait_ge(ac_mm, 3 * h)
                nc.scalar.activation(kTh[:, 0:CK], kT_ps[layer], ACT.Identity,
                                     bias=ring[w][:, W_COL:W_COL + 1]).then_inc(kTh_out, 1)

            def vT_copy(h, w, layer):
                act.wait_ge(vT_mm, h + 1)
                if some(h):
                    act.wait_ge(vw_mm, h)
                nc.scalar.activation(vTh[:], vT_ps[layer], ACT.Identity, bias=ring[w][:, W_COL + 3:W_COL + 4])\
                    .then_inc(vTh_out, 1)

            def bqk_copy(h, hh, w, layer=0):
                act.wait_ge(ac_mm, 3 * h + DC + 1)
                ps = ac_ps(layer, w, DC)
                nc.scalar.copy(AC[:, DC, :, hh, :].rearrange("p b a t -> p b (a t)"),
                               ps[:, 0:CK].rearrange("p (b t) -> p b t", b=B)).then_inc(bqk_out, 1)
                nc.scalar.copy(ACb[:, DC, hh], ps[:, CK:CK + 1]).then_inc(bqk_out, 1)

            def vw_odd(h, hp, w):
                act.wait_ge(vw_mm, h + 1)
                rows_to = slice(S2 * (w % 2), S2 * (w % 2) + S2)
                nc.scalar.copy(VW[rows_to, 1::2, hp, :], vw_ps[S2:P]).then_inc(vw_out_act, 1)

            def hT_out_of(ps, n, p, layer):
                at = 4 * layer
                for c in range(DC):
                    nc.scalar.activation(hT[p][:, c], ps[:, c * P:(c + 1) * P], ACT.Identity,
                                         bias=ln_all[:, at + DC + c:at + DC + c + 1],
                                         scale=ln_all[:, at + c:at + c + 1]).then_inc(hT_out, 1)

            def tile0(b, p, first=False, last=False):
                i = 2 * b + p
                w1, w2 = 2 * p, 2 * p + 1
                h1, h2 = SLOTS * b + w1, SLOTS * b + w2
                hp = 2 * b + p
                if not (first and p == 0):
                    kT_copy(h1, w1)
                if not (first and p == 0):
                    oT0_copy(i - 1)
                vT_copy(h1, w1, 0)
                high_parts(h2, w2)
                bqk_copy(h1, bass.ds(h1, 1), w1)
                pT0_copy(i, 0)
                vw_odd(h1, hp, w1)
                pT0_copy(i, 1)
                if not (last and p == 1):
                    high_parts(h2 + 1, (w2 + 1) % SLOTS)
                kT_copy(h2, w2)
                pT0_copy(i, 2)
                vT_copy(h2, w2, 0)
                pT0_copy(i, 3)
                if p == 0 and not last:
                    q_out(b + 1)
                if p == 1 and last:
                    act.wait_ge(ln_in, 16)
                    act.wait_ge(hT_mm, 2)
                    for n in range(2):
                        hT_out_of(first_hT_ps[n], n, n, 0)
                    bqk_copy(h2, bass.ds(h2, 1), w2)
                else:
                    exp0(i + 1, 1 - p)
                    bqk_copy(h2, bass.ds(h2, 1), w2)
                    vw_odd(h2, hp, w2)

            act.wait_ge(bqs_done, 1)
            high_parts(0, 0)
            q_out(0)
            kT_copy(0, 0)
            exp0(0, 0)
            tile0(0, 0, first=True)
            tile0(0, 1, first=True)
            with act.Fori(1, B - 1) as b:
                tile0(b, 0)
                tile0(b, 1)
            tile0(B - 1, 0, last=True)
            tile0(B - 1, 1, last=True)

            def hT_copies(n, p, layer):
                act.wait_ge(hT_mm, n + 1)
                act.wait_ge(s_mm, n - 1)
                hT_out_of(hT_ps, n, p, layer)

            def exp1(n):
                act.wait_ge(sub_done, n + 1)
                nc.scalar.activation(px[:], sx[:], ACT.Exp, scale=SCALE1).then_inc(exp_done, 1)

            def pT_copies(n):
                for g in range(2):
                    act.wait_ge(pT_mm, 3 * n + g + 1)
                    if g == 0 and some(n):
                        act.wait_ge(o_mm, n)
                    nc.scalar.copy(pT[:, 4 * g:4 * g + 4], pT_ps[g][:, :].rearrange("p (j t) -> p j t", j=4))\
                        .then_inc(pT_out, 1)
                act.wait_ge(pT_mm, 3 * n + 3)
                nc.scalar.copy(pTb[:], pTb_ps).then_inc(pT_out, 1)

            def hTm_copies(i):
                act.wait_ge(hTm_mm, i + 2)
                at = 4 * LAYERS
                for t in range(i, i + 2):
                    if t >= 2:
                        act.wait_ge(hTm_lo, t - 1)
                    for c in range(DC):
                        nc.scalar.activation(hTm[t % 2][:, c], hTm_ps[t][:, c * P:(c + 1) * P],
                                             ACT.Identity, bias=ln_all[:, at + DC + c:at + DC + c + 1],
                                             scale=ln_all[:, at + c:at + c + 1]).then_inc(hTm_out, 1)
                    act.wait_ge(hTm_out, DC * (t + 1))
                    nc.scalar.copy(hTmh[:, :, t * P:(t + 1) * P], hTm[t % 2]).then_inc(hTm_hi, 1)

            def fc_high(q):
                act.wait_ge(mlp_in, 48)
                low, w, high = fc_quarter(q)
                nc.scalar.copy(high, w).then_inc(fc_hi, 1)

            def attention(layer):
                def pair(n, first=False, last=False):
                    for p in range(2):
                        if last and p == 0 and layer + 1 < LAYERS:
                            high_parts((layer + 1) * H, 0, layer + 1)
                        if last and p == 1 and layer + 1 < LAYERS:
                            kT_copy((layer + 1) * H, 0, layer + 1)
                            high_parts((layer + 1) * H + 1, 1, layer + 1)
                        if first and p == 0:
                            act.wait_ge(half_sub, layer + 1)
                            nc.scalar.activation(px[:, 0:HP], sx[:, 0:HP], ACT.Exp, scale=SCALE1).then_inc(half_exp, 1)
                            act.wait_ge(sub_done, n + 1)
                            nc.scalar.activation(px[:, HP:], sx[:, HP:], ACT.Exp, scale=SCALE1).then_inc(exp_done, 1)
                        else:
                            exp1(n + p)
                        if last and p == 0 and layer + 1 == LAYERS:
                            hTm_copies(0)
                        pT_copies(n + p)
                        if not last:
                            hT_copies(n + p + 2, p, layer)
                            if first and layer + 1 == LAYERS:
                                fc_high(2 * p)
                                fc_high(2 * p + 1)
                        elif layer + 1 < LAYERS:
                            hT_copies(n + p + 2, p, layer + 1)
                        elif p == 0:
                            hTm_copies(2)

                n0 = layer * TILES
                if layer == 0:
                    oT0_copy(TILES - 1)
                vw_odd((layer + 1) * H - 1, HP - 1, SLOTS - 1)
                pair(n0, first=True)
                with act.Fori(1, B - 1) as b:
                    pair(b * 2 + n0)
                pair(n0 + TILES - 2, last=True)

            attention(0)

            def round1(r, last=False):
                for w in range(SLOTS):
                    h, at = r * SLOTS + w, (r - SLOTS) * SLOTS + w
                    if not (last and w >= SLOTS - 2):
                        high_parts(h + 2, (w + 2) % SLOTS, 1)
                    bqk_copy(h, bass.ds(at, 1), w, 1)
                    if not (last and w == SLOTS - 1):
                        kT_copy(h + 1, (w + 1) % SLOTS, 1)
                        vw_odd(h, (r - SLOTS) * 2 + w // 2, w)
                        vT_copy(h + 1, (w + 1) % SLOTS, 1)

            vT_copy(H, 0, 1)
            with act.Fori(SLOTS, LAYERS * SLOTS - 1) as r:
                round1(r)
            round1(LAYERS * SLOTS - 1, last=True)
            attention(1)

            for half in range(TILES // HALF):
                for f in range(FC):
                    k = half * FC + f
                    act.wait_ge(g_mm, k + 1)
                    if k >= GELUS:
                        act.wait_ge(g_lo, k - GELUS + 1)
                    nc.scalar.activation(gelu[:, k % GELUS], g_ps[f % 2], ACT.Gelu, bias=bfc1[:, f:f + 1])\
                        .then_inc(g_out, 1)
                    if half == 0 and f >= 6:
                        hTm_copies(2 * f - 8)

        @block.vector
        def _(dve):
            dve.wait_ge(w0_in, 16)
            for c in range(DC):
                nc.vector.tensor_copy(
                    wk_rep[:, c].rearrange("p (k g d) -> p k g d", k=KVH, g=G),
                    w0[:, c, D:D + KVH * HD].rearrange("p (k d) -> p k d", k=KVH).unsqueeze(2)
                    .to_broadcast([P, KVH, G, HD])).then_inc(wkrep_done, 1)
            dve.wait_ge(const_in, 32)
            for c in range(DC):
                dve.wait_ge(kT0_out, c + 1)
                nc.vector.tensor_tensor(
                    kblk[:, c], kT0[:, c, 0:S2].unsqueeze(1).to_broadcast([P, NHC, S2]),
                    blockmask[:, :].unsqueeze(2).to_broadcast([P, NHC, S2]), ALU.mult).then_inc(kblk_done, 1)
            def tile_of(i):
                return X[:, bass.ds(i, 1), :].rearrange("p a d -> p (a d)")

            def ln_moments(x, n):
                if some(n):
                    dve.wait_ge(ln_done, n)
                nc.vector.bn_stats(stats[:], x).then_inc(ln_stats, 1)
                dve.wait_ge(ln_stats, n + 1)
                nc.vector.tensor_copy(carrier[:], stats[:, 0:1])
                nc.vector.bn_aggr(mv[:], stats[:]).then_inc(ln_mv, 1)

            def ln_normal(out, x, n):
                dve.wait_ge(ln_rstd, n + 1)
                nc.vector.tensor_scalar(out, x, mv[:, 0:1], rstd[:], ALU.subtract, ALU.mult).then_inc(ln_done, 1)

            def batch_moments(k):
                first, n = BATCHES[k]
                done = BATCH_END[k] - n
                if k:
                    dve.wait_ge(m_mv, done)
                for j in range(n):
                    nc.vector.bn_stats(stats4[:, j, :], tile_of(first + j)).then_inc(m_stats, 1)
                if k:
                    dve.wait_ge(m_done, done)
                for j in range(n):
                    dve.wait_ge(m_stats, done + j + 1)
                    nc.vector.bn_aggr(mv4[:, j, :], stats4[:, j, :]).then_inc(m_mv, 1)

            def batch_normal(k):
                first, n = BATCHES[k]
                dve.wait_ge(m_rstd, k + 1)
                for j in range(n):
                    if k == 1:
                        dve.wait_ge(hT_mm, LAYERS * TILES)
                    elif k == 2:
                        dve.wait_ge(hTm_mm, j + 1)
                    nc.vector.tensor_scalar(xn[j][:], tile_of(first + j), mv4[:, j, 0:1], rstd4[:, j:j + 1],
                                            ALU.subtract, ALU.mult).then_inc(m_done, 1)

            dve.wait_ge(mask_in, 16)

            def masked0(i, p, q):
                if q == 0 and not (isinstance(i, int) and i < 2):
                    dve.wait_ge(pT0_mm, 4 * i - 4)
                dve.wait_ge(s0_mm, QUARTERS * i + q + 1)
                nc.vector.tensor_tensor(
                    sc0[p][:, q * QH * S2:(q + 1) * QH * S2].rearrange("p (h t) -> p h t", t=S2),
                    s0_ps.rearrange("p (j t) -> p j t", t=S2),
                    mask[:, bass.ds(i, 1), :].to_broadcast([P, QH, S2]), ALU.add).then_inc(sc0_done, 1)

            def max0(i, p):
                dve.wait_ge(sc0_done, QUARTERS * i + QUARTERS)
                nc.vector.tensor_reduce(mx0[:], sc0[p].rearrange("p (h t) -> p h t", t=S2), AX_X, ALU.max)\
                    .then_inc(mx0_done, 1)

            def sub0(i, p):
                dve.wait_ge(mx0_done, i + 1)
                nc.vector.tensor_tensor(
                    sc0[p].rearrange("p (h t) -> p h t", t=S2), sc0[p].rearrange("p (h t) -> p h t", t=S2),
                    mx0[:].unsqueeze(2).to_broadcast([P, NH, S2]), ALU.subtract).then_inc(sub0_done, 1)

            def out0(i, p):
                dve.wait_ge(pv0_mm, i + 1)
                o = o0_ps.rearrange("p (h e) -> p h e", e=VO)
                nc.vector.reciprocal(rden0[:].unsqueeze(2), o[:, :, HD:VO]).then_inc(rden0_done, 1)
                dve.wait_ge(rden0_done, i + 1)
                nc.vector.tensor_tensor(o0[p][:].rearrange("p (h d) -> p h d", d=HD), o[:, :, 0:HD],
                                        rden0[:].unsqueeze(2).to_broadcast([P, NH, HD]), ALU.mult)\
                    .then_inc(o0_done, 1)

            def residual0(i):
                dve.wait_ge(wo0_mm, i + 1)
                if some(i):
                    dve.wait_ge(ln_done, i)
                dve.wait_ge(xbo_done, i + 1)
                nc.vector.tensor_tensor(y0[:], wo0_ps, tile_of(i), ALU.add).then_inc(y0_done, 1)
                dve.wait_ge(y0_done, i + 1)
                ln_moments(y0[:], i)

            def normal0(i):
                if some(i):
                    dve.wait_ge(z1_done, i)
                ln_normal(z0[:], y0[:], i)

            def ac_copy(h, hh, w, j, layer=0):
                dve.wait_ge(ac_mm, 3 * h + j + 1)
                ps = ac_ps(layer, w, j)
                nc.vector.tensor_copy(AC[:, j, :, hh, :].rearrange("p b a t -> p b (a t)"),
                                      ps[:, 0:CK].rearrange("p (b t) -> p b t", b=B)).then_inc(ac_out, 1)
                nc.vector.tensor_copy(ACb[:, j, hh], ps[:, CK:CK + 1]).then_inc(ac_out, 1)

            def kT_low(h, w, layer=0):
                dve.wait_ge(kTh_out, h + 1)
                nc.vector.scalar_tensor_tensor(kTl[:, 0:CK], kT_ps[layer], ring[w][:, W_COL:W_COL + 1],
                                               kTh[:, 0:CK].bitcast(F32), ALU.add, ALU.subtract).then_inc(kT_out, 1)

            def vT_low(h, w, layer=0):
                dve.wait_ge(vTh_out, h + 1)
                nc.vector.scalar_tensor_tensor(vTl, vT_ps[layer], ring[w][:, W_COL + 3:W_COL + 4],
                                               vTh[:].bitcast(F32), ALU.add, ALU.subtract).then_inc(vT_out, 1)

            def low_parts(h, w):
                dve.wait_ge(w_hi, 2 * h + 1)
                nc.vector.tensor_tensor(wl[w][:, W_POOL:], ring[w][:, W_POOL:W_COL],
                                        wh[1][w][:, W_POOL:].bitcast(F32), ALU.subtract).then_inc(w_lo_dve, 1)

            def vwb_add(h, layer):
                dve.wait_ge(vwb_mm, h + 1)
                if some(h):
                    dve.wait_ge(vwb_out, h)
                nc.vector.tensor_tensor(VWb[0:H, :], VWb[0:H, :], vwb_ps[layer], ALU.add).then_inc(vwb_out, 1)

            def vw_even(h, hp, w):
                dve.wait_ge(vw_mm, h + 1)
                rows_to = slice(S2 * (w % 2), S2 * (w % 2) + S2)
                nc.vector.tensor_copy(VW[rows_to, 0::2, bass.ds(hp, 1), :].rearrange("p b a d -> p b (a d)"),
                                      vw_ps[0:S2]).then_inc(vw_out_dve, 1)

            def tile0(b, p, first=False, last=False):
                i = 2 * b + p
                w1, w2 = 2 * p, 2 * p + 1
                h1, h2 = SLOTS * b + w1, SLOTS * b + w2
                hh1, hh2 = bass.ds(SLOTS * b + w1, 1), bass.ds(SLOTS * b + w2, 1)
                hp = 2 * b + p
                next_tile = not (last and p == 1)
                if next_tile and not (first and p == 0):
                    masked0(i + 1, 1 - p, 0)
                if not (first and p == 0):
                    kT_low(h1, w1)
                if not next_tile:
                    dve.wait_ge(x1_done, 2)
                    batch_moments(0)
                if next_tile:
                    masked0(i + 1, 1 - p, 1)
                vT_low(h1, w1)
                ac_copy(h1, hh1, w1, 0)
                if next_tile:
                    masked0(i + 1, 1 - p, 2)
                ac_copy(h1, hh1, w1, 1)
                if not (first and p == 0):
                    residual0(i - 1)
                if next_tile:
                    masked0(i + 1, 1 - p, 3)
                vwb_add(h1, 0)
                if next_tile:
                    max0(i + 1, 1 - p)
                vw_even(h1, hp, w1)
                if not next_tile:
                    batch_normal(0)
                kT_low(h2, w2)
                if next_tile:
                    sub0(i + 1, 1 - p)
                vT_low(h2, w2)
                if not (first and p == 0):
                    normal0(i - 1)
                ac_copy(h2, hh2, w2, 0)
                out0(i, p)
                ac_copy(h2, hh2, w2, 1)
                if next_tile:
                    vwb_add(h2, 0)
                    vw_even(h2, hp, w2)

            for q in range(QUARTERS):
                masked0(0, 0, q)
            max0(0, 0)
            masked0(1, 1, 0)
            kT_low(0, 0)
            sub0(0, 0)
            dve.wait_ge(fills, N_FILLS)
            dve.wait_ge(bv_in, 16)
            dve.wait_ge(v0_mm, 1)
            v_ps = s_banks[:, 2, 0:B * KVH * HD].rearrange("p (b k d) -> p b k d", b=B, k=KVH)
            bv = rows[:, 4 * D:].rearrange("p (k d) -> p k d", k=KVH).unsqueeze(1).to_broadcast([P, B, KVH, HD])
            for half in range(2):
                part = slice(S2 * half, S2 * half + S2)
                nc.vector.tensor_tensor(vblk[part, :, :, VO * half:VO * half + HD], v_ps[part], bv[part], ALU.add)\
                    .then_inc(v0_out, 1)
            tile0(0, 0, first=True)
            tile0(0, 1, first=True)
            with dve.Fori(1, B - 1) as b:
                tile0(b, 0)
                tile0(b, 1)
            tile0(B - 1, 0, last=True)
            tile0(B - 1, 1, last=True)

            def scores_out(n, b):
                dve.wait_ge(s_mm, n + 1)
                nc.vector.tensor_tensor(
                    sx[:, :, 0:S2], sx_ps.rearrange("p r (j t) -> p (r j) t", t=S2),
                    AC[:, DC, bass.ds(b, 1)].rearrange("p a h t -> p (a h) t"), ALU.add).then_inc(sx_done, 1)
                nc.vector.tensor_tensor(sx[:, :, S2:KEYS], sxb_ps.unsqueeze(2), ACb[:, DC, :].unsqueeze(2), ALU.add)\
                    .then_inc(sx_done, 1)
                dve.wait_ge(sx_done, 2 * n + 2)
                nc.vector.tensor_reduce(mx[:], sx[:], AX_X, ALU.max).then_inc(mx_done, 1)
                dve.wait_ge(mx_done, n + 1)
                nc.vector.tensor_tensor(sx[:], sx[:], mx[:].unsqueeze(2).to_broadcast([P, H, KEYS]), ALU.subtract)\
                    .then_inc(sub_done, 1)

            def sums(n):
                dve.wait_ge(exp_done, n + 1)
                nc.vector.tensor_reduce(sm[:], px[:], AX_X, ALU.add).then_inc(sm_done, 1)
                dve.wait_ge(sm_done, n + 1)
                nc.vector.reciprocal(rs[:], sm[:]).then_inc(rs_done, 1)

            def weights(n):
                dve.wait_ge(rs_done, n + 1)
                if some(n):
                    dve.wait_ge(pT_mm, 3 * n)
                nc.vector.tensor_tensor(pm[:], px[:, :, 0:S2], rs[:].unsqueeze(2).to_broadcast([P, H, S2]),
                                        ALU.mult).then_inc(pm_done, 1)
                nc.vector.tensor_tensor(pmb[:, 0:H].unsqueeze(2), px[:, :, S2:KEYS], rs[:].unsqueeze(2), ALU.mult)\
                    .then_inc(pm_done, 1)

            def first_tile(layer):
                n = layer * TILES
                h0, h1 = slice(0, HP), slice(HP, H)

                def add_bqk(h, half, done):
                    nc.vector.tensor_tensor(sx[:, h, 0:S2], sx_ps[:, half].rearrange("p (j t) -> p j t", t=S2),
                                            AC[:, DC, 0, h, :], ALU.add).then_inc(done, 1)

                def maximum(h, done):
                    nc.vector.tensor_reduce(mx[:, h], sx[:, h, :], AX_X, ALU.max).then_inc(done, 1)

                def subtract(h, done):
                    nc.vector.tensor_tensor(sx[:, h, :], sx[:, h, :], mx[:, h].unsqueeze(2).to_broadcast([P, HP, KEYS]),
                                            ALU.subtract).then_inc(done, 1)

                def total(h, done):
                    nc.vector.tensor_reduce(sm[:, h], px[:, h, :], AX_X, ALU.add).then_inc(done, 1)

                def divide(h, done):
                    nc.vector.tensor_tensor(pm[:, h, :], px[:, h, 0:S2], rs[:, h].unsqueeze(2)
                                            .to_broadcast([P, HP, S2]), ALU.mult).then_inc(done, 1)
                    nc.vector.tensor_tensor(pmb[:, h].unsqueeze(2), px[:, h, S2:KEYS], rs[:, h].unsqueeze(2), ALU.mult)\
                        .then_inc(done, 1)

                dve.wait_ge(bqk_out, (layer + 1) * H * 2)
                dve.wait_ge(half_mm, layer + 1)
                nc.vector.tensor_tensor(sx[:, :, S2:KEYS], sxb_ps.unsqueeze(2), ACb[:, DC, :].unsqueeze(2), ALU.add)\
                    .then_inc(sx_done, 1)
                add_bqk(h0, 0, half_sx)
                dve.wait_ge(sx_done, 2 * n + 1)
                dve.wait_ge(half_sx, layer + 1)
                maximum(h0, half_mx)
                dve.wait_ge(s_mm, n + 1)
                add_bqk(h1, 1, sx_done)
                dve.wait_ge(half_mx, layer + 1)
                subtract(h0, half_sub)
                dve.wait_ge(sx_done, 2 * n + 2)
                maximum(h1, mx_done)
                dve.wait_ge(mx_done, n + 1)
                subtract(h1, sub_done)
                if layer == 0:
                    vwb_add((layer + 1) * H - 1, layer)
                vw_even((layer + 1) * H - 1, HP - 1, SLOTS - 1)
                if layer == 0:
                    residual0(TILES - 1)
                dve.wait_ge(half_exp, layer + 1)
                total(h0, half_sm)
                dve.wait_ge(half_sm, layer + 1)
                nc.vector.reciprocal(rs[:, h0], sm[:, h0]).then_inc(half_rs, 1)
                if some(n):
                    dve.wait_ge(pT_mm, 3 * n)
                dve.wait_ge(half_rs, layer + 1)
                divide(h0, half_pm)
                if layer == 0:
                    normal0(TILES - 1)
                ln_moments(tile_of(2), ln_of1(n + 2))
                dve.wait_ge(exp_done, n + 1)
                total(h1, sm_done)
                dve.wait_ge(sm_done, n + 1)
                nc.vector.reciprocal(rs[:, h1], sm[:, h1]).then_inc(rs_done, 1)
                dve.wait_ge(rs_done, n + 1)
                divide(h1, pm_done)

            def x_add(n, i):
                dve.wait_ge(o_mm, n + 1)
                nc.vector.tensor_tensor(tile_of(i), tile_of(i), o_ps, ALU.add).then_inc(x_done, 1)

            def attention(layer):
                n0 = layer * TILES
                heads = layer * H + H

                def pair(b, first=False, last=False):
                    for p in range(2):
                        i = 2 * b + p
                        n = n0 + i
                        mlp = last and layer + 1 == LAYERS
                        ahead = p if last else i + 2
                        if first and p == 0:
                            first_tile(layer)
                            dve.wait_ge(hT_mm, n + 1)
                            ln_normal(xn[0][:], tile_of(2), ln_of1(n + 2))
                            continue
                        if mlp and p == 0:
                            batch_moments(1)
                        scores_out(n, b)
                        if layer == 0 and first and p == 1:
                            dve.wait_ge(x1_done, TILES)
                        if mlp and p == 0:
                            batch_normal(1)
                        if not mlp:
                            ln_moments(tile_of(ahead), ln_of1(n + 2))
                        if last and p == 1 and not mlp:
                            kT_low(heads, 0, layer + 1)
                        sums(n)
                        if not mlp:
                            dve.wait_ge(hT_mm, n + 1)
                            ln_normal(xn[p][:], tile_of(ahead), ln_of1(n + 2))
                        weights(n)
                        if last and p == 1 and not mlp:
                            low_parts(heads, 0)
                            low_parts(heads + 1, 1)
                            for j in range(DC):
                                ac_copy(heads, slice(0, 1), 0, j, layer + 1)
                        x_add(n - 1, i - 1)
                pair(0, first=True)
                with dve.Fori(1, B - 1) as b:
                    pair(b)
                pair(B - 1, last=True)
                if layer + 1 < LAYERS:
                    x_add(n0 + TILES - 1, TILES - 1)

            attention(0)
            dve.wait_ge(x_done, TILES)
            nc.vector.memset(VWb[0:H, :], 0.0).then_inc(vwb_zero, 1)
            dve.wait_ge(vwb_zero, 1)

            def round1(r, last=False):
                for w in range(SLOTS):
                    h, at = r * SLOTS + w, (r - SLOTS) * SLOTS + w
                    if not (last and w >= SLOTS - 2):
                        low_parts(h + 2, (w + 2) % SLOTS)
                    if not (last and w == SLOTS - 1):
                        kT_low(h + 1, (w + 1) % SLOTS, 1)
                    vwb_add(h, 1)
                    if not (last and w == SLOTS - 1):
                        vw_even(h, (r - SLOTS) * 2 + w // 2, w)
                        ac_copy(h + 1, bass.ds(at + 1, 1), (w + 1) % SLOTS, 0, 1)
                        vT_low(h + 1, (w + 1) % SLOTS, 1)
                        ac_copy(h + 1, bass.ds(at + 1, 1), (w + 1) % SLOTS, 1, 1)

            vT_low(H, 0, 1)
            with dve.Fori(SLOTS, LAYERS * SLOTS - 1) as r:
                round1(r)
            round1(LAYERS * SLOTS - 1, last=True)
            attention(1)

            def gelu_parts(k):
                f = k % FC
                dve.wait_ge(g_out, k + 1)
                if k == FC:
                    dve.wait_ge(y_mm, HALF)
                nc.vector.tensor_copy(gTh[:, f], gelu[:, k % GELUS]).then_inc(g_hi, 1)
                dve.wait_ge(g_hi, k + 1)
                nc.vector.tensor_tensor(gTl[:, f], gelu[:, k % GELUS], gTh[:, f].bitcast(F32), ALU.subtract)\
                    .then_inc(g_lo, 1)

            def y_out(i):
                dve.wait_ge(xb2_done, i + 1)
                dve.wait_ge(y_mm, i + 1)
                nc.vector.tensor_tensor(tile_of(i), tile_of(i), y_ps[i % 2], ALU.add).then_inc(y_done, 1)

            gelu_parts(0)
            gelu_parts(1)
            x_add(LAYERS * TILES - 1, TILES - 1)
            dve.wait_ge(x_done, LAYERS * TILES)
            batch_moments(2)
            gelu_parts(2)
            batch_normal(2)
            for f in range(3, FC):
                gelu_parts(f)
            for i in range(HALF):
                y_out(i)
            for f in range(FC):
                gelu_parts(FC + f)
            for i in range(HALF, TILES):
                y_out(i)

        @block.tensor
        def _(pe):
            def mm(out, lhsT, rhs, k=0, n=1, **kw):
                return nc.tensor.matmul(out, lhsT, rhs, start=(k == 0), stop=(k == n - 1), **kw)

            def mm3(out, lhsT, rhs, k=0, n=1, **kw):
                (ah, al), (bh, bl) = lhsT, rhs
                nc.tensor.matmul(out, ah, bh, start=(k == 0), stop=False, **kw)
                nc.tensor.matmul(out, al, bh, start=False, stop=False, **kw)
                return nc.tensor.matmul(out, ah, bl, start=False, stop=(k == n - 1), **kw)

            pe.wait_ge(fills, 1)
            for _ in range(WARM_UPS):
                mm(bank7[:, 0:P], ones[:], ones[:])

            pe.wait_ge(ctx_in, 16)
            pe.wait_ge(w0_in, 16)
            pe.wait_ge(wkrep_done, DC)
            for m in range(DC):
                for c in range(DC):
                    last = mm(s_banks[:, m, 0:CK], wk_rep[:, c, m * P:(m + 1) * P], ctxT[:, c], c, DC)
                last.then_inc(kT0_mm, 1)

            def q0(b, i=None):
                if i is None:
                    pe.wait_ge(xt0_in, 16)
                else:
                    pe.wait_ge(xt_in, 16)
                    if some(i):
                        pe.wait_ge(y0_done, i)
                for m in range(DC):
                    for c in range(DC):
                        last = mm(q0_ps[m], w0[:, c, m * P:(m + 1) * P], xT[:, c, bass.ds(b * S, S)], c, DC,
                                  skip_group_check=True)
                    last.then_inc(q0_mm, 1)

            wv = slice(D + KVH * HD, D + 2 * KVH * HD)
            for b in range(B):
                for half in range(2):
                    for c in range(DC):
                        last = mm(s_banks[S2 * half:S2 * half + S2, 2, b * KVH * HD:(b + 1) * KVH * HD],
                                  ctxT[:, c, b * S2:(b + 1) * S2], w0[:, c, wv], c, DC)
            last.then_inc(v0_mm, 1)
            q0(0)

            def s0(i, p, q):
                if p == 0 and q == 0:
                    pe.wait_ge(q0_out, i + DC)
                    pe.wait_ge(kblk_done, i + DC)
                if isinstance(i, int) and i == 0 and q == 0:
                    pe.wait_ge(kT0_out, DC)
                else:
                    pe.wait_ge(sc0_done, QUARTERS * i + q)
                c, half = q // 2, q % 2
                mm(s0_ps, qT0[:, c, p * P:(p + 1) * P],
                   kblk[:, c, half * QH:(half + 1) * QH, :].rearrange("p h t -> p (h t)")).then_inc(s0_mm, 1)

            def turn0(i, p, g):
                if g == 0:
                    pe.wait_ge(exp0_done, i + 1)
                if some(4 * i + g):
                    pe.wait_ge(pT0_out, 4 * i + g)
                for j in range(4):
                    last = nc.tensor.transpose(pT0_ps[:, j * P:(j + 1) * P],
                                               sc0[p][:, (4 * g + j) * P:(4 * g + j + 1) * P], ident[:])
                last.then_inc(pT0_mm, 1)

            def values0(i, g, b):
                pe.wait_ge(pT0_out, 4 * i + g + 1)
                if g == 0:
                    if some(i):
                        pe.wait_ge(o0_done, i)
                    pe.wait_ge(v0_out, 2)
                for j in range(4):
                    hp = 4 * g + j
                    last = mm(o0_ps[:, hp * 2 * VO:(hp + 1) * 2 * VO], pT0[:, hp],
                              vblk[:, bass.ds(b, 1), hp * 2 // G, :].rearrange("p a e -> p (a e)"),
                              skip_group_check=True)
                if g == 3:
                    last.then_inc(pv0_mm, 1)

            def turn_o0(i, p, batches):
                pe.wait_ge(o0_done, i + 1)
                pe.wait_ge(q0_out, DC * batches)
                if some(i):
                    pe.wait_ge(y0_done, i)
                for c in range(DC):
                    last = nc.tensor.transpose(oT0_ps[:, c * P:(c + 1) * P], o0[p][:, c * P:(c + 1) * P], ident[:])
                last.then_inc(oT0_mm, 1)

            def wo0(i):
                pe.wait_ge(oT0_out, i + 1)
                for c in range(DC):
                    last = mm(wo0_ps, oT0[:, c], w0[:, c, D + 2 * KVH * HD:], c, DC, skip_group_check=True)
                last.then_inc(wo0_mm, 1)

            def col(layer, w, at, n=P):
                return wh[layer][w][:, at:at + n], wl[w][:, at:at + n]

            def ctx_chunk(c):
                return ctxh[:, c], ctxl[:, c]

            def keys(h, w, layer=0):
                pe.wait_ge(w_lo, 2 * h + 1)
                if some(h):
                    if layer == 0:
                        pe.wait_ge(vwb_out, h)
                    else:
                        pe.wait_ge(kT_out, h)
                for c in range(DC):
                    last = mm3(kT_ps[layer], col(layer, w, W_K + c * K), ctx_chunk(c), c, DC)
                last.then_inc(kT_mm, 1)

            def vals(h, w, layer=0):
                pe.wait_ge(kT_out, h + 1) if layer == 0 else pe.wait_ge(vT_out, h)
                for c in range(DC):
                    last = mm3(vT_ps[layer], col(layer, w, W_V + c * K), ctx_chunk(c), c, DC, skip_group_check=True)
                last.then_inc(vT_mm, 1)

            def ac(h, w, j, layer=0):
                if j == 0:
                    pe.wait_ge(kT_out, h + 1)
                    pe.wait_ge(headcols, 4 * h + 4)
                    if some(h):
                        pe.wait_ge(ac_out, 4 * h)
                elif layer == 1:
                    pe.wait_ge(bqk_out, 2 * h)
                elif j == DC:
                    pe.wait_ge(ac_out, 4 * h + 2)
                elif some(h):
                    pe.wait_ge(bqk_out, 2 * h)
                lhsT = col(layer, w, W_QT + j * P) if j < DC else (bqh[:], bql)
                mm3(ac_ps(layer, w, j), lhsT, (kTh[:], kTl[:])).then_inc(ac_mm, 1)

            def vwb(h, w, layer):
                if layer == 0:
                    pe.wait_ge(vT_out, h + 1)
                else:
                    pe.wait_ge(vwb_out, h)
                    pe.wait_ge(w_lo_dve, h - (H - 1))
                mm3(vwb_ps[layer], col(layer, w, W_BV, H), col(layer, w, W_O, D)).then_inc(vwb_mm, 1)

            def vw(h, w, layer=0):
                pe.wait_ge(vT_out, h + 1)
                if some(h):
                    pe.wait_ge(vw_out_dve, h)
                    pe.wait_ge(vw_out_act, h)
                for pair_of in range(2):
                    at = slice(pair_of * P, (pair_of + 1) * P)
                    last = mm3(vw_ps[:, pair_of], (vTh[:, at], vTl[:, at]), col(layer, w, W_O, D),
                               skip_group_check=True)
                last.then_inc(vw_mm, 1)

            def hT_turn(ps, n, p):
                if isinstance(n, int) and n < 2:
                    pe.wait_ge(m_done, n + 1)
                else:
                    pe.wait_ge(ln_done, ln_of1(n) + 1)
                for c in range(DC):
                    last = nc.tensor.transpose(ps[:, c * P:(c + 1) * P], xn[p][:, c * P:(c + 1) * P], ident[:])
                last.then_inc(hT_mm, 1)

            def tile0(b, p, first=False, last=False):
                i = 2 * b + p
                w1, w2 = 2 * p, 2 * p + 1
                h1, h2 = SLOTS * b + w1, SLOTS * b + w2
                next_tile = not (last and p == 1)
                if next_tile:
                    s0(i + 1, 1 - p, 0)
                if not (first and p == 0):
                    keys(h1, w1, 0)
                if not (first and p == 0):
                    turn_o0(i - 1, 1 - p, b + 1 if p == 0 or last else b + 2)
                if next_tile:
                    s0(i + 1, 1 - p, 1)
                vals(h1, w1, 0)
                ac(h1, w1, 0)
                if next_tile:
                    s0(i + 1, 1 - p, 2)
                ac(h1, w1, 1)
                if not (first and p == 0):
                    wo0(i - 1)
                if next_tile:
                    s0(i + 1, 1 - p, 3)
                ac(h1, w1, 2)
                vwb(h1, w1, 0)
                turn0(i, p, 0)
                vw(h1, w1)
                turn0(i, p, 1)
                values0(i, 0, b)
                keys(h2, w2, 0)
                turn0(i, p, 2)
                values0(i, 1, b)
                vals(h2, w2, 0)
                turn0(i, p, 3)
                values0(i, 2, b)
                if not next_tile:
                    pe.wait_ge(y0_done, i)
                    for n in range(2):
                        hT_turn(first_hT_ps[n], n, n)
                ac(h2, w2, 0)
                values0(i, 3, b)
                ac(h2, w2, 1)
                if p == 0 and not last:
                    q0(b + 1, i)
                ac(h2, w2, 2)
                if next_tile:
                    vwb(h2, w2, 0)
                    vw(h2, w2)

            for q in range(QUARTERS - 1):
                s0(0, 0, q)
            pe.wait_ge(ctx_lo, DC)
            pe.wait_ge(fills, N_FILLS)
            keys(0, 0)
            s0(0, 0, QUARTERS - 1)
            pe.wait_ge(ident_in, 16)
            tile0(0, 0, first=True)
            tile0(0, 1, first=True)
            with pe.Fori(1, B - 1) as b:
                tile0(b, 0)
                tile0(b, 1)
            tile0(B - 1, 0, last=True)
            tile0(B - 1, 1, last=True)

            def hT_turn_ahead(n, p):
                pe.wait_ge(hT_out, DC * n)
                hT_turn(hT_ps, n, p)

            def scores(n, p, b):
                pe.wait_ge(hT_out, DC * n + DC)
                if some(n):
                    pe.wait_ge(sx_done, 2 * n)
                for half in range(2):
                    for c in range(DC):
                        mm(sx_ps[:, half], hT[p][:, c],
                           AC[:, c, bass.ds(b, 1), half * HP:(half + 1) * HP, :].rearrange("p a h t -> p (a h t)"),
                           c, DC)
                for c in range(DC):
                    last = mm(sxb_ps, hT[p][:, c], ACb[:, c, :], c, DC)
                last.then_inc(s_mm, 1)

            def first_scores(layer):
                n = layer * TILES
                pe.wait_ge(hT_out, DC * n + DC)
                if some(n):
                    pe.wait_ge(sx_done, 2 * n)
                for c in range(DC):
                    mm(sxb_ps, hT[0][:, c], ACb[:, c, :], c, DC)
                for half in range(2):
                    for c in range(DC):
                        last = mm(sx_ps[:, half], hT[0][:, c],
                                  AC[:, c, 0, half * HP:(half + 1) * HP, :].rearrange("p h t -> p (h t)"), c, DC)
                    last.then_inc(s_mm if half else half_mm, 1)

            def half_turn(n, g):
                if some(n):
                    pe.wait_ge(pT_out, 3 * n)
                for j in range(4):
                    hp = 4 * g + j
                    last = nc.tensor.transpose(pT_ps[g][:, j * P:(j + 1) * P],
                                               pm[:, 2 * hp:2 * hp + 2, :].rearrange("p h t -> p (h t)"), ident[:])
                last.then_inc(pT_mm, 1)

            def bias_turn():
                nc.tensor.transpose(pTb_ps, pmb[:], ident[:]).then_inc(pT_mm, 1)

            def weights_turn(n):
                pe.wait_ge(pm_done, 2 * n + 2)
                half_turn(n, 0)
                half_turn(n, 1)
                bias_turn()

            def first_turn_values(n):
                def rest():
                    pe.wait_ge(pm_done, 2 * n + 2)
                    half_turn(n, 1)
                    pe.wait_ge(y0_done, TILES)
                    bias_turn()
                    hT_turn_ahead(n + 2, 0)

                pe.wait_ge(half_pm, n // TILES * 2 + 2)
                half_turn(n, 0)
                values(n, 0, halfway=rest)

            def values(n, b, halfway=None):
                if some(n):
                    pe.wait_ge(x_done, n)
                for hp in range(HP):
                    if halfway and hp == HP // 2:
                        halfway()
                    if hp % 4 == 0:
                        pe.wait_ge(pT_out, 3 * n + hp // 4 + 1)
                    mm(o_ps, pT[:, hp], VW[:, bass.ds(b, 1), hp, :].rearrange("p a d -> p (a d)"), hp, HP + 1)
                pe.wait_ge(pT_out, 3 * n + 3)
                mm(o_ps, pTb[:], VWb[:], HP, HP + 1).then_inc(o_mm, 1)

            def hTm_turn(i):
                if i == 0:
                    pe.wait_ge(hT_out, LAYERS * TILES * DC)
                elif i < 6:
                    pe.wait_ge(hTm_out, DC * i)
                for t in range(i, i + 2):
                    pe.wait_ge(m_done, BATCH_END[0] + t + 1)
                    for c in range(DC):
                        last = nc.tensor.transpose(hTm_ps[t][:, c * P:(c + 1) * P],
                                                   xn[t % HALF][:, c * P:(c + 1) * P], ident[:])
                    last.then_inc(hTm_mm, 1)

            def fc1_product(half, f):
                if f == 0:
                    pe.wait_ge(fc_lo, 4)
                    pe.wait_ge(hTm_lo, (half + 1) * HALF)
                if half or f >= 2:
                    pe.wait_ge(g_out, half * FC + f - 1)
                for c in range(DC):
                    w, t = slice(f * P, (f + 1) * P), slice(half * HALF * P, (half + 1) * HALF * P)
                    last = mm3(g_ps[f % 2], (fc1h[:, c, w], fc1l[:, c, w]), (hTmh[:, c, t], hTml[:, c, t]), c, DC)
                last.then_inc(g_mm, 1)

            def attention(layer):
                n0 = layer * TILES
                heads = layer * H + H

                def pair(b, first=False, last=False):
                    n = n0 + 2 * b
                    mlp = last and layer + 1 == LAYERS
                    for p in range(2):
                        if p == 0:
                            if mlp:
                                hTm_turn(0)
                            scores(n + 1, 1, b)
                            if first:
                                pe.wait_ge(bqk_out, 2 * heads)
                                pe.wait_ge(vwb_out, heads)
                                pe.wait_ge(vw_out_dve, heads)
                                pe.wait_ge(vw_out_act, heads)
                                pe.wait_ge(bo_in, 16 * layer + 16)
                        elif not last:
                            scores(n + 2, 0, b + 1)
                        elif not mlp:
                            for j in range(DC):
                                ac(heads, 0, j, layer + 1)
                        if first and p == 0:
                            first_turn_values(n)
                            continue
                        weights_turn(n + p)
                        if not mlp:
                            hT_turn_ahead(n + p + 2, p)
                        if last and p == 0 and not mlp:
                            pe.wait_ge(sx_done, 2 * n + 4)
                            keys(heads, 0, layer + 1)
                        if mlp and p == 0:
                            hTm_turn(2)
                            values(n + p, b)
                            pe.wait_ge(sx_done, 2 * LAYERS * TILES)
                            for f in range(2):
                                fc1_product(0, f)
                        else:
                            values(n + p, b)

                pe.wait_ge(ac_out, 4 * heads)
                pe.wait_ge(vwb_out, heads - 1)
                pe.wait_ge(vT_out, heads)
                if layer == 0:
                    pe.wait_ge(o0_done, TILES)
                first_scores(layer)
                if layer == 0:
                    pe.wait_ge(hT_out, 2 * DC)
                    turn_o0(TILES - 1, 1, B)
                    vwb(heads - 1, SLOTS - 1, layer)
                vw(heads - 1, SLOTS - 1, layer)
                if layer == 0:
                    wo0(TILES - 1)
                pair(0, first=True)
                with pe.Fori(1, B - 1) as b:
                    pair(b)
                pair(B - 1, last=True)

            attention(0)

            def round1(r, last=False):
                for w in range(SLOTS):
                    h = r * SLOTS + w
                    ac(h, w, DC, 1)
                    if not (last and w == SLOTS - 1):
                        keys(h + 1, (w + 1) % SLOTS, 1)
                    pe.wait_ge(x_done, TILES)
                    vwb(h, w, 1)
                    if not (last and w == SLOTS - 1):
                        vw(h, w, 1)
                        vals(h + 1, (w + 1) % SLOTS, 1)
                        for j in range(DC):
                            ac(h + 1, (w + 1) % SLOTS, j, 1)

            vals(H, 0, 1)
            with pe.Fori(SLOTS, LAYERS * SLOTS - 1) as r:
                round1(r)
            round1(LAYERS * SLOTS - 1, last=True)
            attention(1)

            for half in range(TILES // HALF):
                for f in range(0 if half else 2, FC):
                    if half == 0 and f >= 6:
                        hTm_turn(2 * f - 8)
                    fc1_product(half, f)
                for j in range(HALF):
                    i = half * HALF + j
                    if i >= 2:
                        pe.wait_ge(y_done, i - 1)
                    for f in range(FC):
                        if j == 0:
                            pe.wait_ge(g_lo, half * FC + f + 1)
                        t = slice(j * P, (j + 1) * P)
                        last = mm3(y_ps[i % 2], (gTh[:, f, t], gTl[:, f, t]), (fc2h[:, f], fc2l[:, f]), f, FC)
                    last.then_inc(y_mm, 1)


def kernel(**inputs):
    import numpy as np
    import concourse.bacc as _bacc
    from concourse.bass_utils import run_bass_kernel_spmd as _run

    a = {n: np.asarray(v) for n, v in inputs.items()}

    def columns(v):
        return v.reshape(-1, P).T

    def rows_by_chunk(w):
        return w.reshape(DC, P, -1).transpose(1, 0, 2)

    x, c = a["x"], a["ctx_2048"]
    p0, p1 = "L0_xattn_", "L1_xattn_"
    bk_rep = np.broadcast_to(a[p0 + "bk"].reshape(KVH, 1, HD), (KVH, G, HD)).reshape(-1)
    heads = np.zeros((LAYERS, H, P, W_N), np.float32)
    for i in range(LAYERS):
        def get(name):
            return a[f"{p1}{name}{i + 1}"]
        for at, name in ((W_K, "wk"), (W_V, "wv")):
            heads[i, :, :, at:at + D] = get(name).reshape(DC, P, H, K).transpose(2, 1, 0, 3).reshape(H, P, D)
        heads[i, :, :, W_QT:W_QT + D] = get("wq").reshape(D, H, K).transpose(1, 2, 0)
        heads[i, :, :, W_O:W_O + D] = get("wo").reshape(H, K, D)
        for h in range(H):
            heads[i, h, :, W_BV + h] = get("bias_v").reshape(H, K)[h]
        for j, name in enumerate(("bk", "bq", "bias_k", "bv")):
            heads[i, :, :, W_COL + j] = get(name).reshape(H, K)
    blockmask = np.zeros((P, NHC), np.float32)
    for row in range(P):
        blockmask[row, row // HD] = 1.0
    arrays = {
        "x_tok": x.reshape(TILES, P, D).transpose(1, 0, 2),
        "xT": rows_by_chunk(x.reshape(-1, D).T),
        "ctxT": rows_by_chunk(c.reshape(-1, D).T),
        "mask": a["mask_Bx1xSxS2_ff0"].reshape(TILES, P, S2).transpose(1, 0, 2),
        "w0": np.concatenate([rows_by_chunk(a[p0 + n]) for n in ("Wq", "Wk", "Wv", "Wo")], axis=2),
        "cols0": np.concatenate([columns(a[p0 + "bq"]), columns(bk_rep)], axis=1),
        "rows": np.concatenate([a[p0 + "bo"], a[p0 + "gamma"], a[p0 + "beta"], a[p1 + "b_fc2"], a[p0 + "bv"]])[None],
        "heads": heads.reshape(LAYERS * H, P, W_N),
        "bo": np.stack([a[f"{p1}bo{i + 1}"] for i in range(LAYERS)]),
        "ln": np.concatenate([columns(a[p1 + n]) for n in ("ln1_scale", "ln1_offset", "ln2_scale", "ln2_offset",
                                                           "ln_mlp_scale", "ln_mlp_offset")], axis=1),
        "fc1": rows_by_chunk(a[p1 + "w_fc1"]),
        "bfc1": columns(a[p1 + "b_fc1"]),
        "fc2": a[p1 + "w_fc2"].reshape(FC, P, D).transpose(1, 0, 2),
        "blockmask": blockmask,
        "ident": np.eye(P, dtype=np.float32),
    }
    nc = _bacc.Bacc("TRN2", target_bir_lowering=False, num_devices=1)
    feed, args = {}, []
    for name, value in arrays.items():
        value = np.ascontiguousarray(value)
        feed[f"in_{name}_dram"] = value
        args.append(nc.dram_tensor(f"in_{name}_dram", value.shape, mybir.dt.from_np(value.dtype),
                                   kind="ExternalInput").ap())
    args.append(nc.dram_tensor("out_dram", (P, TILES, D), F32, kind="ExternalOutput").ap())
    build(nc, *args)
    got = _run(nc, [feed], core_ids=[0]).results[0]["out_dram"]
    return got.transpose(1, 0, 2).reshape(B, S, D)
```
